# Optimizing a Trainium2 kernel written in Bass

```python
import numpy as np
import jax
import jax.numpy as jnp

def _softmax(x, axis=-1):
    return jax.nn.softmax(x, axis=axis)

def _gelu(x):
    return jax.nn.gelu(x, approximate=True)

def _silu(x):
    return jax.nn.silu(x)

def _sigmoid(x):
    return jax.nn.sigmoid(x)

def _layernorm(x, axis=-1, eps=1e-05):
    m = jnp.mean(x, axis=axis, keepdims=True)
    v = jnp.var(x, axis=axis, keepdims=True)
    return (x - m) / jnp.sqrt(v + eps)

def _scatter_add(tgt, idx, src, axis=0):
    return tgt.at[idx].add(src)

def _segment_sum(src, seg, n):
    return jax.ops.segment_sum(src, seg, n)
kernel_name = 'mk_perceiver_d1_seqx_r2_d69334'

def setup_inputs(seed: int=0):
    np.random.seed(seed)
    _w = jnp.asarray

    def _rec_inputs():
        import jax
        import jax.numpy as jnp
        _rk = jax.random.key(seed)
        x = -0.0002928 + 1 * jax.random.normal(jax.random.fold_in(_rk, 1), (32, 32, 512), jnp.float32)
        _lenS = 32 - jax.random.randint(jax.random.fold_in(_rk, 7), (32,), 0, max(1, 32 // 4) + 1, jnp.int32)
        _lenS2 = 257 - jax.random.randint(jax.random.fold_in(_rk, 8), (32,), 0, max(1, 257 // 4) + 1, jnp.int32)
        _ctx_1024P = jax.random.normal(jax.random.fold_in(_rk, 11), (32, 16, 512), jnp.float32)
        _ctx_1024c = jax.random.dirichlet(jax.random.fold_in(_rk, 511), 0.3 * jnp.ones((16,), jnp.float32), (32, 257))
        _ctx_1024t = jnp.einsum('bsk,bkd->bsd', _ctx_1024c, _ctx_1024P)
        _ctx_1024t = _ctx_1024t * jax.lax.rsqrt(jnp.mean(jnp.square(_ctx_1024t)) + 1e-12) * 0.953939
        ctx_1024 = -1.39393e-06 + 0.999914 * (_ctx_1024t + 0.3 * jax.random.normal(jax.random.fold_in(_rk, 611), (32, 257, 512), jnp.float32))
        _validS = jnp.arange(32)[None, :] < _lenS[:, None]
        _validS2 = jnp.arange(257)[None, :] < _lenS2[:, None]
        _causal = jnp.tril(jnp.ones((32, 32), dtype=bool))
        mask_1x1xSxS2_ik0 = jnp.where(jnp.broadcast_to(_validS2[0:1, None, None, :], (1, 1, 32, 257)), 0, 1).astype(jnp.int32)
        return (x, ctx_1024, mask_1x1xSxS2_ik0)
    x, ctx_1024, mask_1x1xSxS2_ik0 = _rec_inputs()

    def _L0_xattn_setup():
        import jax, jax.numpy as jnp
        import numpy as np
        B, S, D, H = (2, 1024, 512, 16)
        DK = D // H
        key = jax.random.key(seed)
        ks = jax.random.split(key, 12)
        std = 1.0 / np.sqrt(D)
        inp = {'query': jax.random.normal(ks[0], (B, S, D), jnp.float32), 'key': jax.random.normal(ks[1], (B, S, D), jnp.float32), 'value': jax.random.normal(ks[2], (B, S, D), jnp.float32), 'mask': jnp.tril(jnp.ones((S, S), jnp.int32))[None, None, :, :], 'Wq': jax.random.normal(ks[3], (D, D), jnp.float32) * std, 'bq': jax.random.normal(ks[4], (D,), jnp.float32) * std, 'Wk': jax.random.normal(ks[5], (D, D), jnp.float32) * std, 'bk': jax.random.normal(ks[6], (D,), jnp.float32) * std, 'Wv': jax.random.normal(ks[7], (D, D), jnp.float32) * std, 'bv': jax.random.normal(ks[8], (D,), jnp.float32) * std, 'Wo': jax.random.normal(ks[9], (D, D), jnp.float32) * std, 'bo': jax.random.normal(ks[10], (D,), jnp.float32) * std}
        return inp
    _L0_xattn_all = _L0_xattn_setup()
    _L0_xattn_in = {k: v for k, v in _L0_xattn_all.items() if k in ('Wq', 'bq', 'Wk', 'bk', 'Wv', 'bv', 'Wo', 'bo')}
    del _L0_xattn_all

    def _L0_attn_setup():
        import jax, jax.numpy as jnp
        import numpy as np
        D = 512

        def _bind(a, b):
            return jnp.fft.irfft(jnp.fft.rfft(a, axis=-1) * jnp.fft.rfft(b, axis=-1), n=a.shape[-1], axis=-1)

        def _unbind(s, q):
            return jnp.fft.irfft(jnp.fft.rfft(s, axis=-1) * jnp.conj(jnp.fft.rfft(q, axis=-1)), n=q.shape[-1], axis=-1)
        key = jax.random.key(seed)
        ks = jax.random.split(key, 7)
        scale = 1.0 / np.sqrt(D)
        x = jax.random.normal(ks[0], (4, 2048, D), dtype=jnp.float32)
        Wq = jax.random.normal(ks[1], (D, D), dtype=jnp.float32) * scale
        Wk = jax.random.normal(ks[2], (D, D), dtype=jnp.float32) * scale
        Wv = jax.random.normal(ks[3], (D, D), dtype=jnp.float32) * scale
        bq = jnp.zeros((D,), jnp.float32)
        bk = jnp.zeros((D,), jnp.float32)
        bv = jnp.zeros((D,), jnp.float32)
        return {'x': x, 'Wq': Wq, 'bq': bq, 'Wk': Wk, 'bk': bk, 'Wv': Wv, 'bv': bv}
    _L0_attn_all = _L0_attn_setup()
    _L0_attn_in = {k: v for k, v in _L0_attn_all.items() if k in ('Wq', 'bq', 'Wk', 'bk', 'Wv', 'bv')}
    del _L0_attn_all

    def _L0_ffn_setup():
        import jax, jax.numpy as jnp
        import numpy as np
        D = 512
        H = 2048
        E = 8
        B, N = (2, 1024)
        key = jax.random.key(seed)
        ks = jax.random.split(key, 5)
        x = jax.random.normal(ks[0], (B, N, D), dtype=jnp.float32)
        W1 = jax.random.normal(ks[1], (E, D, H), dtype=jnp.float32) / np.sqrt(D)
        W2 = jax.random.normal(ks[2], (E, H, D), dtype=jnp.float32) / np.sqrt(H)
        Wg = jax.random.normal(ks[3], (D, E), dtype=jnp.float32) / np.sqrt(D)
        bg = jax.random.normal(ks[4], (E,), dtype=jnp.float32) * 0.01
        return {'x': x, 'W1': W1, 'W2': W2, 'Wg': Wg, 'bg': bg}
    _L0_ffn_all = _L0_ffn_setup()
    _L0_ffn_in = {k: v for k, v in _L0_ffn_all.items() if k in ('W1', 'W2', 'Wg', 'bg')}
    del _L0_ffn_all
    return {'x': x, 'ctx_1024': ctx_1024, 'mask_1x1xSxS2_ik0': mask_1x1xSxS2_ik0, 'L0_xattn_Wq': _L0_xattn_in['Wq'], 'L0_xattn_bq': _L0_xattn_in['bq'], 'L0_xattn_Wk': _L0_xattn_in['Wk'], 'L0_xattn_bk': _L0_xattn_in['bk'], 'L0_xattn_Wv': _L0_xattn_in['Wv'], 'L0_xattn_bv': _L0_xattn_in['bv'], 'L0_xattn_Wo': _L0_xattn_in['Wo'], 'L0_xattn_bo': _L0_xattn_in['bo'], 'L0_attn_Wq': _L0_attn_in['Wq'], 'L0_attn_bq': _L0_attn_in['bq'], 'L0_attn_Wk': _L0_attn_in['Wk'], 'L0_attn_bk': _L0_attn_in['bk'], 'L0_attn_Wv': _L0_attn_in['Wv'], 'L0_attn_bv': _L0_attn_in['bv'], 'L0_ffn_W1': _L0_ffn_in['W1'], 'L0_ffn_W2': _L0_ffn_in['W2'], 'L0_ffn_Wg': _L0_ffn_in['Wg'], 'L0_ffn_bg': _L0_ffn_in['bg']}

def reference(x, ctx_1024, mask_1x1xSxS2_ik0, L0_xattn_Wq, L0_xattn_bq, L0_xattn_Wk, L0_xattn_bk, L0_xattn_Wv, L0_xattn_bv, L0_xattn_Wo, L0_xattn_bo, L0_attn_Wq, L0_attn_bq, L0_attn_Wk, L0_attn_bk, L0_attn_Wv, L0_attn_bv, L0_ffn_W1, L0_ffn_W2, L0_ffn_Wg, L0_ffn_bg):
    import jax
    import jax.numpy as jnp

    def _L0_xattn_ref(query, key, value, mask, Wq, bq, Wk, bk, Wv, bv, Wo, bo):
        import jax, jax.numpy as jnp
        import numpy as np
        B, S, D, H = (2, 1024, 512, 16)
        DK = D // H
        b = query.shape[0]
        Q = query @ Wq.T + bq
        K = key @ Wk.T + bk
        V = value @ Wv.T + bv
        Q = Q.reshape(b, -1, H, DK).transpose(0, 2, 1, 3)
        K = K.reshape(b, -1, H, DK).transpose(0, 2, 1, 3)
        V = V.reshape(b, -1, H, DK).transpose(0, 2, 1, 3)
        scores = jnp.einsum('bhqd,bhkd->bhqk', Q, K) / jnp.sqrt(jnp.float32(DK))
        scores = jnp.where(mask == 0, -jnp.inf, scores)
        weights = jax.nn.softmax(scores, axis=-1)
        attn = jnp.einsum('bhqk,bhkd->bhqd', weights, V)
        attn = attn.transpose(0, 2, 1, 3).reshape(b, -1, D)
        return attn @ Wo.T + bo

    def _L0_attn_ref(x, Wq, bq, Wk, bk, Wv, bv):
        import jax, jax.numpy as jnp
        import numpy as np
        D = 512

        def _bind(a, b):
            return jnp.fft.irfft(jnp.fft.rfft(a, axis=-1) * jnp.fft.rfft(b, axis=-1), n=a.shape[-1], axis=-1)

        def _unbind(s, q):
            return jnp.fft.irfft(jnp.fft.rfft(s, axis=-1) * jnp.conj(jnp.fft.rfft(q, axis=-1)), n=q.shape[-1], axis=-1)
        q = jnp.einsum('bsd,de->bse', x, Wq) + bq
        k = jnp.einsum('bsd,de->bse', x, Wk) + bk
        v = jnp.einsum('bsd,de->bse', x, Wv) + bv
        x_k = _bind(k, v)
        s = jnp.sum(x_k, axis=1, keepdims=True)
        out = _unbind(s, q)
        return out

    def _L0_ffn_ref(x, W1, W2, Wg, bg):
        import jax, jax.numpy as jnp
        import numpy as np
        D = 512
        H = 2048
        E = 8
        B, N = (2, 1024)
        b, n, d = x.shape
        e = Wg.shape[1]
        xf = x.reshape(b * n, d)
        logits = xf @ Wg + bg
        one_hot = jax.nn.one_hot(jnp.argmax(logits, axis=-1), e, dtype=x.dtype)
        h = jax.nn.gelu(jnp.einsum('td,edh->eth', xf, W1), approximate=True)
        y = jnp.einsum('eth,ehd->etd', h, W2)
        out = jnp.einsum('etd,te->td', y, one_hot)
        return out.reshape(b, n, d)
    x = x + _L0_xattn_ref(_layernorm(x, axis=-1), ctx_1024, ctx_1024, mask_1x1xSxS2_ik0, L0_xattn_Wq, L0_xattn_bq, L0_xattn_Wk, L0_xattn_bk, L0_xattn_Wv, L0_xattn_bv, L0_xattn_Wo, L0_xattn_bo)
    x = x + _L0_attn_ref(_layernorm(x, axis=-1), L0_attn_Wq, L0_attn_bq, L0_attn_Wk, L0_attn_bk, L0_attn_Wv, L0_attn_bv)
    x = x + _L0_ffn_ref(_layernorm(x, axis=-1), L0_ffn_W1, L0_ffn_W2, L0_ffn_Wg, L0_ffn_bg)
    return x

_drawn_inputs = setup_inputs


def setup_inputs(seed=0):
    import zlib

    import numpy as np

    out = dict(_drawn_inputs(seed))
    spreads = {'L0_attn_bq': (0.0, 0.1), 'L0_attn_bk': (0.0, 0.1), 'L0_attn_bv': (0.0, 0.1)}
    factors = {'L0_xattn_bk': 64.0,
     'L0_ffn_W1': 57.772,
     'L0_ffn_W2': 48.014,
     'L0_ffn_Wg': 51.044,
     'L0_ffn_bg': 64.0}
    for name, (base, spread) in spreads.items():
        noise = np.random.default_rng([zlib.crc32(name.encode()), seed]).standard_normal(out[name].shape)
        drawn = base * np.exp(spread * noise) if base else spread * noise
        out[name] = jnp.asarray(drawn.astype(out[name].dtype))
    for name, factor in factors.items():
        out[name] = (out[name] * factor).astype(out[name].dtype)
    return out
```

```python
from contextlib import ExitStack
from itertools import count

import concourse.bass as bass
from concourse import mybir

F32 = mybir.dt.float32
F16 = mybir.dt.float16
I32 = mybir.dt.int32
U32 = mybir.dt.uint32
ALU = mybir.AluOpType
ACT = mybir.ActivationFunctionType
AX_X = mybir.AxisListType.X

P = 128
B, S, D = 32, 32, 512
L = 257
H = 16
DK = D // H
KC = D // P
HC = P // DK
T = B * S
NT = T // P
PB = 2
STEPS = B // PB
LM = 256
PAIRS = PB * KC
E, FF = 8, 2048
FC = FF // P
CAP = 160
CB = CAP - P
ROUNDS = -(-T // CAP)
PIECES = 8
NF = D // 2
EPS = 1e-5

SX = 2.0 ** 8
SW = 2.0 ** 12
SK = 2.0 ** 6
SP_ = 2.0 ** 12
SF = 2.0 ** 8
SG = 2.0 ** 6
S2 = 2.0 ** 7
SH = 2.0 ** 3
NEG = -1e30
ISD = 1.0 / (float(DK) ** 0.5)


def perceiver_block(nc, i, out):
    ctx = ExitStack()
    with ctx:
        def sem(name):
            return ctx.enter_context(nc.semaphore(name))

        KB = 1024
        arena = ctx.enter_context(nc.sbuf_tensor("arena", [P, 204 * KB // 4], F32))
        banks = [ctx.enter_context(nc.psum_tensor(f"bank{n}", [P, 512], F32)) for n in range(8)]
        BA, BB, BC, BD, BE, BF, BG, BH = banks
        proj_banks = (BA, BB)

        def size(shape, dt):
            n = 2 if dt == F16 else 4
            for x in shape:
                n *= x
            return n

        def view(off, shape, dt, parts=P):
            n = size(shape, dt)
            assert off % 4 == 0 and n % 4 == 0 and off + n <= 204 * KB, (off, n)
            a = arena[0:parts, off // 4:(off + n) // 4]
            if dt != F32:
                a = a.bitcast(dt)
            if len(shape) > 1:
                names = [f"d{k}" for k in range(len(shape))]
                a = a.rearrange(f"p ({' '.join(names)}) -> p {' '.join(names)}",
                                **{k: v for k, v in zip(names, shape)})
            return a

        class Region:
            def __init__(self, start, end):
                self.at, self.end = start, end

            def take(self, shape, dt, parts=P):
                v = view(self.at, shape, dt, parts)
                self.at += -(-size(shape, dt) // 32) * 32
                assert self.at <= self.end, (self.at, self.end)
                return v

        keep = Region(0, 26 * KB)
        x_tok = keep.take([NT, D], F32)
        ident = keep.take([P], F32)
        ident16 = keep.take([P], F16)
        bq_col = keep.take([KC], F32)
        bq_scaled = keep.take([KC], F32)
        mask_bias = keep.take([L], F32)
        stats = keep.take([NT, 6], F32)
        mean_var = keep.take([NT, 2], F32)
        var_eps = keep.take([NT], F32)
        minus_half = keep.take([NT], F32)
        rstd = keep.take([NT], F32)
        score_sums = keep.take([PAIRS], F32)
        sums_scaled = keep.take([PAIRS], F32)
        recip = keep.take([PAIRS], F32)
        row_max = keep.take([PAIRS], F32)
        neg_max = keep.take([PAIRS], F32)
        diag = keep.take([PAIRS], F32)
        own_head = keep.take([HC], F32)
        dft_bias = keep.take([KC, 4], F32)
        lhs_bind = keep.take([3, 2, B], F32)
        bind_sums = keep.take([4, 2, B], F32)

        xa = Region(26 * KB, 204 * KB)
        qT = [xa.take([KC, T], F16) for _ in range(2)]
        wk = [xa.take([KC, D], F16) for _ in range(2)]
        wv = [xa.take([KC, D], F16) for _ in range(2)]
        wo = [xa.take([KC, D], F16) for _ in range(2)]
        att_off = xa.at
        attT = [xa.take([KC, T], F16) for _ in range(2)]
        lnT = attT
        stage_off = xa.at
        ctx_stage = [xa.take([KC, PB * LM], F32) for _ in range(2)]
        ctx_hl = [[xa.take([KC, PB * LM], F16) for _ in range(2)] for _ in range(2)]
        wq = ctx_hl[1]
        w_stage = ctx_stage
        kT = [xa.take([KC, PB, L + 1], F16) for _ in range(2)]
        v_off = xa.at
        v_hl = [[xa.take([PB * 2, D], F16) for _ in range(2)] for _ in range(2)]
        q_bd = [xa.take([KC, PB, P], F16) for _ in range(2)]
        sm_off = xa.at
        sm = xa.take([PAIRS, L], F32)
        p_all = xa.take([2, PAIRS, L + 1], F16)
        p_hl = [p_all[:, n] for n in range(2)]
        pt_off = xa.at
        pT = xa.take([PB, 2, 2, KC, P], F16)
        pT_last = xa.take([PAIRS, P], F16, parts=2 * PAIRS)
        vl_all = xa.take([2, STEPS, P], F16, parts=2 * PAIRS)
        vl_cur = xa.take([2, P], F16, parts=2 * PAIRS)
        att_st = [xa.take([KC, PB, S], F16) for _ in range(2)]
        klast = [xa.take([KC, B], F16) for _ in range(2)]
        ctxl_stage = xa.take([KC, B], F32)
        ctxl = [xa.take([KC, B], F16) for _ in range(2)]
        bk_col = xa.take([KC], F32)
        bv_col = xa.take([KC], F32)
        mask_int = view(sm_off, [L], I32)
        xhat0 = view(v_off, [NT, D], F32)
        q_f = [view(pt_off + n * 2 * KB, [D], F32) for n in range(2)]
        bv_bc = [view(pt_off + 4 * KB + n * KB, [KC, P], F16) for n in range(2)]
        bo_bc = view(pt_off + 6 * KB, [D], F32)
        vlast = [view(sm_off + 2 * KB + n * KB, [D], F16, parts=B) for n in range(2)]
        bias_tile = view(sm_off + 4 * KB, [D], F32)

        fa = Region(26 * KB, 152 * KB)
        kq_off = fa.at
        wf = [[fa.take([KC, D], F16) for _ in range(2)] for _ in range(3)]
        ln1T = [fa.take([KC, T], F16) for _ in range(2)]
        spec_off = fa.at
        spec = [fa.take([KC, T], F32) for _ in range(3)]
        dft = [fa.take([KC, D], F16) for _ in range(2)]
        idft = fa.take([KC, D], F32)
        wt_off = fa.at
        wt = [[fa.take([KC, D], F16) for _ in range(2)] for _ in range(1)]
        prod = view(wt_off, [2, T], F32)
        xhat1 = view(spec_off, [NT, D], F32)
        ab_stage = fa.take([KC, 4], F32)
        ab = [fa.take([KC, 4], F16) for _ in range(2)]
        wt_stage = [view((172 + 8 * n) * KB, [KC, D], F32) for n in range(3)]

        PW = KC * 512
        ea = Region(26 * KB, 172 * KB)
        w_hl = [[ea.take([PW], F16) for _ in range(2)] for _ in range(PIECES)]
        l2_f = ea.take([NT, D], F32)
        l2_hl = [ea.take([NT, D], F16) for _ in range(2)]
        hid_hl = [ea.take([FC, CAP], F16) for _ in range(2)]
        l2T_off = ea.at
        l2T = ea.take([NT, 2, KC, P], F16)
        ea_end = ea.at
        ea = Region(l2T_off, ea_end)
        hid_f = [ea.take([2, CAP], F32) for _ in range(2)]
        xs = ea.take([KC, 2, CAP], F16)
        yT = ea.take([KC, CAP], F32)
        y_rows = [ea.take([D], F32), ea.take([D], F32, parts=CB)]
        x2_rows = [ea.take([D], F32), ea.take([D], F32, parts=CB)]
        ea = Region(ea_end, 172 * KB)
        perm = ea.take([NT, CAP], F16)
        slot_iota = ea.take([CAP], F32)
        tri16 = ea.take([P], F16)
        ones16 = ea.take([P], F16)
        wg_stage = ea.take([KC, E], F32)
        wg_hl = [ea.take([KC, E], F16) for _ in range(2)]
        bg_bc = ea.take([E], F32)
        rank_order = ea.take([E], F32)
        tok_ids = ea.take([NT, 2], F16)
        id_offset = ea.take([2], F32)
        logits, is_max, score, onehot, slot_of = (ea.take([NT, E], F32) for _ in range(5))
        onehot16 = ea.take([NT, E], F16)
        top, top2 = (ea.take([NT], F32) for _ in range(2))
        most = ea.take([1], F32)
        more_rounds = ea.take([1], I32)
        ids_next = [ea.take([2], I32), ea.take([2], I32, parts=CB)]
        ids = [ea.take([2], I32), ea.take([2], I32, parts=CB)]
        e_stage = [view((172 + 8 * n) * KB, [PW], F32) for n in range(4)]


        names = """x_landed consts_landed wq_landed wk_landed wv_landed wo_landed ctxl_landed bias_landed
        ctx_landed0 ctx_landed1 dft_landed idft_landed wt_landed0 wt_landed1 wt_landed2 ab_landed out_landed
        vlast_stored vl_landed
        ln_var ln_rstd ln_out tr_ps tr_hi tr_free w_hi w_lo q_ps q_f32 q_hi q_lo ctxl_split last_ps last_hi last_lo
        bias_ps bias_done x_biased proj_ps proj_hi proj_free split_hi split_lo s_ps s_free s_max s_neg exp_done
        sums_sc recip_done p_hi p_lo q_ready vl_ready pt_ps pt_dve pt_act pv_ps pv_hi pv_free att_copied
        wo_ps x1_done fold_ps fold_hi fold_free ab_split abias_ps abias_done wt_hi wt_lo spec_ps spec_done
        unbound irfft_ps x2_done chain_dve chain_pool pool_waits
        gate_landed x2_stored wg_split l2_hi l2_lo lt_ps lt_done logits_ps onehot_done rank_ps routed
        e_landed0 e_landed1 e_landed2 e_landed3 e_hi e_lo perm_done xs_ps xs_done h_ps gelu_done h_hi h_lo
        y_ps y_done yt_ps y_out ids_done rows_landed scattered shifted ranks_moved""".split()
        s = {n: sem(n) for n in names}

        def from_zero(count):
            return max(count, 0) if isinstance(count, int) else count

        def hl_passes(a, b):
            return ((a[0], b[0]), (a[0], b[1]), (a[1], b[0]))

        def gate_transpose_out(eng, e, t):
            eng.wait_ge(s["lt_ps"], t + 1)
            e.activation(l2T[:, t].rearrange("p h c x -> p (h c x)"), proj_banks[t % 2][:].bitcast(F16), ACT.Copy
                         ).then_inc(s["lt_done"], 1)

        block = ctx.enter_context(nc.Block())

        @block.sync
        def _(sp):
            sp.dma_start(x_tok, i["x_t"]).then_inc(s["x_landed"], 16)
            for src, dst in ((i["ident"], ident), (i["ident16"], ident16), (i["bq"], bq_col), (i["bk"], bk_col),
                             (i["bv"], bv_col), (i["diag"], diag[0:2 * PAIRS]),
                             (i["own_head"], own_head)):
                sp.dma_start(dst, src).then_inc(s["consts_landed"], 16)
            for g in range(HC):
                sp.dma_start(mask_int[g * S:(g + 1) * S], i["mask"]).then_inc(s["consts_landed"], 16)
            sp.dma_start(bo_bc, i["bo"].partition_broadcast(P)).then_inc(s["bias_landed"], 16)
            sp.dma_start(w_stage[0], i["wq_t"]).then_inc(s["wq_landed"], 16)
            sp.dma_start(w_stage[1], i["wk_t"]).then_inc(s["wk_landed"], 16)
            sp.dma_start(ctxl_stage, i["ctx_last"]).then_inc(s["ctxl_landed"], 16)
            sp.wait_ge(s["w_lo"], 1)
            sp.dma_start(w_stage[0], i["wv_t"]).then_inc(s["wv_landed"], 16)
            sp.wait_ge(s["w_lo"], 2)
            sp.dma_start(w_stage[1], i["wo_t"]).then_inc(s["wo_landed"], 16)
            sp.wait_ge(s["w_lo"], 3)
            sp.dma_start(ctx_stage[0], i["ctx_t"][0]).then_inc(s["ctx_landed0"], 16)
            sp.wait_ge(s["w_lo"], 4)
            sp.dma_start(ctx_stage[1], i["ctx_t"][1]).then_inc(s["ctx_landed1"], 16)
            sp.wait_ge(s["last_lo"], 2)
            for n in range(2):
                sp.dma_start(i["vlast_dram"][n], vlast[n]).then_inc(s["vlast_stored"], 16)
            sp.wait_ge(s["vlast_stored"], 32)
            for rows, dst, n in ((0, 0, 0), (PAIRS, 0, 0), (0, 1, 1), (PAIRS, 1, 1)):
                sp.dma_start(vl_all[rows:rows + PAIRS, dst],
                             i["vlast_dram"][n].rearrange("(t b) (c x) -> (b c) t x", b=PB, c=KC)
                             ).then_inc(s["vl_landed"], 16)
            with sp.Fori(1, STEPS // PB) as k:
                for par in range(2):
                    st = k * 2 + par
                    sp.wait_ge(s["split_lo"], from_zero(st - 1))
                    sp.dma_start(ctx_stage[par], i["ctx_t"][bass.ds(st, 1)].rearrange("a p c t -> p (a c) t")
                                 ).then_inc(s[f"ctx_landed{par}"], 16)
            sp.wait_ge(s["split_lo"], STEPS)
            sp.wait_ge(s["wo_ps"], NT)
            for n in range(3):
                sp.dma_start(wt_stage[n], i["awt"][n]).then_inc(s[f"wt_landed{n}"], 16)
            sp.dma_start(ab_stage, i["ab"]).then_inc(s["ab_landed"], 16)
            for n in range(2):
                sp.dma_start(dft[n], i["dft16"][n]).then_inc(s["dft_landed"], 16)
            sp.dma_start(idft, i["idft"]).then_inc(s["idft_landed"], 16)
            for src, dst in ((i["slot_iota"], slot_iota), (i["tri16"], tri16), (i["ones16"], ones16),
                             (i["wg"], wg_stage), (i["bg"].partition_broadcast(P), bg_bc),
                             (i["rank_order"], rank_order), (i["tok_ids"], tok_ids), (i["id_offset"], id_offset)):
                sp.dma_start(dst, src).then_inc(s["gate_landed"], 16)

            def load_piece(e, n, done):
                sp.wait_ge(s["e_lo"], done)
                src = i["w1"] if n < 4 else i["w2"]
                sp.dma_start(e_stage[n % 4], src[bass.ds(e * 4 + n % 4, 1)].rearrange("a p x -> p (a x)")
                             ).then_inc(s[f"e_landed{n % 4}"], 16)

            sp.wait_ge(s["wt_lo"], 3)
            for n in range(4):
                load_piece(0, n, 0)
            sp.wait_ge(s["x2_done"], NT)
            sp.dma_start(i["x2_dram"].rearrange("(t p) d -> p t d", p=P), x_tok).then_inc(s["x2_stored"], 16)
            for n in range(4, PIECES):
                load_piece(0, n, n - 3)

            def rest_of_round(r):
                with sp.Fori(1, E) as e:
                    for n in range(PIECES):
                        load_piece(e, n, r * (E * PIECES) + e * PIECES + (n - 3))

            rest_of_round(0)
            sp.wait_ge(s["routed"], 1)
            with sp.If(sp.value_load(more_rounds[0:1, 0:1], min_val=0, max_val=1) > 0):
                with sp.Fori(1, ROUNDS) as r:
                    for n in range(PIECES):
                        load_piece(0, n, r * (E * PIECES) + (n - 3))
                    rest_of_round(r)

        @block.gpsimd
        def _(pool):
            g = nc.gpsimd

            def power(n):
                pool.wait_ge(s["ln_var"], n)
                g.tensor_tensor(rstd, var_eps, minus_half, ALU.pow).then_inc(s["ln_rstd"], 1)

            g.memset(minus_half, -0.5).then_inc(s["chain_pool"], 1)
            pool.wait_ge(s["chain_pool"], 1)
            power(1)
            for n in range(KC * 2):
                pool.wait_ge(s["q_f32"], n + 1)
                c, half = divmod(n, 2)
                g.tensor_copy(qT[0][:, c, half * D:(half + 1) * D], q_f[n % 2]).then_inc(s["q_hi"], 1)
            pool.wait_ge(s["bias_done"], 1)
            pool.wait_ge(s["ln_out"], NT)
            g.tensor_tensor(x_tok, x_tok, bias_tile.unsqueeze(1).broadcast_to((P, NT, D)), ALU.add
                            ).then_inc(s["x_biased"], 1)
            pool.wait_ge(s["q_lo"], KC * 2)
            pool.wait_ge(s["last_lo"], 2)

            def step(st, cur=True, prev=True):
                if prev:
                    pool.wait_ge(s["vl_landed"], 64)
                    pool.wait_ge(s["pv_ps"], from_zero(st * 2 - 2))
                    pool.sem_inc(s["pool_waits"], 1)
                    g.tensor_copy(vl_cur, vl_all[:, :, bass.ds(st - 1, 1), :].rearrange("p h a x -> p h (a x)")
                                  ).then_inc(s["vl_ready"], 1)
                if cur:
                    pool.wait_ge(s["s_ps"], st * PAIRS)
                    pool.sem_inc(s["pool_waits"], 1)
                    for n in range(2):
                        for b in range(PB):
                            g.tensor_tensor(q_bd[n][:, :, b, :].rearrange("p c (r q) -> p c r q", r=HC),
                                            qT[n][:, :, bass.ds(st * (PB * S) + b * S, S)].unsqueeze(2)
                                            .broadcast_to((P, KC, HC, S)),
                                            own_head.unsqueeze(1).unsqueeze(3).broadcast_to((P, KC, HC, S)), ALU.mult)
                        last = g.tensor_copy(kT[n][:, :, :, LM], klast[n][:, :, bass.ds(st * PB, PB)])
                    last.then_inc(s["q_ready"], 1)
                if prev:
                    pool.wait_ge(s["pv_free"], st * 2)
                    pool.sem_inc(s["pool_waits"], 1)
                    for n in range(2):
                        last = g.tensor_copy(attT[n][:, :, bass.ds(st * (PB * S) - PB * S, PB * S)],
                                             att_st[n].rearrange("p c b q -> p c (b q)"))
                    last.then_inc(s["att_copied"], 1)

            step(0, prev=False)
            step(1)
            with pool.Fori(1, STEPS // 2 - 1) as k:
                for par in range(2):
                    step(k * 2 + par)
            step(STEPS - 2)
            step(STEPS - 1)
            step(STEPS, cur=False)
            power(2)
            power(3)
            pool.wait_ge(s["x2_stored"], 16)

            out_rows = out.rearrange("b q d -> (b q) d")

            def scatter(n):
                pool.wait_ge(s["y_out"], n + 1)
                pool.sem_inc(s["pool_waits"], 1)
                for part in range(2):
                    g.indirect_dma_start(out=out_rows, out_offset=bass.IndirectOffsetOnAxis(
                                             ap=ids[part][:, 1:2].bitcast(U32), axis=0),
                                         in_=y_rows[part], in_offset=None, bounds_check=T - 1, oob_is_err=False
                                         ).then_inc(s["scattered"], 16)

            def expert(n, prev=True):
                for k in range(FC // 2):
                    pool.wait_ge(s["gelu_done"], n * 8 + k + 1)
                    pool.sem_inc(s["pool_waits"], 1)
                    g.tensor_scalar(hid_hl[0][:, 2 * k:2 * k + 2, :], hid_f[k % 2], SH, 1.0, ALU.mult, ALU.mult
                                    ).then_inc(s["h_hi"], 1)
                if prev:
                    scatter(n - 1)
                pool.wait_ge(s["shifted"], n + 1)
                pool.sem_inc(s["pool_waits"], 1)
                for part in range(2):
                    g.indirect_dma_start(out=x2_rows[part], out_offset=None, in_=i["x2_dram"],
                                         in_offset=bass.IndirectOffsetOnAxis(ap=ids[part][:, 0:1].bitcast(U32), axis=0)
                                         ).then_inc(s["rows_landed"], 16)

            def round_(r):
                expert(r * E, prev=False)
                with pool.Fori(1, E) as e:
                    expert(r * E + e)
                scatter(r * E + (E - 1))
                pool.wait_ge(s["scattered"], r * (32 * E) + 32 * E)
                pool.sem_inc(s["pool_waits"], 1)

            round_(0)
            pool.wait_ge(s["routed"], 1)
            with pool.If(pool.value_load(more_rounds[0:1, 0:1], min_val=0, max_val=1) > 0):
                with pool.Fori(1, ROUNDS) as r:
                    round_(r)

        @block.scalar
        def _(act):
            a = nc.scalar

            def hi(dst, src, scale):
                return a.activation(dst, src, ACT.Copy, scale=scale)

            def weight_hi(n, dst, src, landed):
                act.wait_ge(s[landed], 16)
                hi(dst[0], src, SW).then_inc(s["w_hi"], 1)

            weight_hi(0, wq, w_stage[0], "wq_landed")
            weight_hi(1, wk, w_stage[1], "wk_landed")
            for t in range(NT):
                act.wait_ge(s["tr_ps"], t + 1)
                hi(lnT[0][:, :, t * P:(t + 1) * P], proj_banks[t % 2][:].rearrange("p (c x) -> p c x", c=KC), SX
                   ).then_inc(s["tr_hi"], 1)
            act.wait_ge(s["ctxl_landed"], 16)
            hi(ctxl[0], ctxl_stage, SX).then_inc(s["ctxl_split"], 1)
            weight_hi(2, wv, w_stage[0], "wv_landed")
            for n in range(KC * 2):
                act.wait_ge(s["q_ps"], n + 1)
                act.wait_ge(s["q_lo"], from_zero(n - 1))
                a.activation(q_f[n % 2], (BC, BD)[n % 2][:], ACT.Identity, bias=bq_scaled[:, n // 2:n // 2 + 1],
                             scale=1.0 / SW).then_inc(s["q_f32"], 1)
            weight_hi(3, wo, w_stage[1], "wo_landed")
            act.wait_ge(s["last_ps"], 1)
            hi(klast[0], BE[:, 0:KC * B].rearrange("p (c b) -> p c b", c=KC), SK / (SX * SW)).then_inc(s["last_hi"], 1)
            act.wait_ge(s["last_ps"], 2)
            hi(vlast[0], BF[0:B, :], 1.0 / SW).then_inc(s["last_hi"], 1)
            act.wait_ge(s["ctx_landed0"], 16)
            hi(ctx_hl[0][0], ctx_stage[0], SX).then_inc(s["split_hi"], 1)

            def step(st, par, landed, cur=True, prev=True, nxt=True):
                n0 = st * 8

                def k_hi(c):
                    if cur:
                        act.wait_ge(s["proj_ps"], n0 + c + 1)
                        hi(kT[0][:, c, :, 0:LM], proj_banks[c % 2][:].rearrange("p (b x) -> p b x", b=PB),
                           SK / (SX * SW)).then_inc(s["proj_hi"], 1)

                def v_hi(t):
                    if cur:
                        act.wait_ge(s["proj_ps"], n0 + 5 + t)
                        hi(v_hl[par][0][:, t, :], proj_banks[t % 2][:], 1.0 / SW).then_inc(s["proj_hi"], 1)

                def exp(m, b):
                    act.wait_ge(s["s_neg"], m * 2 + 1 + b)
                    for j in range(b * KC, b * KC + KC):
                        a.activation(sm[:, j, :], sm[:, j, :], ACT.Exp, bias=neg_max[:, j:j + 1],
                                     scale=ISD / (SX * SK), accum_out=score_sums[:, j:j + 1]
                                     ).then_inc(s["exp_done"], 1)

                def p_hi(m, b):
                    act.wait_ge(s["recip_done"], m * 2 + 1 + b)
                    for j in range(b * KC, b * KC + KC):
                        hi(p_hl[0][:, j, 0:L], sm[:, j, :], recip[:, j:j + 1]).then_inc(s["p_hi"], 1)

                def pt_copy(b):
                    act.wait_ge(s["pt_ps"], st * 5 - 5 + (2, 5)[b])
                    a.activation(pT[:, b, 1].rearrange("p h c x -> p (h c x)"), BF[:].bitcast(F16), ACT.Copy
                                 ).then_inc(s["pt_act"], 1)

                if prev:
                    exp(st - 1, 1)
                k_hi(0)
                if prev:
                    p_hi(st - 1, 1)
                k_hi(1)
                if prev:
                    pt_copy(0)
                if nxt:
                    act.wait_ge(s[f"ctx_landed{1 - par}"], landed)
                    hi(ctx_hl[1 - par][0], ctx_stage[1 - par], SX).then_inc(s["split_hi"], 1)
                k_hi(2)
                if prev:
                    pt_copy(1)
                k_hi(3)
                if prev:
                    act.wait_ge(s["att_copied"], from_zero(st - 1))
                    for b in range(PB):
                        act.wait_ge(s["pv_ps"], st * 2 - 1 + b)
                        for r in range(HC):
                            rows = slice(r * DK, (r + 1) * DK)
                            last = hi(att_st[0][rows, :, b, :],
                                      (BG, BH)[b][rows, :].rearrange("p (c x) -> p c x", c=KC)[:, :, r * S:(r + 1) * S],
                                      1.0 / SP_)
                        last.then_inc(s["pv_hi"], 1)
                v_hi(0)
                v_hi(1)
                if cur:
                    exp(st, 0)
                v_hi(2)
                if cur:
                    p_hi(st, 0)
                v_hi(3)

            step(0, 0, 16, prev=False)
            step(1, 1, 32)
            with act.Fori(1, STEPS // 2 - 1) as k:
                step(k * 2, 0, k * 16 + 16)
                step(k * 2 + 1, 1, k * 16 + 32)
            step(STEPS - 2, 0, STEPS // 2 * 16)
            step(STEPS - 1, 1, 0, nxt=False)
            step(STEPS, 0, 0, cur=False, nxt=False)

            act.wait_ge(s["ab_landed"], 16)
            hi(ab[0], ab_stage, SW).then_inc(s["ab_split"], 1)
            for m in range(3):
                act.wait_ge(s[f"wt_landed{m}"], 16)
                act.wait_ge(s["fold_ps"], 4 * m)
                hi(wt[0][0], wt_stage[m], SW).then_inc(s["wt_hi"], 1)
                for c in range(KC):
                    n = m * KC + c
                    act.wait_ge(s["fold_ps"], n + 1)
                    hi(wf[m][0][:, c, :], (BC, BD)[n % 2][:], SF / (SW * SW)).then_inc(s["fold_hi"], 1)
            act.wait_ge(s["abias_ps"], 1)
            hi(dft_bias, BE[:, 0:KC * 4].rearrange("p (c m) -> p c m", c=KC), 1.0 / (SW * SW)).then_inc(s["abias_done"], 1)
            for t in range(NT):
                act.wait_ge(s["tr_ps"], NT + t + 1)
                hi(ln1T[0][:, :, t * P:(t + 1) * P], proj_banks[t % 2][:].rearrange("p (c x) -> p c x", c=KC), SX
                   ).then_inc(s["tr_hi"], 1)
            act.wait_ge(s["abias_done"], 1)
            for n in range(3 * KC * 2):
                m, c, half = SPEC_ORDER[n]
                act.wait_ge(s["spec_ps"], n + 1)
                a.activation(spec[m][:, c, half * D:(half + 1) * D], (BC, BD)[n % 2][:], ACT.Identity,
                             bias=dft_bias[:, c, m:m + 1], scale=1.0 / (SX * SF)).then_inc(s["spec_done"], 1)

            act.wait_ge(s["gate_landed"], 16 * 8)
            hi(wg_hl[0], wg_stage, SG).then_inc(s["wg_split"], 1)
            for t in range(NT):
                act.wait_ge(s["ln_out"], 2 * NT + t + 1)
                hi(l2_hl[0][:, t, :], l2_f[:, t, :], SX).then_inc(s["l2_hi"], 1)
                if t >= 1:
                    gate_transpose_out(act, a, t - 1)
            gate_transpose_out(act, a, NT - 1)

            def piece_hi(n, k):
                act.wait_ge(s[f"e_landed{k % 4}"], n * 32 + (16 * (k // 4) + 16))
                hi(w_hl[k][0], e_stage[k % 4], SG if k < 4 else S2).then_inc(s["e_hi"], 1)

            def expert(n, nxt=True):
                for k in range(FC // 2):
                    act.wait_ge(s["h_ps"], n * 8 + k + 1)
                    act.wait_ge(s["h_lo"], from_zero(n * 8 + k - 1))
                    a.activation(hid_f[k % 2], proj_banks[k % 2][:, 0:2 * CAP].rearrange("p (c x) -> p c x", c=2),
                                 ACT.Gelu_apprx_tanh, scale=1.0 / (SX * SG)).then_inc(s["gelu_done"], 1)
                    if nxt and k % 2:
                        piece_hi(n + 1, k // 2)
                for c in range(KC):
                    act.wait_ge(s["y_ps"], n * 4 + c + 1)
                    hi(yT[:, c, :], (BC, BD)[c % 2][:, 0:CAP], 1.0 / (S2 * SH)).then_inc(s["y_done"], 1)
                    if nxt:
                        piece_hi(n + 1, 4 + c)

            def round_(r):
                act.wait_ge(s["y_ps"], r * (4 * E))
                for k in range(PIECES):
                    piece_hi(r * E, k)
                expert(r * E)
                with act.Fori(1, E - 1) as e:
                    expert(r * E + e)
                expert(r * E + (E - 1), nxt=False)

            act.wait_ge(s["spec_ps"], 3 * KC * 2)
            act.wait_ge(s["unbound"], 2)
            round_(0)
            act.wait_ge(s["routed"], 1)
            with act.If(act.value_load(more_rounds[0:1, 0:1], min_val=0, max_val=1) > 0):
                with act.Fori(1, ROUNDS) as r:
                    round_(r)

        @block.vector
        def _(dve):
            v = nc.vector
            chain = count(1)

            def lo(dst, src, scale, h):
                return v.scalar_tensor_tensor(dst, src, scale, h, ALU.mult, ALU.subtract)

            def layer_norm(n, dst):
                for t in range(NT):
                    last = v.bn_stats(stats[:, t, :], x_tok[:, t, :])
                last.then_inc(s["chain_dve"], 1)
                dve.wait_ge(s["chain_dve"], next(chain))
                for t in range(NT):
                    last = v.bn_aggr(mean_var[:, t, :], stats[:, t, :])
                last.then_inc(s["chain_dve"], 1)
                dve.wait_ge(s["chain_dve"], next(chain))
                v.tensor_scalar(var_eps, mean_var[:, :, 1], EPS, None, ALU.add).then_inc(s["ln_var"], 1)
                dve.wait_ge(s["ln_rstd"], n)
                for t in range(NT):
                    v.tensor_scalar(dst[:, t, :], x_tok[:, t, :], mean_var[:, t, 0:1], rstd[:, t:t + 1],
                                    ALU.subtract, ALU.mult).then_inc(s["ln_out"], 1)

            def weight_lo(n, w, src):
                dve.wait_ge(s["w_hi"], n + 1)
                lo(w[1], src, SW, w[0]).then_inc(s["w_lo"], 1)

            dve.wait_ge(s["x_landed"], 16)
            layer_norm(1, xhat0)
            dve.wait_ge(s["consts_landed"], 16 * (7 + HC))
            v.tensor_scalar(bq_scaled, bq_col, SX, None, ALU.mult)
            v.tensor_scalar(mask_bias, mask_int, 0.0, NEG, ALU.is_equal, ALU.mult).then_inc(s["chain_dve"], 1)
            dve.wait_ge(s["chain_dve"], next(chain))
            for n in range(2):
                k_bias = kT[n][:, :, :, L]
                src = bk_col.unsqueeze(2).broadcast_to((P, KC, PB))
                if n == 0:
                    v.tensor_scalar(k_bias, src, SK, None, ALU.mult).then_inc(s["chain_dve"], 1)
                    dve.wait_ge(s["chain_dve"], next(chain))
                else:
                    v.scalar_tensor_tensor(k_bias, src, SK, kT[0][:, :, :, L], ALU.mult, ALU.subtract)
            bv_all = bv_col.unsqueeze(2).broadcast_to((P, KC, P))
            v.tensor_scalar(bv_bc[0], bv_all, SW, None, ALU.mult).then_inc(s["chain_dve"], 1)
            dve.wait_ge(s["chain_dve"], next(chain))
            lo(bv_bc[1], bv_all, SW, bv_bc[0])
            weight_lo(0, wq, w_stage[0])
            weight_lo(1, wk, w_stage[1])
            for t in range(NT):
                dve.wait_ge(s["tr_hi"], t + 1)
                lo(lnT[1][:, :, t * P:(t + 1) * P], proj_banks[t % 2][:].rearrange("p (c x) -> p c x", c=KC), SX,
                   lnT[0][:, :, t * P:(t + 1) * P]).then_inc(s["tr_free"], 1)
            dve.wait_ge(s["ctxl_split"], 1)
            lo(ctxl[1], ctxl_stage, SX, ctxl[0]).then_inc(s["ctxl_split"], 1)
            weight_lo(2, wv, w_stage[0])
            for n in range(KC * 2):
                c, half = divmod(n, 2)
                cols = slice(half * D, (half + 1) * D)
                dve.wait_ge(s["q_hi"], n + 1)
                v.tensor_tensor(qT[1][:, c, cols], q_f[n % 2], qT[0][:, c, cols], ALU.subtract).then_inc(s["q_lo"], 1)
            weight_lo(3, wo, w_stage[1])
            dve.wait_ge(s["last_hi"], 1)
            lo(klast[1], BE[:, 0:KC * B].rearrange("p (c b) -> p c b", c=KC), SK / (SX * SW), klast[0]
               ).then_inc(s["last_lo"], 1)
            dve.wait_ge(s["last_hi"], 2)
            lo(vlast[1], BF[0:B, :], 1.0 / SW, vlast[0]).then_inc(s["last_lo"], 1)
            dve.wait_ge(s["bias_landed"], 16)
            dve.wait_ge(s["bias_ps"], 1)
            v.scalar_tensor_tensor(bias_tile, BG[:], 1.0 / (SW * SW), bo_bc, ALU.mult, ALU.add
                                   ).then_inc(s["bias_done"], 1)
            dve.wait_ge(s["split_hi"], 1)
            lo(ctx_hl[0][1], ctx_stage[0], SX, ctx_hl[0][0]).then_inc(s["split_lo"], 1)
            dve.wait_ge(s["x_biased"], 1)
            dve.wait_ge(s["vlast_stored"], 32)

            def step(st, par, cur=True, prev=True, nxt=True):
                n0 = st * 8

                def k_lo(c):
                    if cur:
                        dve.wait_ge(s["proj_hi"], n0 + c + 1)
                        lo(kT[1][:, c, :, 0:LM], proj_banks[c % 2][:].rearrange("p (b x) -> p b x", b=PB),
                           SK / (SX * SW), kT[0][:, c, :, 0:LM]).then_inc(s["proj_free"], 1)

                def v_lo(t):
                    if cur:
                        dve.wait_ge(s["proj_hi"], n0 + 5 + t)
                        lo(v_hl[par][1][:, t, :], proj_banks[t % 2][:], 1.0 / SW, v_hl[par][0][:, t, :]
                           ).then_inc(s["proj_free"], 1)

                def scores(j):
                    bank = (BC, BD)[j % 2]
                    dve.wait_ge(s["s_ps"], n0 + j + 1)
                    v.scalar_tensor_tensor(sm[:, j, :], bank[:, 0:L], bank[:, L:L + 1], mask_bias,
                                           ALU.add, ALU.add).then_inc(s["s_free"], 1)

                def maxima(b):
                    js = slice(b * KC, b * KC + KC)
                    dve.wait_ge(s["s_free"], n0 + 4 + 4 * b)
                    v.reduce_max(row_max[:, js], sm[:, js, :], AX_X).then_inc(s["s_max"], 1)
                    dve.wait_ge(s["s_max"], st * 2 + 1 + b)
                    v.tensor_scalar(neg_max[:, js], row_max[:, js], -ISD / (SX * SK), None, ALU.mult
                                    ).then_inc(s["s_neg"], 1)

                def reciprocals(m, b):
                    js = slice(b * KC, b * KC + KC)
                    dve.wait_ge(s["exp_done"], m * 8 + 4 + 4 * b)
                    v.tensor_scalar(sums_scaled[:, js], score_sums[:, js], 1.0 / SP_, None, ALU.mult
                                    ).then_inc(s["sums_sc"], 1)
                    dve.wait_ge(s["sums_sc"], m * 2 + 1 + b)
                    v.reciprocal(recip[:, js], sums_scaled[:, js]).then_inc(s["recip_done"], 1)

                def p_lo(m, b):
                    for j in range(b * KC, b * KC + KC):
                        dve.wait_ge(s["p_hi"], m * 8 + 1 + j)
                        v.scalar_tensor_tensor(p_hl[1][:, j, 0:L], sm[:, j, :], recip[:, j:j + 1],
                                               p_hl[0][:, j, 0:L], ALU.mult, ALU.subtract
                                               ).then_inc(s["p_lo"], 1)

                def pt_copy(b):
                    dve.wait_ge(s["pt_ps"], st * 5 - 5 + (1, 4)[b])
                    v.tensor_copy(pT[:, b, 0].rearrange("p h c x -> p (h c x)"), BE[:].bitcast(F16)
                                  ).then_inc(s["pt_dve"], 1)

                if prev:
                    reciprocals(st - 1, 1)
                k_lo(0)
                if prev:
                    p_lo(st - 1, 1)
                k_lo(1)
                if prev:
                    pt_copy(0)
                k_lo(2)
                if prev:
                    dve.wait_ge(s["pt_ps"], st * 5 - 2)
                    v.tensor_tensor(pT_last,
                                    BH[0:2 * PAIRS, 0:P // 2].bitcast(F16).unsqueeze(1).broadcast_to((2 * PAIRS, PAIRS, P)),
                                    diag[0:2 * PAIRS].unsqueeze(2).broadcast_to((2 * PAIRS, PAIRS, P)),
                                    ALU.mult).then_inc(s["pt_dve"], 1)
                    pt_copy(1)
                if nxt:
                    dve.wait_ge(s["split_hi"], st + 2)
                    lo(ctx_hl[1 - par][1], ctx_stage[1 - par], SX, ctx_hl[1 - par][0]).then_inc(s["split_lo"], 1)
                k_lo(3)
                if prev:
                    for b in range(PB):
                        dve.wait_ge(s["pv_hi"], st * 2 - 1 + b)
                        for r in range(HC):
                            rows = slice(r * DK, (r + 1) * DK)
                            last = lo(att_st[1][rows, :, b, :],
                                      (BG, BH)[b][rows, :].rearrange("p (c x) -> p c x", c=KC)[:, :, r * S:(r + 1) * S],
                                      1.0 / SP_, att_st[0][rows, :, b, :])
                        last.then_inc(s["pv_free"], 1)
                v_lo(0)
                if cur:
                    scores(0)
                    scores(1)
                v_lo(1)
                if cur:
                    scores(2)
                    scores(3)
                    maxima(0)
                    scores(4)
                    scores(5)
                    reciprocals(st, 0)
                v_lo(2)
                if cur:
                    scores(6)
                    scores(7)
                    maxima(1)
                v_lo(3)
                if cur:
                    p_lo(st, 0)

            step(0, 0, prev=False)
            step(1, 1)
            with dve.Fori(1, STEPS // 2 - 1) as k:
                step(k * 2, 0)
                step(k * 2 + 1, 1)
            step(STEPS - 2, 0)
            step(STEPS - 1, 1, nxt=False)
            step(STEPS, 0, cur=False, nxt=False)

            for t in range(NT):
                dve.wait_ge(s["wo_ps"], t + 1)
                last = v.scalar_tensor_tensor(x_tok[:, t, :], (BA, BB, BC, BD)[t % 4][:], 1.0 / (SX * SW), x_tok[:, t, :],
                                              ALU.mult, ALU.add).then_inc(s["x1_done"], 1)
            dve.wait_ge(s["x1_done"], NT)
            layer_norm(2, xhat1)
            dve.wait_ge(s["ab_split"], 1)
            lo(ab[1], ab_stage, SW, ab[0]).then_inc(s["ab_split"], 1)
            for m in range(3):
                dve.wait_ge(s["wt_hi"], m + 1)
                lo(wt[0][1], wt_stage[m], SW, wt[0][0]).then_inc(s["wt_lo"], 1)
                for c in range(KC):
                    n = m * KC + c
                    dve.wait_ge(s["fold_hi"], n + 1)
                    lo(wf[m][1][:, c, :], (BC, BD)[n % 2][:], SF / (SW * SW), wf[m][0][:, c, :]).then_inc(s["fold_free"], 1)
            for t in range(NT):
                dve.wait_ge(s["tr_hi"], NT + t + 1)
                lo(ln1T[1][:, :, t * P:(t + 1) * P], proj_banks[t % 2][:].rearrange("p (c x) -> p c x", c=KC), SX,
                   ln1T[0][:, :, t * P:(t + 1) * P]).then_inc(s["tr_free"], 1)

            dve.wait_ge(s["spec_done"], 2 * KC * 2)
            kre, kim = spec[1][:, 0:2, :], spec[1][:, 2:4, :]
            vre, vim = spec[2][:, 0:2, :], spec[2][:, 2:4, :]
            for n, (p_, q_) in enumerate(((kre, vre), (kim, vim), (kre, vim), (kim, vre))):
                v.tensor_tensor(prod, p_, q_, ALU.mult).then_inc(s["chain_dve"], 1)
                dve.wait_ge(s["chain_dve"], next(chain))
                v.reduce_sum(bind_sums[:, n], prod.rearrange("p c (b q) -> p c b q", q=S), AX_X).then_inc(s["chain_dve"], 1)
                dve.wait_ge(s["chain_dve"], next(chain))
            rr, ii, ri, ir = (bind_sums[:, n] for n in range(4))
            a1, a2, b2 = (lhs_bind[:, n] for n in range(3))
            v.tensor_tensor(a1, rr, ii, ALU.subtract)
            v.tensor_tensor(a2, ri, ir, ALU.add)
            v.tensor_tensor(b2, ii, rr, ALU.subtract).then_inc(s["chain_dve"], 1)
            dve.wait_ge(s["chain_dve"], next(chain))
            v.tensor_copy(a1[0:1, 0, :], rr[0:1, 0, :])
            v.tensor_copy(b2[0:1, 0, :], ii[0:1, 0, :])
            v.memset(a2[0:1, 0, :], 0.0).then_inc(s["chain_dve"], 1)
            dve.wait_ge(s["chain_dve"], next(chain))

            def over_tokens(z):
                return z.unsqueeze(3).broadcast_to((P, 2, B // 2, S))

            for half in range(2):
                dve.wait_ge(s["spec_done"], 2 * KC * 2 + KC * (half + 1))
                bs = slice(half * (B // 2), (half + 1) * (B // 2))
                cols = slice(half * D, (half + 1) * D)
                four = "p c (b q) -> p c b q"
                qre, qim = (spec[0][:, n:n + 2, cols].rearrange(four, q=S) for n in (0, 2))
                pre, pim = (spec[1][:, n:n + 2, cols].rearrange(four, q=S) for n in (0, 2))
                tmp = prod[:, :, cols].rearrange(four, q=S)
                for dst, (c0, c1) in ((pre, (a1, a2)), (pim, (a2, b2))):
                    v.tensor_tensor(dst, qre, over_tokens(c0[:, :, bs]), ALU.mult)
                    v.tensor_tensor(tmp, qim, over_tokens(c1[:, :, bs]), ALU.mult).then_inc(s["chain_dve"], 1)
                    dve.wait_ge(s["chain_dve"], next(chain))
                    v.tensor_tensor(dst, dst, tmp, ALU.add).then_inc(s["chain_dve"], 1)
                    dve.wait_ge(s["chain_dve"], next(chain))
                v.memset(row_max[:, 0:1], 0.0).then_inc(s["unbound"], 1)
            for t in range(NT):
                dve.wait_ge(s["irfft_ps"], t + 1)
                v.tensor_tensor(x_tok[:, t, :], (BA, BB, BE, BF)[t % 4][:], x_tok[:, t, :], ALU.add
                                ).then_inc(s["x2_done"], 1)


            dve.wait_ge(s["x2_done"], NT)
            layer_norm(3, l2_f)
            dve.wait_ge(s["wg_split"], 1)
            lo(wg_hl[1], wg_stage, SG, wg_hl[0]).then_inc(s["wg_split"], 1)
            for t in range(NT):
                dve.wait_ge(s["l2_hi"], t + 1)
                lo(l2_hl[1][:, t, :], l2_f[:, t, :], SX, l2_hl[0][:, t, :]).then_inc(s["l2_lo"], 1)

            def by_tile(z):
                return z.unsqueeze(1).broadcast_to((P, NT, E))

            def by_expert(z):
                return z.unsqueeze(2).broadcast_to((P, NT, E))

            dve.wait_ge(s["logits_ps"], 1)
            v.scalar_tensor_tensor(
                logits, BC[:, 0:NT * E].rearrange("p (t e) -> p t e", e=E), 1.0 / (SX * SG), by_tile(bg_bc),
                ALU.mult, ALU.add).then_inc(s["chain_dve"], 1)
            dve.wait_ge(s["chain_dve"], next(chain))
            v.reduce_max(top, logits, AX_X).then_inc(s["chain_dve"], 1)
            dve.wait_ge(s["chain_dve"], next(chain))
            v.tensor_tensor(is_max, logits, by_expert(top), ALU.is_equal).then_inc(s["chain_dve"], 1)
            dve.wait_ge(s["chain_dve"], next(chain))
            v.tensor_tensor(score, is_max, by_tile(rank_order), ALU.mult).then_inc(s["chain_dve"], 1)
            dve.wait_ge(s["chain_dve"], next(chain))
            v.reduce_max(top2, score, AX_X).then_inc(s["chain_dve"], 1)
            dve.wait_ge(s["chain_dve"], next(chain))
            v.tensor_tensor(onehot, score, by_expert(top2), ALU.is_equal).then_inc(s["chain_dve"], 1)
            dve.wait_ge(s["chain_dve"], next(chain))
            v.tensor_copy(onehot16, onehot).then_inc(s["onehot_done"], 1)
            dve.wait_ge(s["rank_ps"], 1)
            v.scalar_tensor_tensor(
                slot_of, BD[:, 0:NT * E].rearrange("p (t e) -> p t e", e=E), 1.0, onehot, ALU.add, ALU.mult).then_inc(s["chain_dve"], 1)
            dve.wait_ge(s["chain_dve"], next(chain))
            v.tensor_scalar(slot_of, slot_of, -1.0, None, ALU.add).then_inc(s["chain_dve"], 1)
            dve.wait_ge(s["chain_dve"], next(chain))
            v.reduce_max(most, BE[:, 0:E], AX_X).then_inc(s["chain_dve"], 1)
            dve.wait_ge(s["chain_dve"], next(chain))
            v.tensor_scalar(more_rounds, most, float(CAP), None, ALU.is_gt).then_inc(s["routed"], 1)

            def slots(n, e):
                dve.wait_ge(s["xs_ps"], n * 4)
                v.tensor_tensor(perm, slot_iota.unsqueeze(1).broadcast_to((P, NT, CAP)),
                                slot_of[:, :, bass.ds(e, 1)].broadcast_to((P, NT, CAP)), ALU.is_equal
                                ).then_inc(s["perm_done"], 1)

            def piece_lo(n, k):
                dve.wait_ge(s["e_hi"], n * 8 + k + 1)
                lo(w_hl[k][1], e_stage[k % 4], SG if k < 4 else S2, w_hl[k][0]).then_inc(s["e_lo"], 1)

            def gathered(n):
                for c in range(KC):
                    dve.wait_ge(s["xs_ps"], n * 4 + c + 1)
                    v.tensor_copy(xs[:, c].rearrange("p h x -> p (h x)"), (BG, BH)[c % 2][:, 0:2 * CAP]
                                  ).then_inc(s["xs_done"], 1)

            def take_ids(n):
                v.tensor_tensor(ids_next[0], BH[:, 2 * CAP:2 * CAP + 2], id_offset, ALU.add)
                v.tensor_tensor(ids_next[1], BH[0:CB, 2 * CAP + 2:2 * CAP + 4], id_offset[0:CB], ALU.add
                                ).then_inc(s["ids_done"], 1)

            def rows_out(n):
                dve.wait_ge(s["yt_ps"], n + 1)
                dve.wait_ge(s["rows_landed"], n * 32 + 32)
                v.tensor_tensor(y_rows[0], BE[:], x2_rows[0], ALU.add)
                v.tensor_tensor(y_rows[1], BF[0:CB, :], x2_rows[1], ALU.add).then_inc(s["y_out"], 1)

            def expert(n, e, prev=True, nxt=True):
                if nxt:
                    slots(n + 1, e + 1)
                for k in range(FC // 2):
                    dve.wait_ge(s["h_hi"], n * 8 + k + 1)
                    v.scalar_tensor_tensor(hid_hl[1][:, 2 * k:2 * k + 2, :], hid_f[k % 2], SH,
                                           hid_hl[0][:, 2 * k:2 * k + 2, :], ALU.mult, ALU.subtract
                                           ).then_inc(s["h_lo"], 1)
                    if nxt and k % 2:
                        piece_lo(n + 1, k // 2)
                if prev:
                    rows_out(n - 1)
                if nxt:
                    gathered(n + 1)
                    for c in range(KC):
                        piece_lo(n + 1, 4 + c)
                dve.wait_ge(s["ids_done"], n + 1)
                dve.wait_ge(s["scattered"], n * 32)
                v.tensor_copy(ids[0], ids_next[0])
                v.tensor_copy(ids[1], ids_next[1]).then_inc(s["shifted"], 1)
                if nxt:
                    dve.wait_ge(s["shifted"], n + 1)
                    take_ids(n + 1)

            def round_(r, first):
                if not first:
                    v.tensor_scalar(slot_of, slot_of, -float(CAP), None, ALU.add).then_inc(s["ranks_moved"], 1)
                    dve.wait_ge(s["ranks_moved"], r)
                slots(r * E, 0)
                for k in range(PIECES):
                    piece_lo(r * E, k)
                gathered(r * E)
                take_ids(r * E)
                expert(r * E, 0, prev=False)
                with dve.Fori(1, E - 1) as e:
                    expert(r * E + e, e)
                expert(r * E + (E - 1), E - 1, nxt=False)
                rows_out(r * E + (E - 1))

            round_(0, True)
            dve.wait_ge(s["routed"], 1)
            with dve.If(dve.value_load(more_rounds[0:1, 0:1], min_val=0, max_val=1) > 0):
                with dve.Fori(1, ROUNDS) as r:
                    round_(r, False)

        @block.tensor
        def _(pe):
            m = nc.tensor

            def product(out_ap, pairs):
                pairs = list(pairs)
                for n, (w, x) in enumerate(pairs):
                    last = m.matmul(out_ap, w, x, start=(n == 0), stop=(n == len(pairs) - 1))
                return last

            def split_product(out_ap, w, x, wi, xi):
                return product(out_ap, [(u[wi(c)], z[xi(c)]) for c in range(KC) for u, z in hl_passes(w, x)])

            def transpose_tokens(base, src):
                for t in range(NT):
                    pe.wait_ge(s["ln_out"], base + t + 1)
                    pe.wait_ge(s["tr_free"], from_zero(base + t - 1))
                    for c in range(KC):
                        last = m.transpose(proj_banks[t % 2][:, c * P:(c + 1) * P], src[:, t, c * P:(c + 1) * P], ident)
                    last.then_inc(s["tr_ps"], 1)

            pe.wait_ge(s["consts_landed"], 16 * (7 + HC))
            transpose_tokens(0, xhat0)
            pe.wait_ge(s["tr_free"], NT)
            pe.wait_ge(s["w_lo"], 1)
            for n in range(KC * 2):
                c, half = divmod(n, 2)
                pe.wait_ge(s["q_f32"], from_zero(n - 1))
                split_product((BC, BD)[n % 2][:], wq, lnT,
                              lambda k: (slice(None), k, slice(c * P, (c + 1) * P)),
                              lambda k: (slice(None), k, slice(half * D, (half + 1) * D))).then_inc(s["q_ps"], 1)
            pe.wait_ge(s["w_lo"], 3)
            pe.wait_ge(s["ctxl_split"], 2)
            for c in range(KC):
                last = split_product(BE[:, c * B:(c + 1) * B], wk, ctxl,
                                     lambda k: (slice(None), k, slice(c * P, (c + 1) * P)),
                                     lambda k: (slice(None), k, slice(None)))
            last.then_inc(s["last_ps"], 1)
            split_product(BF[0:B, :], ctxl, wv, lambda k: (slice(None), k, slice(None)),
                          lambda k: (slice(None), k, slice(None))).then_inc(s["last_ps"], 1)
            pe.wait_ge(s["w_lo"], 4)
            split_product(BG[:], bv_bc, wo, lambda k: (slice(None), k, slice(None)),
                          lambda k: (slice(None), k, slice(None))).then_inc(s["bias_ps"], 1)
            pe.wait_ge(s["bias_done"], 1)
            pe.wait_ge(s["last_lo"], 2)
            pe.wait_ge(s["q_lo"], KC * 2)

            def step(st, par, cur=True, prev=True):
                n0 = st * 8

                def k_proj(c):
                    if cur:
                        pe.wait_ge(s["proj_free"], from_zero(n0 + c - 1))
                        split_product(proj_banks[c % 2][:], wk, ctx_hl[par],
                                      lambda k: (slice(None), k, slice(c * P, (c + 1) * P)),
                                      lambda k: (slice(None), k, slice(None))).then_inc(s["proj_ps"], 1)

                def v_proj(t):
                    if cur:
                        pe.wait_ge(s["proj_free"], n0 + 3 + t)
                        split_product(proj_banks[t % 2][:], ctx_hl[par], wv,
                                      lambda k: (slice(None), k, slice(t * P, (t + 1) * P)),
                                      lambda k: (slice(None), k, slice(None))).then_inc(s["proj_ps"], 1)

                def p_transposes(b):
                    for kt in range(2):
                        bank = (BE, BF)[kt][:].bitcast(F16)
                        for n in range(2):
                            for c in range(KC):
                                slot = n * KC + c
                                last = m.transpose(bank[:, slot * P:(slot + 1) * P],
                                                   p_hl[n][:, b * KC + c, kt * P:(kt + 1) * P], ident16)
                        last.then_inc(s["pt_ps"], 1)

                def attention(b):
                    vv = v_hl[1 - par]
                    for c in range(KC):
                        cols = slice(c * P, (c + 1) * P)
                        j = b * KC + c
                        pairs = [(vv[u][:, b * 2 + kt, cols], pT[:, b, kt, z, c, :])
                                 for kt in range(2) for u, z in ((0, 0), (0, 1), (1, 0))]
                        pairs += [(vl_cur[:, 0, :], pT_last[:, j, :]),
                                  (vl_cur[0:PAIRS, 1, :], pT_last[0:PAIRS, j, :])]
                        last = product((BG, BH)[b][:, cols], pairs)
                    last.then_inc(s["pv_ps"], 1)

                def scores(j):
                    b, c = divmod(j, KC)
                    pe.wait_ge(s["s_free"], from_zero(n0 + j - 1))
                    product((BC, BD)[j % 2][:, 0:L + 1],
                            [(u[:, c, b, :], z[:, c, b, :]) for u, z in hl_passes(q_bd, kT)]
                            ).then_inc(s["s_ps"], 1)

                if cur:
                    pe.wait_ge(s["split_lo"], st + 1)
                k_proj(0)
                k_proj(1)
                if prev:
                    pe.wait_ge(s["p_lo"], st * 8 - 4)
                    p_transposes(0)
                k_proj(2)
                if prev:
                    pe.wait_ge(s["p_lo"], st * 8)
                    pe.wait_ge(s["pv_free"], from_zero(st * 2 - 2))
                    m.transpose(BH[0:2 * PAIRS, 0:P // 2].bitcast(F16),
                                p_all[:, :, :, LM].rearrange("p h j -> p (h j)"), ident16).then_inc(s["pt_ps"], 1)
                    pe.wait_ge(s["pt_dve"], st * 3 - 2)
                    pe.wait_ge(s["pt_act"], st * 2 - 1)
                    p_transposes(1)
                k_proj(3)
                if prev:
                    pe.wait_ge(s["vl_ready"], st)
                    for b in range(PB):
                        pe.wait_ge(s["pt_dve"], st * 3 - 1 + b)
                        pe.wait_ge(s["pt_act"], st * 2 - 1 + b)
                        attention(b)
                v_proj(0)
                if cur:
                    pe.wait_ge(s["q_ready"], st + 1)
                    pe.wait_ge(s["proj_free"], n0 + 4)
                    scores(0)
                    scores(1)
                v_proj(1)
                if cur:
                    scores(2)
                    scores(3)
                v_proj(2)
                if cur:
                    scores(4)
                    scores(5)
                v_proj(3)
                if cur:
                    scores(6)
                    scores(7)

            step(0, 0, prev=False)
            step(1, 1)
            with pe.Fori(1, STEPS // 2 - 1) as k:
                step(k * 2, 0)
                step(k * 2 + 1, 1)
            step(STEPS - 2, 0)
            step(STEPS - 1, 1)
            step(STEPS, 0, cur=False)

            pe.wait_ge(s["att_copied"], STEPS)
            for t in range(NT):
                pe.wait_ge(s["x1_done"], from_zero(t - 3))
                split_product((BA, BB, BC, BD)[t % 4][:], attT, wo,
                              lambda k: (slice(None), k, slice(t * P, (t + 1) * P)),
                              lambda k: (slice(None), k, slice(None))).then_inc(s["wo_ps"], 1)
            pe.wait_ge(s["x1_done"], NT)

            pe.wait_ge(s["dft_landed"], 32)
            for mm in range(3):
                pe.wait_ge(s["wt_lo"], mm + 1)
                for c in range(KC):
                    n = mm * KC + c
                    pe.wait_ge(s["fold_free"], from_zero(n - 1))
                    split_product((BC, BD)[n % 2][:], wt[0], dft,
                                  lambda k: (slice(None), k, slice(c * P, (c + 1) * P)),
                                  lambda k: (slice(None), k, slice(None))).then_inc(s["fold_ps"], 1)
            pe.wait_ge(s["ab_split"], 2)
            for c in range(KC):
                last = split_product(BE[:, c * 4:(c + 1) * 4], dft, ab,
                                     lambda k: (slice(None), k, slice(c * P, (c + 1) * P)),
                                     lambda k: (slice(None), k, slice(None)))
            last.then_inc(s["abias_ps"], 1)
            transpose_tokens(NT, xhat1)
            pe.wait_ge(s["tr_free"], 2 * NT)
            pe.wait_ge(s["fold_free"], 3 * KC)
            for n in range(3 * KC * 2):
                mm, c, half = SPEC_ORDER[n]
                pe.wait_ge(s["spec_done"], from_zero(n - 1))
                split_product((BC, BD)[n % 2][:], wf[mm], ln1T,
                              lambda k: (slice(None), k, slice(c * P, (c + 1) * P)),
                              lambda k: (slice(None), k, slice(half * D, (half + 1) * D))).then_inc(s["spec_ps"], 1)
            pe.wait_ge(s["idft_landed"], 16)
            for t in range(NT):
                pe.wait_ge(s["unbound"], 1 + t // (NT // 2))
                pe.wait_ge(s["x2_done"], from_zero(t - 3))
                product((BA, BB, BE, BF)[t % 4][:],
                        [(spec[1][:, c, t * P:(t + 1) * P], idft[:, c, :]) for c in range(KC)]
                        ).then_inc(s["irfft_ps"], 1)


            pe.wait_ge(s["x2_done"], NT)
            for t in range(NT):
                pe.wait_ge(s["l2_lo"], t + 1)
                pe.wait_ge(s["lt_done"], from_zero(t - 1))
                bank = proj_banks[t % 2][:].bitcast(F16)
                for n in range(2):
                    for c in range(KC):
                        slot = n * KC + c
                        last = m.transpose(bank[:, slot * P:(slot + 1) * P], l2_hl[n][:, t, c * P:(c + 1) * P], ident16)
                last.then_inc(s["lt_ps"], 1)
            pe.wait_ge(s["wg_split"], 2)
            for t in range(NT):
                pe.wait_ge(s["lt_done"], t + 1)
                last = product(BC[:, t * E:(t + 1) * E],
                               [(l2T[:, t, u, c, :], wg_hl[z][:, c, :]) for c in range(KC)
                                for u, z in ((0, 0), (0, 1), (1, 0))])
            last.then_inc(s["logits_ps"], 1)
            pe.wait_ge(s["onehot_done"], 1)
            for t in range(NT):
                product(BD[:, t * E:(t + 1) * E],
                        [(tri16, onehot16[:, t, :])] + [(ones16, onehot16[:, k, :]) for k in range(t)])
            product(BE[:, 0:E], [(ones16, onehot16[:, k, :]) for k in range(NT)]).then_inc(s["rank_ps"], 1)
            pe.wait_ge(s["routed"], 1)

            def gather(n):
                pe.wait_ge(s["perm_done"], n + 1)
                for c in range(KC):
                    bank = (BG, BH)[c % 2]
                    pe.wait_ge(s["xs_done"], from_zero(n * 4 + c - 1))
                    if c == 1:
                        pe.wait_ge(s["ids_done"], n)
                    for z in range(2):
                        last = product(bank[:, z * CAP:(z + 1) * CAP],
                                       [(l2_hl[z][:, t, c * P:(c + 1) * P], perm[:, t, :]) for t in range(NT)])
                    if c == KC - 1:
                        product(bank[:, 2 * CAP:2 * CAP + 2], [(perm[:, t, 0:P], tok_ids[:, t, :]) for t in range(NT)])
                        last = product(bank[0:CB, 2 * CAP + 2:2 * CAP + 4],
                                       [(perm[:, t, P:CAP], tok_ids[:, t, :]) for t in range(NT)])
                    last.then_inc(s["xs_ps"], 1)

            def rows(n):
                pe.wait_ge(s["y_done"], n * 4 + 4)
                pe.wait_ge(s["y_out"], n)
                for c in range(KC):
                    m.transpose(BE[:, c * P:(c + 1) * P], yT[:, c, 0:P], ident)
                for c in range(KC):
                    last = m.transpose(BF[0:CB, c * P:(c + 1) * P], yT[:, c, P:CAP], ident)
                last.then_inc(s["yt_ps"], 1)

            def expert(n, prev=True, nxt=True):
                pe.wait_ge(s["xs_done"], n * 4 + 4)
                for k in range(FC // 2):
                    pe.wait_ge(s["e_lo"], n * 8 + k // 2 + 1)
                    pe.wait_ge(s["gelu_done"], from_zero(n * 8 + k - 1))
                    for f in range(2):
                        at = (2 * k + f) % 4 * P
                        w = [z.rearrange("p (c f) -> p c f", c=KC) for z in w_hl[k // 2]]
                        last = product(proj_banks[k % 2][:, f * CAP:(f + 1) * CAP],
                                       [(w[u][:, c, at:at + P], xs[:, c, z, :]) for c in range(KC)
                                        for u, z in ((0, 0), (0, 1), (1, 0))])
                    last.then_inc(s["h_ps"], 1)
                if prev:
                    rows(n - 1)
                if nxt:
                    gather(n + 1)
                for c in range(KC):
                    pe.wait_ge(s["e_lo"], n * 8 + 5 + c)
                    pe.wait_ge(s["y_done"], from_zero(n * 4 + c - 1))
                    if c == 0:
                        pe.wait_ge(s["h_lo"], n * 8 + 8)
                    w = [z.rearrange("p (f d) -> p f d", f=FC) for z in w_hl[4 + c]]
                    product((BC, BD)[c % 2][:, 0:CAP],
                            [(w[u][:, f, :], hid_hl[z][:, f, :]) for f in range(FC)
                             for u, z in ((0, 0), (0, 1), (1, 0))]).then_inc(s["y_ps"], 1)

            def round_(r):
                gather(r * E)
                expert(r * E, prev=False)
                with pe.Fori(1, E - 1) as e:
                    expert(r * E + e)
                expert(r * E + (E - 1), nxt=False)
                rows(r * E + (E - 1))

            round_(0)
            with pe.If(pe.value_load(more_rounds[0:1, 0:1], min_val=0, max_val=1) > 0):
                with pe.Fori(1, ROUNDS) as r:
                    round_(r)


SPEC_ORDER = [(m, c, h) for m in (1, 2) for c in range(KC) for h in range(2)] + \
             [(0, c, h) for h in range(2) for c in range(KC)]


def host_constants():
    import numpy as np
    n = np.arange(D)
    f = np.arange(NF)
    ang = 2 * np.pi * ((n[:, None] * f[None, :]) % D) / D
    fwd = np.concatenate([np.cos(ang), -np.sin(ang)], 1)
    fwd[:, NF] = np.where(n % 2, -1.0, 1.0)
    inv = fwd.T * (2.0 / D)
    inv[0] /= 2
    inv[NF] /= 2
    fs = fwd * SW
    h = fs.astype(np.float16)
    dft16 = np.stack([h, (fs - h).astype(np.float16)])

    def chunks(a):
        return np.ascontiguousarray(a.reshape(KC, P, -1).swapaxes(0, 1))
    return {
        "dft16": np.stack([chunks(a) for a in dft16]),
        "idft": chunks(inv.astype(np.float32)),
        "ident": np.eye(P, dtype=np.float32),
        "ident16": np.eye(P, dtype=np.float16),
        "own_head": np.repeat(np.eye(HC, dtype=np.float32), DK, 0),
        "slot_iota": np.tile(np.arange(CAP, dtype=np.float32), (P, 1)),
        "tri16": np.triu(np.ones((P, P), np.float16), 1),
        "ones16": np.ones((P, P), np.float16),
        "rank_order": np.tile(np.arange(E, 0, -1, dtype=np.float32), (P, 1)),
        "tok_ids": np.stack([np.arange(T), np.arange(T) - 2 * T], 1).reshape(NT, P, 2).swapaxes(0, 1).astype(np.float16),
        "id_offset": np.tile(np.array([0, 2 * T], np.float32), (P, 1)),
        "diag": np.tile(np.eye(PAIRS, dtype=np.float32), (2, 1)),
    }


def lay_out(x, ctx_1024, mask_1x1xSxS2_ik0, L0_xattn_Wq, L0_xattn_bq, L0_xattn_Wk, L0_xattn_bk, L0_xattn_Wv,
            L0_xattn_bv, L0_xattn_Wo, L0_xattn_bo, L0_attn_Wq, L0_attn_bq, L0_attn_Wk, L0_attn_bk, L0_attn_Wv,
            L0_attn_bv, L0_ffn_W1, L0_ffn_W2, L0_ffn_Wg, L0_ffn_bg):
    import numpy as np
    a = np.asarray

    def chunks(w):
        return np.ascontiguousarray(a(w).reshape(KC, P, -1).swapaxes(0, 1))

    def column(b):
        return np.ascontiguousarray(a(b).reshape(KC, P).T)
    c = a(ctx_1024)
    main = c[:, :LM].reshape(STEPS, PB, LM, KC, P).transpose(0, 4, 3, 1, 2).reshape(STEPS, P, KC, PB * LM)
    last = c[:, LM].reshape(B, KC, P).transpose(2, 1, 0)
    zero = np.zeros_like(a(L0_attn_bq))
    return {
        "x_t": np.ascontiguousarray(a(x).reshape(NT, P, D).swapaxes(0, 1)),
        "ctx_t": np.ascontiguousarray(main), "ctx_last": np.ascontiguousarray(last),
        "mask": np.ascontiguousarray(a(mask_1x1xSxS2_ik0).reshape(S, L)),
        "wq_t": chunks(a(L0_xattn_Wq).T), "wk_t": chunks(a(L0_xattn_Wk).T), "wv_t": chunks(a(L0_xattn_Wv).T),
        "wo_t": chunks(a(L0_xattn_Wo).T),
        "bq": column(L0_xattn_bq), "bk": column(L0_xattn_bk), "bv": column(L0_xattn_bv), "bo": a(L0_xattn_bo),
        "awt": np.stack([chunks(a(w).T) for w in (L0_attn_Wq, L0_attn_Wk, L0_attn_Wv)]),
        "wg": chunks(L0_ffn_Wg), "bg": a(L0_ffn_bg),
        "w1": np.ascontiguousarray(a(L0_ffn_W1).reshape(E, KC, P, 4, 512).transpose(0, 3, 2, 1, 4)).reshape(E * 4, P, -1),
        "w2": np.ascontiguousarray(a(L0_ffn_W2).reshape(E, FC, P, KC, P).transpose(0, 3, 2, 1, 4)).reshape(E * 4, P, -1),
        "ab": chunks(np.stack([a(L0_attn_bq), a(L0_attn_bk), a(L0_attn_bv), zero], 1)),
    }


def kernel(**inputs):
    import numpy as np
    import concourse.bacc as bacc
    from concourse.bass_utils import run_bass_kernel_spmd

    nc = bacc.Bacc("TRN2", target_bir_lowering=False, num_devices=1)
    arrays = {**lay_out(**inputs), **host_constants()}
    i = {n: nc.dram_tensor(f"in_{n}", a.shape, mybir.dt.from_np(a.dtype), kind="ExternalInput").ap()
         for n, a in arrays.items()}
    i["vlast_dram"] = nc.dram_tensor("vlast_dram", (2, B, D), F16, kind="Internal").ap()
    i["x2_dram"] = nc.dram_tensor("x2_dram", (T, D), F32, kind="Internal").ap()
    out = nc.dram_tensor("out", (B, S, D), F32, kind="ExternalOutput").ap()
    perceiver_block(nc, i, out)
    r = run_bass_kernel_spmd(nc, [{f"in_{n}": a for n, a in arrays.items()}], core_ids=[0])
    return r.results[0]["out"]
```

```python
from contextlib import ExitStack
from itertools import count

import concourse.bass as bass
from concourse import mybir

F32 = mybir.dt.float32
F16 = mybir.dt.float16
I32 = mybir.dt.int32
U32 = mybir.dt.uint32
ALU = mybir.AluOpType
ACT = mybir.ActivationFunctionType
AX_X = mybir.AxisListType.X

P = 128
B, S, D = 32, 32, 512
L = 257
H = 16
DK = D // H
KC = D // P
HC = P // DK
T = B * S
NT = T // P
PB = 2
STEPS = B // PB
LM = 256
PAIRS = PB * KC
E, FF = 8, 2048
FC = FF // P
CAP = 160
CB = CAP - P
ROUNDS = -(-T // CAP)
PIECES = 8
NF = D // 2
HT = NT // 2
EPS = 1e-5

SX = 2.0 ** 8
SW = 2.0 ** 12
SK = 2.0 ** 6
SP_ = 2.0 ** 12
SF = 2.0 ** 8
SG = 2.0 ** 6
S2 = 2.0 ** 7
SH = 2.0 ** 3
NEG = -1e30
ISD = 1.0 / (float(DK) ** 0.5)


def perceiver_block(nc, i, out):
    ctx = ExitStack()
    with ctx:
        def sem(name):
            return ctx.enter_context(nc.semaphore(name))

        KB = 1024
        arena = ctx.enter_context(nc.sbuf_tensor("arena", [P, 204 * KB // 4], F32))
        banks = [ctx.enter_context(nc.psum_tensor(f"bank{n}", [P, 512], F32)) for n in range(8)]
        BA, BB, BC, BD, BE, BF, BG, BH = banks
        proj_banks = (BA, BB)
        TR_BANKS = (BE, BF, BG, BH)

        def size(shape, dt):
            n = 2 if dt == F16 else 4
            for x in shape:
                n *= x
            return n

        def view(off, shape, dt, parts=P):
            n = size(shape, dt)
            assert off % 4 == 0 and n % 4 == 0 and off + n <= 204 * KB, (off, n)
            a = arena[0:parts, off // 4:(off + n) // 4]
            if dt != F32:
                a = a.bitcast(dt)
            if len(shape) > 1:
                names = [f"d{k}" for k in range(len(shape))]
                a = a.rearrange(f"p ({' '.join(names)}) -> p {' '.join(names)}",
                                **{k: v for k, v in zip(names, shape)})
            return a

        class Region:
            def __init__(self, start, end):
                self.at, self.end = start, end

            def take(self, shape, dt, parts=P):
                v = view(self.at, shape, dt, parts)
                self.at += -(-size(shape, dt) // 32) * 32
                assert self.at <= self.end, (self.at, self.end)
                return v

        keep = Region(0, 28 * KB)
        x_tok = keep.take([NT, D], F32)
        ident = keep.take([P], F32)
        ident16 = keep.take([P], F16)
        bq_col = keep.take([KC], F32)
        bq_scaled = keep.take([KC], F32)
        mask_bias = keep.take([L], F32)
        stats = keep.take([NT, 6], F32)
        mean_var = keep.take([NT, 2], F32)
        var_eps = keep.take([NT], F32)
        minus_half = keep.take([NT], F32)
        rstd = keep.take([NT], F32)
        score_sums = keep.take([PAIRS], F32)
        sums_scaled = keep.take([PAIRS], F32)
        recip = keep.take([PAIRS], F32)
        row_max = keep.take([PAIRS], F32)
        neg_max = keep.take([PAIRS], F32)
        diag = keep.take([PAIRS], F32)
        own_head = keep.take([HC], F32)
        dft_bias = keep.take([KC, 4], F32)
        lhs_bind = keep.take([3, 2, B], F32)
        bind_sums = keep.take([4, 2, B], F32)

        perm = keep.take([NT, CAP], F16)
        slot_iota = keep.take([CAP], F32)
        tri16 = keep.take([P], F16)
        ones16 = keep.take([P], F16)
        wg_stage = keep.take([KC, E], F32)
        wg_hl = [keep.take([KC, E], F16) for _ in range(2)]
        bg_bc = keep.take([E], F32)
        rank_order = keep.take([E], F32)
        tok_ids = keep.take([NT, 2], F16)
        id_offset = keep.take([2], F32)
        logits, is_max, score, onehot, slot_of = (keep.take([NT, E], F32) for _ in range(5))
        onehot16 = keep.take([NT, E], F16)
        top, top2 = (keep.take([NT], F32) for _ in range(2))
        most = keep.take([1], F32)
        more_rounds = keep.take([1], I32)
        ids_next = [keep.take([2], I32), keep.take([2], I32, parts=CB)]
        ids = [keep.take([2], I32), keep.take([2], I32, parts=CB)]
        ab_stage = keep.take([2, 2, 4], F32)
        ab_sd = keep.take([2, 2, 4], F32)
        ab = [keep.take([2, 2, 4], F16) for _ in range(2)]

        xa = Region(28 * KB, 204 * KB)
        q_off = xa.at
        qT = [xa.take([KC, T], F16) for _ in range(2)]
        wk_off = xa.at
        wk = [xa.take([KC, D], F16) for _ in range(2)]
        wv = [xa.take([KC, D], F16) for _ in range(2)]
        wo_off = xa.at
        wo = [xa.take([KC, D], F16) for _ in range(2)]
        attT = [xa.take([KC, T], F16) for _ in range(2)]
        lnT = attT
        stage_off = xa.at
        ctx_stage = [xa.take([KC, PB * LM], F32) for _ in range(2)]
        ctx_hl = [[xa.take([KC, PB * LM], F16) for _ in range(2)] for _ in range(2)]
        wq = ctx_hl[1]
        kT_off = xa.at
        kT = [xa.take([KC, PB, L + 1], F16) for _ in range(2)]
        v_hl = [xa.take([PB * 2, D], F16) for _ in range(2)]
        q_bd = [xa.take([KC, PB, P], F16) for _ in range(2)]
        sm_off = xa.at
        sm = xa.take([PAIRS, L], F32)
        p_off = xa.at
        p_all = xa.take([2, PAIRS, L + 1], F16)
        p_hl = [p_all[:, n] for n in range(2)]
        pt_off = xa.at
        pT = xa.take([PB, 2, 2, KC, P], F16)
        pT_last = xa.take([PAIRS, P], F16, parts=2 * PAIRS)
        vl_all = xa.take([2, STEPS, P], F16, parts=2 * PAIRS)
        vl_cur = xa.take([2, P], F16, parts=2 * PAIRS)
        att_st = [xa.take([KC, PB, S], F16) for _ in range(2)]
        klast = [xa.take([KC, B], F16) for _ in range(2)]
        ctxl_stage = xa.take([KC, B], F32)
        ctxl = [xa.take([KC, B], F16) for _ in range(2)]
        bk_col = xa.take([KC], F32)
        bv_col = xa.take([KC], F32)
        mask_int = view(sm_off, [L], I32)
        q_f = [view(pt_off + n * 2 * KB, [D], F32) for n in range(2)]
        bv_bc = [view(pt_off + 4 * KB + n * KB, [KC, P], F16) for n in range(2)]
        bo_bc = view(pt_off + 6 * KB, [D], F32)
        vlast = [view(sm_off + 2 * KB + n * KB, [D], F16, parts=B) for n in range(2)]
        bias_tile = view(sm_off + 4 * KB, [D], F32)

        W_HALF = 4 * KB
        wt_off = 204 * KB - 7 * W_HALF
        assert wt_off >= xa.at
        spare_at = [wt_off, wt_off + 2 * W_HALF, wt_off + 4 * W_HALF]
        a_at = [wt_off + (1 + 2 * n) * W_HALF for n in range(3)]
        wt_stage = [view(a, [KC, D], F32) for a in a_at]
        wt_a = [view(a, [2, D], F32) for a in a_at]
        wt_b = [view(a + W_HALF, [2, D], F32) for a in a_at]
        wt_sum = [view(a, [2, D], F32) for a in spare_at]
        wt = [[[view(base + n * W_HALF // 2, [2, D], F16) for n in range(2)] for base in (a_at[k], spare_at[k])]
              for k in range(3)]
        xhat0 = view(wt_off, [NT, D], F32)
        wq_stage, wk_stage = ctx_stage
        wv_stage, wo_stage = wt_stage[2], view(p_off, [KC, D], F32)

        xhat1 = view(q_off, [NT, D], F32)
        ln1T = [view(wk_off + n * 8 * KB, [KC, T], F16) for n in range(2)]
        fa = Region(stage_off, 204 * KB)
        dft_off = fa.at
        dft = [fa.take([2, 2, NF], F16) for _ in range(2)]
        idft = fa.take([KC, NF], F32)
        wf_off = fa.at
        wf = [[fa.take([KC, D], F16) for _ in range(2)] for _ in range(3)]
        assert fa.at <= kT_off
        spec_off = fa.at
        spec = [fa.take([KC, T], F32) for _ in range(3)]
        after_spec = fa.at
        prod = view(dft_off, [2, D], F32)
        spec_ri = [z.rearrange("p (a r) t -> p r a t", r=2) for z in spec]

        PW = KC * 512
        PIECE = 8 * KB
        e_stage = [view((172 + 8 * n) * KB, [PW], F32) for n in range(4)]
        assert wo_off + 3 * PIECE <= dft_off and after_spec + PIECE <= 172 * KB
        piece_at = [wo_off, wo_off + PIECE, wo_off + 2 * PIECE, after_spec,
                    wf_off, wf_off + PIECE, wf_off + 2 * PIECE, dft_off]
        w_hl = [[view(at + n * PIECE // 2, [PW], F16) for n in range(2)] for at in piece_at]
        l2_f = xhat1
        l2_hl = [view(wk_off + n * 8 * KB, [NT, D], F16) for n in range(2)]
        ea = Region(spec_off, after_spec)
        l2T = ea.take([NT, 2, KC, P], F16)
        hid_hl = [ea.take([FC, CAP], F16) for _ in range(2)]
        hid_f = [ea.take([2, CAP], F32) for _ in range(4)]
        xs = ea.take([KC, 2, CAP], F16)
        yT = ea.take([KC, CAP], F32)
        y_rows = [ea.take([D], F32), ea.take([D], F32, parts=CB)]
        x2_rows = [ea.take([D], F32), ea.take([D], F32, parts=CB)]

        names = """x_landed0 x_landed1 ident_landed consts_landed wq_landed wk_landed wv_landed wo_landed ctxl_landed bias_landed
        ctx_landed0 ctx_landed1 dft_landed idft_landed wt_landed0 wt_landed1 wt_landed2 ab_landed out_landed
        vlast_stored vl_landed
        ln_var ln_rstd ln_out tr_ps tr_hi tr_free w_hi w_lo bq_done q_ps q_f32 q_hi q_lo ctxl_split last_ps last_hi last_lo
        bias_ps bias_done x_biased proj_ps proj_hi proj_free split_hi split_lo s_ps s_free s_max s_neg exp_done
        sums_sc recip_done p_hi p_lo q_ready vl_ready pt_ps pt_dve pt_act pv_ps pv_hi pv_free att_copied
        wo_ps x1_done fold_ps fold_hi fold_free wt_sums ab_split abias_ps abias_done wt_hi wt_lo spec_ps spec_done
        unbound irfft_ps x2_done chain_dve chain_pool pool_waits
        gate_landed x2_stored wg_split l2_hi l2_lo lt_ps lt_done logits_ps onehot_done rank_ps routed
        e_landed0 e_landed1 e_landed2 e_landed3 e_hi e_lo perm_done xs_ps xs_done h_ps gelu_done h_hi h_lo
        y_ps y_done yt_ps y_out ids_done rows_landed scattered shifted ranks_moved""".split()
        s = {n: sem(n) for n in names}

        def from_zero(count):
            return max(count, 0) if isinstance(count, int) else count

        def hl_passes(a, b):
            return ((a[0], b[0]), (a[0], b[1]), (a[1], b[0]))

        block = ctx.enter_context(nc.Block())

        @block.sync
        def _(sp):
            for half in range(2):
                ts = slice(half * HT, (half + 1) * HT)
                sp.dma_start(x_tok[:, ts], i["x_t"][:, ts]).then_inc(s[f"x_landed{half}"], 16)
            sp.dma_start(ident, i["ident"]).then_inc(s["ident_landed"], 16)
            sp.dma_start(wq_stage, i["wq_t"]).then_inc(s["wq_landed"], 16)
            for src, dst in ((i["ident16"], ident16), (i["bq"], bq_col), (i["bk"], bk_col),
                             (i["bv"], bv_col), (i["diag"], diag[0:2 * PAIRS]),
                             (i["own_head"], own_head)):
                sp.dma_start(dst, src).then_inc(s["consts_landed"], 16)
            for g in range(HC):
                sp.dma_start(mask_int[g * S:(g + 1) * S], i["mask"]).then_inc(s["consts_landed"], 16)
            sp.dma_start(wk_stage, i["wk_t"]).then_inc(s["wk_landed"], 16)
            sp.dma_start(ctxl_stage, i["ctx_last"]).then_inc(s["ctxl_landed"], 16)
            sp.dma_start(wv_stage, i["wv_t"]).then_inc(s["wv_landed"], 16)
            sp.dma_start(bo_bc, i["bo"].partition_broadcast(P)).then_inc(s["bias_landed"], 16)
            sp.dma_start(wo_stage, i["wo_t"]).then_inc(s["wo_landed"], 16)
            sp.wait_ge(s["w_lo"], 1)
            sp.dma_start(ctx_stage[0], i["ctx_t"][0]).then_inc(s["ctx_landed0"], 16)
            sp.wait_ge(s["w_lo"], 2)
            sp.dma_start(ctx_stage[1], i["ctx_t"][1]).then_inc(s["ctx_landed1"], 16)
            sp.wait_ge(s["tr_ps"], NT)
            sp.wait_ge(s["w_lo"], 3)
            for n in range(3):
                sp.dma_start(wt_stage[n], i["awt"][n].rearrange("p k c d -> p (k c) d")).then_inc(s[f"wt_landed{n}"], 16)
            sp.dma_start(ab_stage, i["ab"]).then_inc(s["ab_landed"], 16)
            for src, dst in ((i["slot_iota"], slot_iota), (i["tri16"], tri16), (i["ones16"], ones16),
                             (i["wg"], wg_stage), (i["bg"].partition_broadcast(P), bg_bc),
                             (i["rank_order"], rank_order), (i["tok_ids"], tok_ids), (i["id_offset"], id_offset)):
                sp.dma_start(dst, src).then_inc(s["gate_landed"], 16)
            sp.wait_ge(s["last_lo"], 2)
            for n in range(2):
                sp.dma_start(i["vlast_dram"][n], vlast[n]).then_inc(s["vlast_stored"], 16)
            sp.wait_ge(s["vlast_stored"], 32)
            for rows, dst, n in ((0, 0, 0), (PAIRS, 0, 0), (0, 1, 1), (PAIRS, 1, 1)):
                sp.dma_start(vl_all[rows:rows + PAIRS, dst],
                             i["vlast_dram"][n].rearrange("(t b) (c x) -> (b c) t x", b=PB, c=KC)
                             ).then_inc(s["vl_landed"], 16)
            with sp.Fori(1, STEPS // PB) as k:
                for par in range(2):
                    st = k * 2 + par
                    sp.wait_ge(s["split_lo"], from_zero(st - 1))
                    sp.dma_start(ctx_stage[par], i["ctx_t"][bass.ds(st, 1)].rearrange("a p c t -> p (a c) t")
                                 ).then_inc(s[f"ctx_landed{par}"], 16)
            sp.wait_ge(s["split_lo"], STEPS)
            for n in range(2):
                sp.dma_start(dft[n], i["dft16"][n]).then_inc(s["dft_landed"], 16)
            sp.dma_start(idft, i["idft"]).then_inc(s["idft_landed"], 16)

            def load_piece(e, n, done):
                sp.wait_ge(s["e_lo"], done)
                src = i["w1"] if n < 4 else i["w2"]
                sp.dma_start(e_stage[n % 4], src[bass.ds(e * 4 + n % 4, 1)].rearrange("a p x -> p (a x)")
                             ).then_inc(s[f"e_landed{n % 4}"], 16)

            sp.wait_ge(s["fold_ps"], 3 * KC)
            sp.wait_ge(s["pv_free"], STEPS * PB)
            for n in range(PIECES):
                load_piece(0, n, from_zero(n - 3))
            sp.wait_ge(s["x2_done"], NT)
            sp.dma_start(i["x2_dram"].rearrange("(t p) d -> p t d", p=P), x_tok).then_inc(s["x2_stored"], 16)

            def rest_of_round(r):
                with sp.Fori(1, E) as e:
                    for n in range(PIECES):
                        load_piece(e, n, r * (E * PIECES) + e * PIECES + (n - 3))

            rest_of_round(0)
            sp.wait_ge(s["routed"], 1)
            with sp.If(sp.value_load(more_rounds[0:1, 0:1], min_val=0, max_val=1) > 0):
                with sp.Fori(1, ROUNDS) as r:
                    for n in range(PIECES):
                        load_piece(0, n, r * (E * PIECES) + (n - 3))
                    rest_of_round(r)

        @block.gpsimd
        def _(pool):
            g = nc.gpsimd

            def power(n):
                ts = slice(n % 2 * HT, (n % 2 + 1) * HT)
                pool.wait_ge(s["ln_var"], n + 1)
                g.tensor_tensor(rstd[:, ts], var_eps[:, ts], minus_half[:, ts], ALU.pow).then_inc(s["ln_rstd"], 1)

            g.memset(minus_half, -0.5).then_inc(s["chain_pool"], 1)
            pool.wait_ge(s["chain_pool"], 1)
            power(0)
            power(1)
            for n in range(KC * 2):
                pool.wait_ge(s["q_f32"], n + 1)
                half, c = divmod(n, KC)
                g.tensor_copy(qT[0][:, c, half * D:(half + 1) * D], q_f[n % 2]).then_inc(s["q_hi"], 1)
            pool.wait_ge(s["q_lo"], KC * 2)
            pool.wait_ge(s["last_lo"], 1)

            def weight_sums(k):
                pool.wait_ge(s[f"wt_landed{k}"], 16)
                pool.wait_ge(s["wt_lo"], 2 * k)
                g.tensor_tensor(wt_sum[k], wt_a[k], wt_b[k], ALU.add).then_inc(s["wt_sums"], 1)
                pool.wait_ge(s["wt_sums"], 2 * k + 1)
                g.tensor_tensor(wt_b[k], wt_a[k], wt_b[k], ALU.subtract).then_inc(s["wt_sums"], 1)

            def step(st, cur=True, prev=True):
                if prev:
                    pool.wait_ge(s["vl_landed"], 64)
                    pool.wait_ge(s["pv_ps"], from_zero(st * 2 - 2))
                    pool.sem_inc(s["pool_waits"], 1)
                    g.tensor_copy(vl_cur, vl_all[:, :, bass.ds(st - 1, 1), :].rearrange("p h a x -> p h (a x)")
                                  ).then_inc(s["vl_ready"], 1)
                if cur:
                    pool.wait_ge(s["s_ps"], st * PAIRS)
                    pool.sem_inc(s["pool_waits"], 1)
                    for n in range(2):
                        for b in range(PB):
                            g.tensor_tensor(q_bd[n][:, :, b, :].rearrange("p c (r q) -> p c r q", r=HC),
                                            qT[n][:, :, bass.ds(st * (PB * S) + b * S, S)].unsqueeze(2)
                                            .broadcast_to((P, KC, HC, S)),
                                            own_head.unsqueeze(1).unsqueeze(3).broadcast_to((P, KC, HC, S)), ALU.mult)
                        last = g.tensor_copy(kT[n][:, :, :, LM], klast[n][:, :, bass.ds(st * PB, PB)])
                    last.then_inc(s["q_ready"], 1)
                if prev:
                    pool.wait_ge(s["pv_free"], st * 2)
                    pool.sem_inc(s["pool_waits"], 1)
                    for n in range(2):
                        last = g.tensor_copy(attT[n][:, :, bass.ds(st * (PB * S) - PB * S, PB * S)],
                                             att_st[n].rearrange("p c b q -> p c (b q)"))
                    last.then_inc(s["att_copied"], 1)

            step(0, prev=False)
            pool.wait_ge(s["bias_done"], 1)
            pool.wait_ge(s["ln_out"], NT)
            g.tensor_tensor(x_tok, x_tok, bias_tile.unsqueeze(1).broadcast_to((P, NT, D)), ALU.add
                            ).then_inc(s["x_biased"], 1)
            weight_sums(0)
            step(1)
            weight_sums(1)
            weight_sums(2)
            with pool.Fori(1, STEPS // 2 - 1) as k:
                for par in range(2):
                    step(k * 2 + par)
            step(STEPS - 2)
            step(STEPS - 1)
            step(STEPS, cur=False)
            for n in range(2, 6):
                power(n)
            pool.wait_ge(s["x2_stored"], 16)

            out_rows = out.rearrange("b q d -> (b q) d")

            def scatter(n):
                pool.wait_ge(s["y_out"], n + 1)
                pool.sem_inc(s["pool_waits"], 1)
                for part in range(2):
                    g.indirect_dma_start(out=out_rows, out_offset=bass.IndirectOffsetOnAxis(
                                             ap=ids[part][:, 1:2].bitcast(U32), axis=0),
                                         in_=y_rows[part], in_offset=None, bounds_check=T - 1, oob_is_err=False
                                         ).then_inc(s["scattered"], 16)

            def expert(n, prev=True):
                for k in range(FC // 2):
                    pool.wait_ge(s["gelu_done"], n * 8 + k + 1)
                    pool.sem_inc(s["pool_waits"], 1)
                    g.tensor_scalar(hid_hl[0][:, 2 * k:2 * k + 2, :], hid_f[k % 4], SH, 1.0, ALU.mult, ALU.mult
                                    ).then_inc(s["h_hi"], 1)
                if prev:
                    scatter(n - 1)
                pool.wait_ge(s["shifted"], n + 1)
                pool.sem_inc(s["pool_waits"], 1)
                for part in range(2):
                    g.indirect_dma_start(out=x2_rows[part], out_offset=None, in_=i["x2_dram"],
                                         in_offset=bass.IndirectOffsetOnAxis(ap=ids[part][:, 0:1].bitcast(U32), axis=0)
                                         ).then_inc(s["rows_landed"], 16)

            def round_(r):
                expert(r * E, prev=False)
                with pool.Fori(1, E) as e:
                    expert(r * E + e)
                scatter(r * E + (E - 1))
                pool.wait_ge(s["scattered"], r * (32 * E) + 32 * E)
                pool.sem_inc(s["pool_waits"], 1)

            round_(0)
            pool.wait_ge(s["routed"], 1)
            with pool.If(pool.value_load(more_rounds[0:1, 0:1], min_val=0, max_val=1) > 0):
                with pool.Fori(1, ROUNDS) as r:
                    round_(r)

        @block.scalar
        def _(act):
            a = nc.scalar

            def hi(dst, src, scale):
                return a.activation(dst, src, ACT.Copy, scale=scale)

            def weight_hi(dst, src, landed):
                act.wait_ge(s[landed], 16)
                hi(dst[0], src, SW).then_inc(s["w_hi"], 1)

            def tokens_hi(dst, base, half):
                for t in range(half * HT, (half + 1) * HT):
                    act.wait_ge(s["tr_ps"], base + t + 1)
                    hi(dst[0][:, :, t * P:(t + 1) * P], TR_BANKS[t % 4][:].rearrange("p (c x) -> p c x", c=KC), SX
                       ).then_inc(s["tr_hi"], 1)

            tokens_hi(lnT, 0, 0)
            weight_hi(wq, wq_stage, "wq_landed")
            tokens_hi(lnT, 0, 1)
            weight_hi(wk, wk_stage, "wk_landed")
            act.wait_ge(s["ctxl_landed"], 16)
            hi(ctxl[0], ctxl_stage, SX).then_inc(s["ctxl_split"], 1)
            act.wait_ge(s["bq_done"], 1)
            for n in range(KC * 2):
                act.wait_ge(s["q_ps"], n + 1)
                act.wait_ge(s["q_lo"], from_zero(n - 1))
                c = n % KC
                a.activation(q_f[n % 2], (BC, BD)[n % 2][:], ACT.Identity, bias=bq_scaled[:, c:c + 1],
                             scale=1.0 / SW).then_inc(s["q_f32"], 1)
                if n == 1:
                    weight_hi(wv, wv_stage, "wv_landed")
                if n == 3:
                    weight_hi(wo, wo_stage, "wo_landed")
                if n == 5:
                    act.wait_ge(s["ctx_landed0"], 16)
                    hi(ctx_hl[0][0], ctx_stage[0], SX).then_inc(s["split_hi"], 1)
            act.wait_ge(s["last_ps"], 1)
            hi(klast[0], BE[:, 0:KC * B].rearrange("p (c b) -> p c b", c=KC), SK / (SX * SW)).then_inc(s["last_hi"], 1)
            act.wait_ge(s["last_ps"], 2)
            hi(vlast[0], BF[0:B, :], 1.0 / SW).then_inc(s["last_hi"], 1)

            def mixing_weights_hi(k):
                for n, src in enumerate((wt_sum[k], wt_b[k])):
                    act.wait_ge(s["wt_sums"], 2 * k + 2)
                    if n == 1:
                        act.wait_ge(s["wt_lo"], 2 * k + 1)
                    hi(wt[k][n][0], src, SW).then_inc(s["wt_hi"], 1)

            def fold_hi(n):
                act.wait_ge(s["fold_ps"], n + 1)
                hi(wf[n // KC][0][:, n % KC, :], proj_banks[n % 2][:], SF / (SW * SW)).then_inc(s["fold_hi"], 1)

            def step(st, par, landed, cur=True, prev=True, nxt=True):
                n0 = st * 8

                def k_hi(c):
                    if cur:
                        act.wait_ge(s["proj_ps"], n0 + c + 1)
                        hi(kT[0][:, c, :, 0:LM], proj_banks[c % 2][:].rearrange("p (b x) -> p b x", b=PB),
                           SK / (SX * SW)).then_inc(s["proj_hi"], 1)
                    else:
                        fold_hi(2 * c)
                        fold_hi(2 * c + 1)

                def v_hi(t):
                    if cur:
                        act.wait_ge(s["proj_ps"], n0 + 5 + t)
                        hi(v_hl[0][:, t, :], proj_banks[t % 2][:], 1.0 / SW).then_inc(s["proj_hi"], 1)
                    else:
                        fold_hi(8 + t)

                def exp(m, b):
                    act.wait_ge(s["s_neg"], m * 2 + 1 + b)
                    for j in range(b * KC, b * KC + KC):
                        a.activation(sm[:, j, :], sm[:, j, :], ACT.Exp, bias=neg_max[:, j:j + 1],
                                     scale=ISD / (SX * SK), accum_out=score_sums[:, j:j + 1]
                                     ).then_inc(s["exp_done"], 1)

                def p_hi(m, b):
                    act.wait_ge(s["recip_done"], m * 2 + 1 + b)
                    for j in range(b * KC, b * KC + KC):
                        hi(p_hl[0][:, j, 0:L], sm[:, j, :], recip[:, j:j + 1]).then_inc(s["p_hi"], 1)

                def pt_copy(b):
                    act.wait_ge(s["pt_ps"], st * 5 - 5 + (2, 5)[b])
                    a.activation(pT[:, b, 1].rearrange("p h c x -> p (h c x)"), BF[:].bitcast(F16), ACT.Copy
                                 ).then_inc(s["pt_act"], 1)

                if prev:
                    exp(st - 1, 1)
                k_hi(0)
                if prev:
                    p_hi(st - 1, 1)
                k_hi(1)
                if prev:
                    pt_copy(0)
                if nxt:
                    act.wait_ge(s[f"ctx_landed{1 - par}"], landed)
                    hi(ctx_hl[1 - par][0], ctx_stage[1 - par], SX).then_inc(s["split_hi"], 1)
                k_hi(2)
                if prev:
                    pt_copy(1)
                k_hi(3)
                if prev:
                    act.wait_ge(s["att_copied"], from_zero(st - 1))
                    for b in range(PB):
                        act.wait_ge(s["pv_ps"], st * 2 - 1 + b)
                        for r in range(HC):
                            rows = slice(r * DK, (r + 1) * DK)
                            last = hi(att_st[0][rows, :, b, :],
                                      (BG, BH)[b][rows, :].rearrange("p (c x) -> p c x", c=KC)[:, :, r * S:(r + 1) * S],
                                      1.0 / SP_)
                        last.then_inc(s["pv_hi"], 1)
                v_hi(0)
                v_hi(1)
                if cur:
                    exp(st, 0)
                v_hi(2)
                if cur:
                    p_hi(st, 0)
                v_hi(3)

            step(0, 0, 16, prev=False)
            mixing_weights_hi(0)
            step(1, 1, 32)
            mixing_weights_hi(1)
            mixing_weights_hi(2)
            act.wait_ge(s["ab_split"], 1)
            hi(ab[0], ab_sd, SW).then_inc(s["ab_split"], 1)
            with act.Fori(1, STEPS // 2 - 1) as k:
                step(k * 2, 0, k * 16 + 16)
                step(k * 2 + 1, 1, k * 16 + 32)
            step(STEPS - 2, 0, STEPS // 2 * 16)
            step(STEPS - 1, 1, 0, nxt=False)
            step(STEPS, 0, 0, cur=False, nxt=False)

            act.wait_ge(s["abias_ps"], 1)
            hi(dft_bias, BG[:, 0:KC * 4].rearrange("p (c m) -> p c m", c=KC), 1.0 / (SW * SW)).then_inc(s["abias_done"], 1)

            def piece_hi(n, k):
                act.wait_ge(s[f"e_landed{k % 4}"], n * 32 + (16 * (k // 4) + 16))
                hi(w_hl[k][0], e_stage[k % 4], SG if k < 4 else S2).then_inc(s["e_hi"], 1)

            tokens_hi(ln1T, NT, 0)
            act.wait_ge(s["abias_done"], 1)
            for n, (m, c, half) in enumerate(SPEC_ORDER):
                if n == 4:
                    tokens_hi(ln1T, NT, 1)
                act.wait_ge(s["spec_ps"], n + 1)
                a.activation(spec[m][:, c, half * D:(half + 1) * D], (BC, BD)[n % 2][:], ACT.Identity,
                             bias=dft_bias[:, c, m:m + 1], scale=1.0 / (SX * SF)).then_inc(s["spec_done"], 1)
                if n in EARLY_PIECES:
                    piece_hi(0, EARLY_PIECES.index(n))

            def gate_transpose_out(t):
                act.wait_ge(s["lt_ps"], t + 1)
                a.activation(l2T[:, t].rearrange("p h c x -> p (h c x)"), (BG, BH)[t % 2][:].bitcast(F16), ACT.Copy
                             ).then_inc(s["lt_done"], 1)

            act.wait_ge(s["gate_landed"], 16 * 8)
            hi(wg_hl[0], wg_stage, SG).then_inc(s["wg_split"], 1)
            act.wait_ge(s["unbound"], 2)
            for half in range(2):
                for t in range(half * HT, (half + 1) * HT):
                    act.wait_ge(s["ln_out"], 2 * NT + t + 1)
                    hi(l2_hl[0][:, t, :], l2_f[:, t, :], SX).then_inc(s["l2_hi"], 1)
                    if t > half * HT:
                        gate_transpose_out(t - 1)
                gate_transpose_out(half * HT + HT - 1)
            for k in range(4, PIECES - 1):
                piece_hi(0, k)

            def expert(n, nxt=True):
                for k in range(FC // 2):
                    act.wait_ge(s["h_ps"], n * 8 + k + 1)
                    act.wait_ge(s["h_lo"], from_zero(n * 8 + k - 3))
                    a.activation(hid_f[k % 4], proj_banks[k % 2][:, 0:2 * CAP].rearrange("p (c x) -> p c x", c=2),
                                 ACT.Gelu_apprx_tanh, scale=1.0 / (SX * SG)).then_inc(s["gelu_done"], 1)
                    if k == 1:
                        piece_hi(n, PIECES - 1)
                    elif nxt and k % 2:
                        piece_hi(n + 1, k // 2 - 1)
                if nxt:
                    piece_hi(n + 1, 3)
                for c in range(KC):
                    act.wait_ge(s["y_ps"], n * 4 + c + 1)
                    hi(yT[:, c, :], (BC, BD)[c % 2][:, 0:CAP], 1.0 / (S2 * SH)).then_inc(s["y_done"], 1)
                    if nxt and c < KC - 1:
                        piece_hi(n + 1, 4 + c)

            def experts(r):
                expert(r * E)
                with act.Fori(1, E - 1) as e:
                    expert(r * E + e)
                expert(r * E + (E - 1), nxt=False)

            experts(0)
            act.wait_ge(s["routed"], 1)
            with act.If(act.value_load(more_rounds[0:1, 0:1], min_val=0, max_val=1) > 0):
                with act.Fori(1, ROUNDS) as r:
                    for k in range(PIECES - 1):
                        piece_hi(r * E, k)
                    experts(r)

        @block.vector
        def _(dve):
            v = nc.vector
            chain = count(1)

            def lo(dst, src, scale, h):
                return v.scalar_tensor_tensor(dst, src, scale, h, ALU.mult, ALU.subtract)

            def variances(half):
                ts = range(half * HT, (half + 1) * HT)
                for t in ts:
                    last = v.bn_aggr(mean_var[:, t, :], stats[:, t, :])
                last.then_inc(s["chain_dve"], 1)
                dve.wait_ge(s["chain_dve"], next(chain))
                v.tensor_scalar(var_eps[:, half * HT:(half + 1) * HT], mean_var[:, half * HT:(half + 1) * HT, 1], EPS, None,
                                ALU.add).then_inc(s["ln_var"], 1)

            def normalise(n, half, dst):
                dve.wait_ge(s["ln_rstd"], 2 * n + half + 1)
                for t in range(half * HT, (half + 1) * HT):
                    v.tensor_scalar(dst[:, t, :], x_tok[:, t, :], mean_var[:, t, 0:1], rstd[:, t:t + 1],
                                    ALU.subtract, ALU.mult).then_inc(s["ln_out"], 1)

            def tokens_lo(dst, base, half):
                for t in range(half * HT, (half + 1) * HT):
                    dve.wait_ge(s["tr_hi"], base + t + 1)
                    lo(dst[1][:, :, t * P:(t + 1) * P], TR_BANKS[t % 4][:].rearrange("p (c x) -> p c x", c=KC), SX,
                       dst[0][:, :, t * P:(t + 1) * P]).then_inc(s["tr_free"], 1)

            def weight_lo(n, w, src):
                dve.wait_ge(s["w_hi"], n + 1)
                lo(w[1], src, SW, w[0]).then_inc(s["w_lo"], 1)

            for half in range(2):
                dve.wait_ge(s[f"x_landed{half}"], 16)
                for t in range(half * HT, (half + 1) * HT):
                    last = v.bn_stats(stats[:, t, :], x_tok[:, t, :])
                last.then_inc(s["chain_dve"], 1)
                dve.wait_ge(s["chain_dve"], next(chain))
                variances(half)
                normalise(0, half, xhat0)
            tokens_lo(lnT, 0, 0)
            weight_lo(0, wq, wq_stage)
            dve.wait_ge(s["consts_landed"], 16 * (6 + HC))
            v.tensor_scalar(bq_scaled, bq_col, SX, None, ALU.mult).then_inc(s["bq_done"], 1)
            tokens_lo(lnT, 0, 1)
            weight_lo(1, wk, wk_stage)
            v.tensor_scalar(mask_bias, mask_int, 0.0, NEG, ALU.is_equal, ALU.mult)
            k_bias = [kT[n][:, :, :, L] for n in range(2)]
            bk_all = bk_col.unsqueeze(2).broadcast_to((P, KC, PB))
            v.tensor_scalar(k_bias[0], bk_all, SK, None, ALU.mult).then_inc(s["chain_dve"], 1)
            dve.wait_ge(s["chain_dve"], next(chain))
            lo(k_bias[1], bk_all, SK, k_bias[0])
            bv_all = bv_col.unsqueeze(2).broadcast_to((P, KC, P))
            v.tensor_scalar(bv_bc[0], bv_all, SW, None, ALU.mult).then_inc(s["chain_dve"], 1)
            dve.wait_ge(s["chain_dve"], next(chain))
            lo(bv_bc[1], bv_all, SW, bv_bc[0])
            dve.wait_ge(s["ctxl_split"], 1)
            lo(ctxl[1], ctxl_stage, SX, ctxl[0]).then_inc(s["ctxl_split"], 1)
            for n in range(KC * 2):
                half, c = divmod(n, KC)
                cols = slice(half * D, (half + 1) * D)
                dve.wait_ge(s["q_hi"], n + 1)
                v.tensor_tensor(qT[1][:, c, cols], q_f[n % 2], qT[0][:, c, cols], ALU.subtract).then_inc(s["q_lo"], 1)
                if n == 1:
                    weight_lo(2, wv, wv_stage)
                if n == 3:
                    weight_lo(3, wo, wo_stage)
                if n == 5:
                    dve.wait_ge(s["split_hi"], 1)
                    lo(ctx_hl[0][1], ctx_stage[0], SX, ctx_hl[0][0]).then_inc(s["split_lo"], 1)
            dve.wait_ge(s["last_hi"], 1)
            lo(klast[1], BE[:, 0:KC * B].rearrange("p (c b) -> p c b", c=KC), SK / (SX * SW), klast[0]
               ).then_inc(s["last_lo"], 1)
            dve.wait_ge(s["last_hi"], 2)
            lo(vlast[1], BF[0:B, :], 1.0 / SW, vlast[0]).then_inc(s["last_lo"], 1)
            dve.wait_ge(s["bias_landed"], 16)
            dve.wait_ge(s["bias_ps"], 1)
            v.scalar_tensor_tensor(bias_tile, BG[:], 1.0 / (SW * SW), bo_bc, ALU.mult, ALU.add
                                   ).then_inc(s["bias_done"], 1)

            def mixing_weights_lo(k):
                for n, src in enumerate((wt_sum[k], wt_b[k])):
                    dve.wait_ge(s["wt_hi"], 2 * k + n + 1)
                    lo(wt[k][n][1], src, SW, wt[k][n][0]).then_inc(s["wt_lo"], 1)

            def fold_lo(n):
                dve.wait_ge(s["fold_hi"], n + 1)
                lo(wf[n // KC][1][:, n % KC, :], proj_banks[n % 2][:], SF / (SW * SW), wf[n // KC][0][:, n % KC, :]
                   ).then_inc(s["fold_free"], 1)

            def step(st, par, cur=True, prev=True, nxt=True):
                n0 = st * 8

                def k_lo(c):
                    if cur:
                        dve.wait_ge(s["proj_hi"], n0 + c + 1)
                        lo(kT[1][:, c, :, 0:LM], proj_banks[c % 2][:].rearrange("p (b x) -> p b x", b=PB),
                           SK / (SX * SW), kT[0][:, c, :, 0:LM]).then_inc(s["proj_free"], 1)
                    else:
                        fold_lo(2 * c)
                        fold_lo(2 * c + 1)

                def v_lo(t):
                    if cur:
                        dve.wait_ge(s["proj_hi"], n0 + 5 + t)
                        lo(v_hl[1][:, t, :], proj_banks[t % 2][:], 1.0 / SW, v_hl[0][:, t, :]
                           ).then_inc(s["proj_free"], 1)
                    else:
                        fold_lo(8 + t)

                def scores(j):
                    bank = (BC, BD)[j % 2]
                    dve.wait_ge(s["s_ps"], n0 + j + 1)
                    v.scalar_tensor_tensor(sm[:, j, :], bank[:, 0:L], bank[:, L:L + 1], mask_bias,
                                           ALU.add, ALU.add).then_inc(s["s_free"], 1)

                def maxima(b):
                    js = slice(b * KC, b * KC + KC)
                    dve.wait_ge(s["s_free"], n0 + 4 + 4 * b)
                    v.reduce_max(row_max[:, js], sm[:, js, :], AX_X).then_inc(s["s_max"], 1)
                    dve.wait_ge(s["s_max"], st * 2 + 1 + b)
                    v.tensor_scalar(neg_max[:, js], row_max[:, js], -ISD / (SX * SK), None, ALU.mult
                                    ).then_inc(s["s_neg"], 1)

                def reciprocals(m, b):
                    js = slice(b * KC, b * KC + KC)
                    dve.wait_ge(s["exp_done"], m * 8 + 4 + 4 * b)
                    v.tensor_scalar(sums_scaled[:, js], score_sums[:, js], 1.0 / SP_, None, ALU.mult
                                    ).then_inc(s["sums_sc"], 1)
                    dve.wait_ge(s["sums_sc"], m * 2 + 1 + b)
                    v.reciprocal(recip[:, js], sums_scaled[:, js]).then_inc(s["recip_done"], 1)

                def p_lo(m, b):
                    for j in range(b * KC, b * KC + KC):
                        dve.wait_ge(s["p_hi"], m * 8 + 1 + j)
                        v.scalar_tensor_tensor(p_hl[1][:, j, 0:L], sm[:, j, :], recip[:, j:j + 1],
                                               p_hl[0][:, j, 0:L], ALU.mult, ALU.subtract
                                               ).then_inc(s["p_lo"], 1)

                def pt_copy(b):
                    dve.wait_ge(s["pt_ps"], st * 5 - 5 + (1, 4)[b])
                    v.tensor_copy(pT[:, b, 0].rearrange("p h c x -> p (h c x)"), BE[:].bitcast(F16)
                                  ).then_inc(s["pt_dve"], 1)

                if prev:
                    reciprocals(st - 1, 1)
                k_lo(0)
                if prev:
                    p_lo(st - 1, 1)
                k_lo(1)
                if prev:
                    pt_copy(0)
                k_lo(2)
                if prev:
                    dve.wait_ge(s["pt_ps"], st * 5 - 2)
                    v.tensor_tensor(pT_last,
                                    BH[0:2 * PAIRS, 0:P // 2].bitcast(F16).unsqueeze(1).broadcast_to((2 * PAIRS, PAIRS, P)),
                                    diag[0:2 * PAIRS].unsqueeze(2).broadcast_to((2 * PAIRS, PAIRS, P)),
                                    ALU.mult).then_inc(s["pt_dve"], 1)
                    pt_copy(1)
                if nxt:
                    dve.wait_ge(s["split_hi"], st + 2)
                    lo(ctx_hl[1 - par][1], ctx_stage[1 - par], SX, ctx_hl[1 - par][0]).then_inc(s["split_lo"], 1)
                k_lo(3)
                if prev:
                    for b in range(PB):
                        dve.wait_ge(s["pv_hi"], st * 2 - 1 + b)
                        for r in range(HC):
                            rows = slice(r * DK, (r + 1) * DK)
                            last = lo(att_st[1][rows, :, b, :],
                                      (BG, BH)[b][rows, :].rearrange("p (c x) -> p c x", c=KC)[:, :, r * S:(r + 1) * S],
                                      1.0 / SP_, att_st[0][rows, :, b, :])
                        last.then_inc(s["pv_free"], 1)
                v_lo(0)
                if cur:
                    if not prev:
                        dve.wait_ge(s["x_biased"], 1)
                        dve.wait_ge(s["vlast_stored"], 32)
                    scores(0)
                    scores(1)
                v_lo(1)
                if cur:
                    scores(2)
                    scores(3)
                    maxima(0)
                    scores(4)
                    scores(5)
                    reciprocals(st, 0)
                v_lo(2)
                if cur:
                    scores(6)
                    scores(7)
                    maxima(1)
                v_lo(3)
                if cur:
                    p_lo(st, 0)

            step(0, 0, prev=False)
            mixing_weights_lo(0)
            dve.wait_ge(s["ab_landed"], 16)
            v.tensor_tensor(ab_sd[:, 0], ab_stage[:, 0], ab_stage[:, 1], ALU.add)
            v.tensor_tensor(ab_sd[:, 1], ab_stage[:, 0], ab_stage[:, 1], ALU.subtract).then_inc(s["ab_split"], 1)
            step(1, 1)
            mixing_weights_lo(1)
            mixing_weights_lo(2)
            dve.wait_ge(s["ab_split"], 2)
            lo(ab[1], ab_sd, SW, ab[0]).then_inc(s["ab_split"], 1)
            with dve.Fori(1, STEPS // 2 - 1) as k:
                step(k * 2, 0)
                step(k * 2 + 1, 1)
            step(STEPS - 2, 0)
            step(STEPS - 1, 1, nxt=False)
            step(STEPS, 0, cur=False, nxt=False)

            def x1(t):
                dve.wait_ge(s["wo_ps"], t + 1)
                v.scalar_tensor_tensor(x_tok[:, t, :], (BA, BB, BC, BD)[t % 4][:], 1.0 / (SX * SW), x_tok[:, t, :],
                                       ALU.mult, ALU.add).then_inc(s["x1_done"], 1)

            for half in range(2):
                for t in range(half * HT, (half + 1) * HT):
                    x1(t)
                    dve.wait_ge(s["x1_done"], t + 1)
                    last = v.bn_stats(stats[:, t, :], x_tok[:, t, :])
                last.then_inc(s["chain_dve"], 1)
                dve.wait_ge(s["chain_dve"], next(chain))
                variances(half)
                normalise(1, half, xhat1)
            tokens_lo(ln1T, NT, 0)
            tokens_lo(ln1T, NT, 1)

            def piece_lo(n, k):
                dve.wait_ge(s["e_hi"], n * 8 + k + 1)
                lo(w_hl[k][1], e_stage[k % 4], SG if k < 4 else S2, w_hl[k][0]).then_inc(s["e_lo"], 1)

            def bind(half):
                bs = slice(half * (B // 2), (half + 1) * (B // 2))
                kre, kim, vre, vim = (spec_ri[m][:, r, :, half * D:(half + 1) * D] for m in (1, 2) for r in (0, 1))
                dve.wait_ge(s["spec_done"], 2 * KC * (half + 1))
                for n, (p_, q_) in enumerate(((kre, vre), (kim, vim), (kre, vim), (kim, vre))):
                    v.tensor_tensor(prod, p_, q_, ALU.mult).then_inc(s["chain_dve"], 1)
                    dve.wait_ge(s["chain_dve"], next(chain))
                    v.reduce_sum(bind_sums[:, n, :, bs], prod.rearrange("p c (b q) -> p c b q", q=S), AX_X
                                 ).then_inc(s["chain_dve"], 1)
                    dve.wait_ge(s["chain_dve"], next(chain))

            piece_lo(0, 0)
            piece_lo(0, 1)
            bind(0)
            piece_lo(0, 2)
            piece_lo(0, 3)
            bind(1)
            rr, ii, ri, ir = (bind_sums[:, n] for n in range(4))
            a1, a2, b2 = (lhs_bind[:, n] for n in range(3))
            v.tensor_tensor(a1, rr, ii, ALU.subtract)
            v.tensor_tensor(a2, ri, ir, ALU.add)
            v.tensor_tensor(b2, ii, rr, ALU.subtract).then_inc(s["chain_dve"], 1)
            dve.wait_ge(s["chain_dve"], next(chain))
            v.tensor_copy(a1[0:1, 0, :], rr[0:1, 0, :])
            v.tensor_copy(b2[0:1, 0, :], ii[0:1, 0, :])
            v.memset(a2[0:1, 0, :], 0.0).then_inc(s["chain_dve"], 1)
            dve.wait_ge(s["chain_dve"], next(chain))

            def over_tokens(z):
                return z.unsqueeze(3).broadcast_to((P, 2, B // 2, S))

            for half in range(2):
                dve.wait_ge(s["spec_done"], 2 * KC * 2 + KC * (half + 1))
                bs = slice(half * (B // 2), (half + 1) * (B // 2))
                cols = slice(half * D, (half + 1) * D)
                four = "p c (b q) -> p c b q"
                qre, qim = (spec_ri[0][:, r, :, cols].rearrange(four, q=S) for r in range(2))
                pre, pim = (spec_ri[1][:, r, :, cols].rearrange(four, q=S) for r in range(2))
                tmp = prod.rearrange(four, q=S)
                for dst, (c0, c1) in ((pre, (a1, a2)), (pim, (a2, b2))):
                    v.tensor_tensor(dst, qre, over_tokens(c0[:, :, bs]), ALU.mult)
                    v.tensor_tensor(tmp, qim, over_tokens(c1[:, :, bs]), ALU.mult).then_inc(s["chain_dve"], 1)
                    dve.wait_ge(s["chain_dve"], next(chain))
                    last = v.tensor_tensor(dst, dst, tmp, ALU.add).then_inc(s["unbound"], 1)
                    dve.wait_ge(s["unbound"], 2 * half + (1 if dst is pre else 2))

            def x2(t):
                bank = (BA, BB, BE, BF)[t % 4]
                even, odd = bank[:, 0:NF], bank[:, NF:D]
                both = x_tok[:, t, :].rearrange("p (h n) -> p h n", h=2)
                dve.wait_ge(s["irfft_ps"], t + 1)
                v.tensor_tensor(both, both, even.unsqueeze(1).broadcast_to((P, 2, NF)), ALU.add
                                ).then_inc(s["chain_dve"], 1)
                dve.wait_ge(s["chain_dve"], next(chain))
                v.tensor_tensor(both[:, 0], both[:, 0], odd, ALU.add)
                v.tensor_tensor(both[:, 1], both[:, 1], odd, ALU.subtract).then_inc(s["x2_done"], 1)

            dve.wait_ge(s["wg_split"], 1)
            lo(wg_hl[1], wg_stage, SG, wg_hl[0]).then_inc(s["wg_split"], 1)
            for half in range(2):
                ts = range(half * HT, (half + 1) * HT)
                for t in ts:
                    x2(t)
                    dve.wait_ge(s["x2_done"], t + 1)
                    last = v.bn_stats(stats[:, t, :], x_tok[:, t, :])
                last.then_inc(s["chain_dve"], 1)
                dve.wait_ge(s["chain_dve"], next(chain))
                variances(half)
                normalise(2, half, l2_f)
                for t in ts:
                    dve.wait_ge(s["l2_hi"], t + 1)
                    lo(l2_hl[1][:, t, :], l2_f[:, t, :], SX, l2_hl[0][:, t, :]).then_inc(s["l2_lo"], 1)

            def by_tile(z):
                return z.unsqueeze(1).broadcast_to((P, NT, E))

            def by_expert(z):
                return z.unsqueeze(2).broadcast_to((P, NT, E))

            dve.wait_ge(s["logits_ps"], 1)
            v.scalar_tensor_tensor(
                logits, BC[:, 0:NT * E].rearrange("p (t e) -> p t e", e=E), 1.0 / (SX * SG), by_tile(bg_bc),
                ALU.mult, ALU.add).then_inc(s["chain_dve"], 1)
            dve.wait_ge(s["chain_dve"], next(chain))
            v.reduce_max(top, logits, AX_X).then_inc(s["chain_dve"], 1)
            dve.wait_ge(s["chain_dve"], next(chain))
            v.tensor_tensor(is_max, logits, by_expert(top), ALU.is_equal).then_inc(s["chain_dve"], 1)
            dve.wait_ge(s["chain_dve"], next(chain))
            v.tensor_tensor(score, is_max, by_tile(rank_order), ALU.mult).then_inc(s["chain_dve"], 1)
            dve.wait_ge(s["chain_dve"], next(chain))
            v.reduce_max(top2, score, AX_X).then_inc(s["chain_dve"], 1)
            dve.wait_ge(s["chain_dve"], next(chain))
            v.tensor_tensor(onehot, score, by_expert(top2), ALU.is_equal).then_inc(s["chain_dve"], 1)
            dve.wait_ge(s["chain_dve"], next(chain))
            v.tensor_copy(onehot16, onehot).then_inc(s["onehot_done"], 1)
            dve.wait_ge(s["rank_ps"], 1)
            v.scalar_tensor_tensor(
                slot_of, BD[:, 0:NT * E].rearrange("p (t e) -> p t e", e=E), 1.0, onehot, ALU.add, ALU.mult).then_inc(s["chain_dve"], 1)
            dve.wait_ge(s["chain_dve"], next(chain))
            v.tensor_scalar(slot_of, slot_of, -1.0, None, ALU.add).then_inc(s["chain_dve"], 1)
            dve.wait_ge(s["chain_dve"], next(chain))
            v.reduce_max(most, BE[:, 0:E], AX_X).then_inc(s["chain_dve"], 1)
            dve.wait_ge(s["chain_dve"], next(chain))
            v.tensor_scalar(more_rounds, most, float(CAP), None, ALU.is_gt).then_inc(s["routed"], 1)

            def slots(n, e):
                dve.wait_ge(s["xs_ps"], n * 4)
                v.tensor_tensor(perm, slot_iota.unsqueeze(1).broadcast_to((P, NT, CAP)),
                                slot_of[:, :, bass.ds(e, 1)].broadcast_to((P, NT, CAP)), ALU.is_equal
                                ).then_inc(s["perm_done"], 1)

            def gathered(n, c):
                dve.wait_ge(s["xs_ps"], n * 4 + c + 1)
                v.tensor_copy(xs[:, c].rearrange("p h x -> p (h x)"), (BG, BH)[c % 2][:, 0:2 * CAP]
                              ).then_inc(s["xs_done"], 1)

            def take_ids(n):
                v.tensor_tensor(ids_next[0], BH[:, 2 * CAP:2 * CAP + 2], id_offset, ALU.add)
                v.tensor_tensor(ids_next[1], BH[0:CB, 2 * CAP + 2:2 * CAP + 4], id_offset[0:CB], ALU.add
                                ).then_inc(s["ids_done"], 1)

            def rows_out(n):
                dve.wait_ge(s["yt_ps"], n + 1)
                dve.wait_ge(s["rows_landed"], n * 32 + 32)
                v.tensor_tensor(y_rows[0], BE[:], x2_rows[0], ALU.add)
                v.tensor_tensor(y_rows[1], BF[0:CB, :], x2_rows[1], ALU.add).then_inc(s["y_out"], 1)

            def expert(n, e, prev=True, nxt=True, after=True):
                for k in range(FC // 2):
                    dve.wait_ge(s["h_hi"], n * 8 + k + 1)
                    v.scalar_tensor_tensor(hid_hl[1][:, 2 * k:2 * k + 2, :], hid_f[k % 4], SH,
                                           hid_hl[0][:, 2 * k:2 * k + 2, :], ALU.mult, ALU.subtract
                                           ).then_inc(s["h_lo"], 1)
                    if k == 1:
                        piece_lo(n, PIECES - 1)
                    elif nxt and k % 2:
                        piece_lo(n + 1, k // 2 - 1)
                if prev:
                    rows_out(n - 1)
                if nxt:
                    gathered(n + 1, 0)
                    gathered(n + 1, 1)
                    piece_lo(n + 1, 3)
                    gathered(n + 1, 2)
                    piece_lo(n + 1, 4)
                    gathered(n + 1, 3)
                    piece_lo(n + 1, 5)
                if after:
                    slots(n + 2, e + 2)
                dve.wait_ge(s["ids_done"], n + 1)
                dve.wait_ge(s["scattered"], n * 32)
                v.tensor_copy(ids[0], ids_next[0])
                v.tensor_copy(ids[1], ids_next[1]).then_inc(s["shifted"], 1)
                if nxt:
                    dve.wait_ge(s["shifted"], n + 1)
                    take_ids(n + 1)
                    piece_lo(n + 1, 6)

            def round_(r, first):
                slots(r * E, 0)
                for k in range(4 if first else 0, PIECES - 1):
                    if not first:
                        piece_lo(r * E, k)
                for c in range(KC):
                    gathered(r * E, c)
                take_ids(r * E)
                slots(r * E + 1, 1)
                if first:
                    for k in range(4, PIECES - 1):
                        piece_lo(0, k)
                expert(r * E, 0, prev=False)
                with dve.Fori(1, E - 2) as e:
                    expert(r * E + e, e)
                expert(r * E + (E - 2), E - 2, after=False)
                expert(r * E + (E - 1), E - 1, nxt=False, after=False)
                rows_out(r * E + (E - 1))

            round_(0, True)
            dve.wait_ge(s["routed"], 1)
            with dve.If(dve.value_load(more_rounds[0:1, 0:1], min_val=0, max_val=1) > 0):
                with dve.Fori(1, ROUNDS) as r:
                    v.tensor_scalar(slot_of, slot_of, -float(CAP), None, ALU.add).then_inc(s["ranks_moved"], 1)
                    dve.wait_ge(s["ranks_moved"], r)
                    round_(r, False)

        @block.tensor
        def _(pe):
            m = nc.tensor

            def product(out_ap, pairs):
                pairs = list(pairs)
                for n, (w, x) in enumerate(pairs):
                    last = m.matmul(out_ap, w, x, start=(n == 0), stop=(n == len(pairs) - 1))
                return last

            def split_product(out_ap, w, x, wi, xi):
                return product(out_ap, [(u[wi(c)], z[xi(c)]) for c in range(KC) for u, z in hl_passes(w, x)])

            def transpose_tokens(base, src, half):
                for t in range(half * HT, (half + 1) * HT):
                    pe.wait_ge(s["ln_out"], base + t + 1)
                    pe.wait_ge(s["tr_free"], from_zero(base + t - 3))
                    for c in range(KC):
                        last = m.transpose(TR_BANKS[t % 4][:, c * P:(c + 1) * P], src[:, t, c * P:(c + 1) * P], ident)
                    last.then_inc(s["tr_ps"], 1)

            def queries(half):
                for c in range(KC):
                    n = half * KC + c
                    pe.wait_ge(s["q_f32"], from_zero(n - 1))
                    split_product((BC, BD)[n % 2][:], wq, lnT,
                                  lambda k: (slice(None), k, slice(c * P, (c + 1) * P)),
                                  lambda k: (slice(None), k, slice(half * D, (half + 1) * D))).then_inc(s["q_ps"], 1)

            pe.wait_ge(s["ident_landed"], 16)
            transpose_tokens(0, xhat0, 0)
            transpose_tokens(0, xhat0, 1)
            pe.wait_ge(s["tr_free"], HT)
            pe.wait_ge(s["w_lo"], 1)
            queries(0)
            pe.wait_ge(s["tr_free"], NT)
            queries(1)
            pe.wait_ge(s["w_lo"], 3)
            pe.wait_ge(s["ctxl_split"], 2)
            for c in range(KC):
                last = split_product(BE[:, c * B:(c + 1) * B], wk, ctxl,
                                     lambda k: (slice(None), k, slice(c * P, (c + 1) * P)),
                                     lambda k: (slice(None), k, slice(None)))
            last.then_inc(s["last_ps"], 1)
            split_product(BF[0:B, :], ctxl, wv, lambda k: (slice(None), k, slice(None)),
                          lambda k: (slice(None), k, slice(None))).then_inc(s["last_ps"], 1)
            pe.wait_ge(s["w_lo"], 4)
            split_product(BG[:], bv_bc, wo, lambda k: (slice(None), k, slice(None)),
                          lambda k: (slice(None), k, slice(None))).then_inc(s["bias_ps"], 1)

            def fold(n):
                mm, c = divmod(n, KC)
                pe.wait_ge(s["fold_free"], from_zero(n - 1))
                for parity in range(2):
                    last = product(proj_banks[n % 2][:, parity * NF:(parity + 1) * NF],
                                   [(u[:, k, c * P:(c + 1) * P], z[:, parity, k, :]) for k in range(2)
                                    for u, z in hl_passes(wt[mm][parity], dft)])
                last.then_inc(s["fold_ps"], 1)

            def step(st, par, cur=True, prev=True):
                n0 = st * 8

                def k_proj(c):
                    if cur:
                        pe.wait_ge(s["proj_free"], from_zero(n0 + c - 1))
                        split_product(proj_banks[c % 2][:], wk, ctx_hl[par],
                                      lambda k: (slice(None), k, slice(c * P, (c + 1) * P)),
                                      lambda k: (slice(None), k, slice(None))).then_inc(s["proj_ps"], 1)
                    else:
                        fold(2 * c)
                        fold(2 * c + 1)

                def v_proj(t):
                    if cur:
                        pe.wait_ge(s["proj_free"], n0 + 3 + t)
                        split_product(proj_banks[t % 2][:], ctx_hl[par], wv,
                                      lambda k: (slice(None), k, slice(t * P, (t + 1) * P)),
                                      lambda k: (slice(None), k, slice(None))).then_inc(s["proj_ps"], 1)
                    else:
                        fold(8 + t)

                def p_transposes(b):
                    for kt in range(2):
                        bank = (BE, BF)[kt][:].bitcast(F16)
                        for n in range(2):
                            for c in range(KC):
                                slot = n * KC + c
                                last = m.transpose(bank[:, slot * P:(slot + 1) * P],
                                                   p_hl[n][:, b * KC + c, kt * P:(kt + 1) * P], ident16)
                        last.then_inc(s["pt_ps"], 1)

                def attention(b):
                    for c in range(KC):
                        cols = slice(c * P, (c + 1) * P)
                        j = b * KC + c
                        pairs = [(v_hl[u][:, b * 2 + kt, cols], pT[:, b, kt, z, c, :])
                                 for kt in range(2) for u, z in ((0, 0), (0, 1), (1, 0))]
                        pairs += [(vl_cur[:, 0, :], pT_last[:, j, :]),
                                  (vl_cur[0:PAIRS, 1, :], pT_last[0:PAIRS, j, :])]
                        last = product((BG, BH)[b][:, cols], pairs)
                    last.then_inc(s["pv_ps"], 1)

                def scores(j):
                    b, c = divmod(j, KC)
                    pe.wait_ge(s["s_free"], from_zero(n0 + j - 1))
                    product((BC, BD)[j % 2][:, 0:L + 1],
                            [(u[:, c, b, :], z[:, c, b, :]) for u, z in hl_passes(q_bd, kT)]
                            ).then_inc(s["s_ps"], 1)

                if cur:
                    pe.wait_ge(s["split_lo"], st + 1)
                k_proj(0)
                k_proj(1)
                if prev:
                    pe.wait_ge(s["p_lo"], st * 8 - 4)
                    p_transposes(0)
                k_proj(2)
                if prev:
                    pe.wait_ge(s["p_lo"], st * 8)
                    pe.wait_ge(s["pv_free"], from_zero(st * 2 - 2))
                    m.transpose(BH[0:2 * PAIRS, 0:P // 2].bitcast(F16),
                                p_all[:, :, :, LM].rearrange("p h j -> p (h j)"), ident16).then_inc(s["pt_ps"], 1)
                    pe.wait_ge(s["pt_dve"], st * 3 - 2)
                    pe.wait_ge(s["pt_act"], st * 2 - 1)
                    p_transposes(1)
                k_proj(3)
                if prev:
                    pe.wait_ge(s["vl_ready"], st)
                    for b in range(PB):
                        pe.wait_ge(s["pt_dve"], st * 3 - 1 + b)
                        pe.wait_ge(s["pt_act"], st * 2 - 1 + b)
                        attention(b)
                v_proj(0)
                if cur:
                    pe.wait_ge(s["q_ready"], st + 1)
                    pe.wait_ge(s["proj_free"], n0 + 4)
                    scores(0)
                    scores(1)
                v_proj(1)
                if cur:
                    scores(2)
                    scores(3)
                v_proj(2)
                if cur:
                    scores(4)
                    scores(5)
                v_proj(3)
                if cur:
                    scores(6)
                    scores(7)

            step(0, 0, prev=False)
            step(1, 1)
            with pe.Fori(1, STEPS // 2 - 1) as k:
                step(k * 2, 0)
                step(k * 2 + 1, 1)
            step(STEPS - 2, 0)
            step(STEPS - 1, 1)
            pe.wait_ge(s["wt_lo"], 6)
            pe.wait_ge(s["dft_landed"], 32)
            pe.wait_ge(s["proj_free"], STEPS * 8)
            step(STEPS, 0, cur=False)
            pe.wait_ge(s["ab_split"], 3)
            for c in range(KC):
                parity, part = divmod(c, 2)
                last = product(BG[:, c * 4:(c + 1) * 4],
                               [(z[:, parity, k, part * P:(part + 1) * P], u[:, parity, k, :]) for k in range(2)
                                for u, z in hl_passes(ab, dft)])
            last.then_inc(s["abias_ps"], 1)

            pe.wait_ge(s["fold_free"], 3 * KC)
            pe.wait_ge(s["att_copied"], STEPS)
            for t in range(NT):
                pe.wait_ge(s["x1_done"], from_zero(t - 3))
                split_product((BA, BB, BC, BD)[t % 4][:], attT, wo,
                              lambda k: (slice(None), k, slice(t * P, (t + 1) * P)),
                              lambda k: (slice(None), k, slice(None))).then_inc(s["wo_ps"], 1)
            pe.wait_ge(s["x1_done"], NT)

            pe.wait_ge(s["abias_done"], 1)
            transpose_tokens(NT, xhat1, 0)
            pe.wait_ge(s["tr_free"], NT + HT)
            for n, (mm, c, half) in enumerate(SPEC_ORDER):
                if n == 4:
                    transpose_tokens(NT, xhat1, 1)
                if n == 2 * KC:
                    pe.wait_ge(s["tr_free"], 2 * NT)
                pe.wait_ge(s["spec_done"], from_zero(n - 1))
                split_product((BC, BD)[n % 2][:], wf[mm], ln1T,
                              lambda k: (slice(None), k, slice(c * P, (c + 1) * P)),
                              lambda k: (slice(None), k, slice(half * D, (half + 1) * D))).then_inc(s["spec_ps"], 1)
            pe.wait_ge(s["idft_landed"], 16)
            for t in range(NT):
                pe.wait_ge(s["unbound"], 2 + 2 * (t // HT))
                pe.wait_ge(s["x2_done"], from_zero(t - 3))
                for parity in range(2):
                    last = product((BA, BB, BE, BF)[t % 4][:, parity * NF:(parity + 1) * NF],
                                   [(spec[1][:, c, t * P:(t + 1) * P], idft[:, c, :])
                                    for c in (2 * parity, 2 * parity + 1)])
                last.then_inc(s["irfft_ps"], 1)

            for t in range(NT):
                pe.wait_ge(s["l2_lo"], t + 1)
                pe.wait_ge(s["lt_done"], from_zero(t - 1))
                bank = (BG, BH)[t % 2][:].bitcast(F16)
                for n in range(2):
                    for c in range(KC):
                        slot = n * KC + c
                        last = m.transpose(bank[:, slot * P:(slot + 1) * P], l2_hl[n][:, t, c * P:(c + 1) * P], ident16)
                last.then_inc(s["lt_ps"], 1)
            pe.wait_ge(s["wg_split"], 2)
            for t in range(NT):
                pe.wait_ge(s["lt_done"], t + 1)
                last = product(BC[:, t * E:(t + 1) * E],
                               [(l2T[:, t, u, c, :], wg_hl[z][:, c, :]) for c in range(KC)
                                for u, z in ((0, 0), (0, 1), (1, 0))])
            last.then_inc(s["logits_ps"], 1)
            pe.wait_ge(s["onehot_done"], 1)
            for t in range(NT):
                product(BD[:, t * E:(t + 1) * E],
                        [(tri16, onehot16[:, t, :])] + [(ones16, onehot16[:, k, :]) for k in range(t)])
            product(BE[:, 0:E], [(ones16, onehot16[:, k, :]) for k in range(NT)]).then_inc(s["rank_ps"], 1)
            pe.wait_ge(s["routed"], 1)

            def gather(n, c):
                bank = (BG, BH)[c % 2]
                pe.wait_ge(s["perm_done"], n + 1)
                pe.wait_ge(s["xs_done"], from_zero(n * 4 + c - 1))
                if c == 1:
                    pe.wait_ge(s["ids_done"], n)
                for z in range(2):
                    last = product(bank[:, z * CAP:(z + 1) * CAP],
                                   [(l2_hl[z][:, t, c * P:(c + 1) * P], perm[:, t, :]) for t in range(NT)])
                if c == KC - 1:
                    product(bank[:, 2 * CAP:2 * CAP + 2], [(perm[:, t, 0:P], tok_ids[:, t, :]) for t in range(NT)])
                    last = product(bank[0:CB, 2 * CAP + 2:2 * CAP + 4],
                                   [(perm[:, t, P:CAP], tok_ids[:, t, :]) for t in range(NT)])
                last.then_inc(s["xs_ps"], 1)

            def rows(n):
                pe.wait_ge(s["y_done"], n * 4 + 4)
                pe.wait_ge(s["y_out"], n)
                for c in range(KC):
                    m.transpose(BE[:, c * P:(c + 1) * P], yT[:, c, 0:P], ident)
                for c in range(KC):
                    last = m.transpose(BF[0:CB, c * P:(c + 1) * P], yT[:, c, P:CAP], ident)
                last.then_inc(s["yt_ps"], 1)

            def expert(n, prev=True, nxt=True):
                pe.wait_ge(s["xs_done"], n * 4 + 4)
                for k in range(FC // 2):
                    pe.wait_ge(s["e_lo"], n * 8 + k // 2 + 1)
                    pe.wait_ge(s["gelu_done"], from_zero(n * 8 + k - 1))
                    for f in range(2):
                        at = (2 * k + f) % 4 * P
                        w = [z.rearrange("p (c f) -> p c f", c=KC) for z in w_hl[k // 2]]
                        last = product(proj_banks[k % 2][:, f * CAP:(f + 1) * CAP],
                                       [(w[u][:, c, at:at + P], xs[:, c, z, :]) for c in range(KC)
                                        for u, z in ((0, 0), (0, 1), (1, 0))])
                    last.then_inc(s["h_ps"], 1)
                if prev:
                    rows(n - 1)
                if nxt:
                    gather(n + 1, 0)
                    gather(n + 1, 1)
                for c in range(KC):
                    pe.wait_ge(s["e_lo"], n * 8 + 5 + c)
                    pe.wait_ge(s["y_done"], from_zero(n * 4 + c - 1))
                    if c == 0:
                        pe.wait_ge(s["h_lo"], n * 8 + 8)
                    w = [z.rearrange("p (f d) -> p f d", f=FC) for z in w_hl[4 + c]]
                    product((BC, BD)[c % 2][:, 0:CAP],
                            [(w[u][:, f, :], hid_hl[z][:, f, :]) for f in range(FC)
                             for u, z in ((0, 0), (0, 1), (1, 0))]).then_inc(s["y_ps"], 1)
                    if nxt and c < 2:
                        gather(n + 1, 2 + c)

            def round_(r):
                for c in range(KC):
                    gather(r * E, c)
                expert(r * E, prev=False)
                with pe.Fori(1, E - 1) as e:
                    expert(r * E + e)
                expert(r * E + (E - 1), nxt=False)
                rows(r * E + (E - 1))

            round_(0)
            with pe.If(pe.value_load(more_rounds[0:1, 0:1], min_val=0, max_val=1) > 0):
                with pe.Fori(1, ROUNDS) as r:
                    round_(r)


SPEC_ORDER = [(m, c, h) for h in range(2) for m in (1, 2) for c in range(KC)] + \
             [(0, c, h) for h in range(2) for c in range(KC)]
EARLY_PIECES = (2, 6, 11, 14)


def host_constants():
    import numpy as np
    n = np.arange(D)
    f = np.concatenate([np.arange(0, NF, 2), np.arange(1, NF, 2)])
    ang = 2 * np.pi * ((n[:, None] * f[None, :]) % D) / D
    h = NF // 2
    fwd = np.concatenate([np.cos(ang)[:, :h], -np.sin(ang)[:, :h], np.cos(ang)[:, h:], -np.sin(ang)[:, h:]], 1)
    fwd[:, h] = np.where(n % 2, -1.0, 1.0)
    inv = fwd.T * (2.0 / D)
    inv[0] /= 2
    inv[h] /= 2
    fs = fwd[:NF] * SW
    hi = fs.astype(np.float16)
    dft16 = np.stack([hi, (fs - hi).astype(np.float16)])

    def chunks(a):
        return np.ascontiguousarray(a.reshape(KC, P, -1).swapaxes(0, 1))
    return {
        "dft16": np.ascontiguousarray(dft16.reshape(2, 2, P, 2, NF).transpose(0, 2, 3, 1, 4)),
        "idft": chunks(inv[:, :NF].astype(np.float32)),
        "ident": np.eye(P, dtype=np.float32),
        "ident16": np.eye(P, dtype=np.float16),
        "own_head": np.repeat(np.eye(HC, dtype=np.float32), DK, 0),
        "slot_iota": np.tile(np.arange(CAP, dtype=np.float32), (P, 1)),
        "tri16": np.triu(np.ones((P, P), np.float16), 1),
        "ones16": np.ones((P, P), np.float16),
        "rank_order": np.tile(np.arange(E, 0, -1, dtype=np.float32), (P, 1)),
        "tok_ids": np.stack([np.arange(T), np.arange(T) - 2 * T], 1).reshape(NT, P, 2).swapaxes(0, 1).astype(np.float16),
        "id_offset": np.tile(np.array([0, 2 * T], np.float32), (P, 1)),
        "diag": np.tile(np.eye(PAIRS, dtype=np.float32), (2, 1)),
    }


def lay_out(x, ctx_1024, mask_1x1xSxS2_ik0, L0_xattn_Wq, L0_xattn_bq, L0_xattn_Wk, L0_xattn_bk, L0_xattn_Wv,
            L0_xattn_bv, L0_xattn_Wo, L0_xattn_bo, L0_attn_Wq, L0_attn_bq, L0_attn_Wk, L0_attn_bk, L0_attn_Wv,
            L0_attn_bv, L0_ffn_W1, L0_ffn_W2, L0_ffn_Wg, L0_ffn_bg):
    import numpy as np
    a = np.asarray

    def chunks(w):
        return np.ascontiguousarray(a(w).reshape(KC, P, -1).swapaxes(0, 1))

    def column(b):
        return np.ascontiguousarray(a(b).reshape(KC, P).T)
    c = a(ctx_1024)
    main = c[:, :LM].reshape(STEPS, PB, LM, KC, P).transpose(0, 4, 3, 1, 2).reshape(STEPS, P, KC, PB * LM)
    last = c[:, LM].reshape(B, KC, P).transpose(2, 1, 0)
    zero = np.zeros_like(a(L0_attn_bq))
    return {
        "x_t": np.ascontiguousarray(a(x).reshape(NT, P, D).swapaxes(0, 1)),
        "ctx_t": np.ascontiguousarray(main), "ctx_last": np.ascontiguousarray(last),
        "mask": np.ascontiguousarray(a(mask_1x1xSxS2_ik0).reshape(S, L)),
        "wq_t": chunks(a(L0_xattn_Wq).T), "wk_t": chunks(a(L0_xattn_Wk).T), "wv_t": chunks(a(L0_xattn_Wv).T),
        "wo_t": chunks(a(L0_xattn_Wo).T),
        "bq": column(L0_xattn_bq), "bk": column(L0_xattn_bk), "bv": column(L0_xattn_bv), "bo": a(L0_xattn_bo),
        "awt": np.stack([chunks(a(w).T).reshape(P, 2, 2, D) for w in (L0_attn_Wq, L0_attn_Wk, L0_attn_Wv)]),
        "wg": chunks(L0_ffn_Wg), "bg": a(L0_ffn_bg),
        "w1": np.ascontiguousarray(a(L0_ffn_W1).reshape(E, KC, P, 4, 512).transpose(0, 3, 2, 1, 4)).reshape(E * 4, P, -1),
        "w2": np.ascontiguousarray(a(L0_ffn_W2).reshape(E, FC, P, KC, P).transpose(0, 3, 2, 1, 4)).reshape(E * 4, P, -1),
        "ab": chunks(np.stack([a(L0_attn_bq), a(L0_attn_bk), a(L0_attn_bv), zero], 1)).reshape(P, 2, 2, 4),
    }


def kernel(**inputs):
    import numpy as np
    import concourse.bacc as bacc
    from concourse.bass_utils import run_bass_kernel_spmd

    nc = bacc.Bacc("TRN2", target_bir_lowering=False, num_devices=1)
    arrays = {**lay_out(**inputs), **host_constants()}
    i = {n: nc.dram_tensor(f"in_{n}", a.shape, mybir.dt.from_np(a.dtype), kind="ExternalInput").ap()
         for n, a in arrays.items()}
    i["vlast_dram"] = nc.dram_tensor("vlast_dram", (2, B, D), F16, kind="Internal").ap()
    i["x2_dram"] = nc.dram_tensor("x2_dram", (T, D), F32, kind="Internal").ap()
    out = nc.dram_tensor("out", (B, S, D), F32, kind="ExternalOutput").ap()
    perceiver_block(nc, i, out)
    r = run_bass_kernel_spmd(nc, [{f"in_{n}": a for n, a in arrays.items()}], core_ids=[0])
    return r.results[0]["out"]
```

```python
from contextlib import ExitStack
from itertools import count

import concourse.bass as bass
from concourse import mybir

F32 = mybir.dt.float32
F16 = mybir.dt.float16
I32 = mybir.dt.int32
U32 = mybir.dt.uint32
ALU = mybir.AluOpType
ACT = mybir.ActivationFunctionType
AX_X = mybir.AxisListType.X

P = 128
B, S, D = 32, 32, 512
L = 257
H = 16
DK = D // H
KC = D // P
HC = P // DK
T = B * S
NT = T // P
PB = 2
STEPS = B // PB
LM = 256
PAIRS = PB * KC
E, FF = 8, 2048
FC = FF // P
CAP = 160
CB = CAP - P
ROUNDS = -(-T // CAP)
PIECES = 8
NF = D // 2
HT = NT // 2
EPS = 1e-5

SX = 2.0 ** 8
SW = 2.0 ** 12
SK = 2.0 ** 6
SP_ = 2.0 ** 12
SF = 2.0 ** 8
SG = 2.0 ** 6
S2 = 2.0 ** 7
SH = 2.0 ** 3
NEG = -1e30
ISD = 1.0 / (float(DK) ** 0.5)


def perceiver_block(nc, i, out):
    ctx = ExitStack()
    with ctx:
        def sem(name):
            return ctx.enter_context(nc.semaphore(name))

        KB = 1024
        arena = ctx.enter_context(nc.sbuf_tensor("arena", [P, 204 * KB // 4], F32))
        banks = [ctx.enter_context(nc.psum_tensor(f"bank{n}", [P, 512], F32)) for n in range(8)]
        BA, BB, BC, BD, BE, BF, BG, BH = banks
        proj_banks = (BA, BB)
        TR_BANKS = (BE, BF, BG, BH)
        FOLD_BANKS = (BC, BA, BD, BB)

        def size(shape, dt):
            n = 2 if dt == F16 else 4
            for x in shape:
                n *= x
            return n

        def view(off, shape, dt, parts=P):
            n = size(shape, dt)
            assert off % 4 == 0 and n % 4 == 0 and off + n <= 204 * KB, (off, n)
            a = arena[0:parts, off // 4:(off + n) // 4]
            if dt != F32:
                a = a.bitcast(dt)
            if len(shape) > 1:
                names = [f"d{k}" for k in range(len(shape))]
                a = a.rearrange(f"p ({' '.join(names)}) -> p {' '.join(names)}",
                                **{k: v for k, v in zip(names, shape)})
            return a

        class Region:
            def __init__(self, start, end):
                self.at, self.end = start, end

            def take(self, shape, dt, parts=P):
                v = view(self.at, shape, dt, parts)
                self.at += -(-size(shape, dt) // 32) * 32
                assert self.at <= self.end, (self.at, self.end)
                return v

        keep = Region(0, 28 * KB)
        x_tok = keep.take([NT, D], F32)
        ident = keep.take([P], F32)
        ident16 = keep.take([P], F16)
        bq_col = keep.take([KC], F32)
        bq_scaled = keep.take([KC], F32)
        mask_bias = keep.take([L], F32)
        stats = keep.take([NT, 6], F32)
        mean_var = keep.take([NT, 2], F32)
        var_eps = keep.take([NT], F32)
        minus_half = keep.take([NT], F32)
        shift = keep.take([NT], F32)
        rstd = keep.take([NT], F32)
        score_sums = keep.take([PAIRS], F32)
        sums_scaled = keep.take([PAIRS], F32)
        recip = keep.take([PAIRS], F32)
        row_max = keep.take([PAIRS], F32)
        neg_max = keep.take([PAIRS], F32)
        diag = keep.take([PAIRS], F32)
        own_head = keep.take([HC], F32)
        dft_bias = keep.take([KC, 4], F32)
        lhs_bind = keep.take([3, 2, B], F32)
        bind_sums = keep.take([4, 2, B], F32)

        perm = keep.take([NT, CAP], F16)
        slot_iota = keep.take([CAP], F32)
        tri16 = keep.take([P], F16)
        ones16 = keep.take([P], F16)
        wg_stage = keep.take([KC, E], F32)
        wg_hl = [keep.take([KC, E], F16) for _ in range(2)]
        bg_bc = keep.take([E], F32)
        rank_order = keep.take([E], F32)
        tok_ids = keep.take([NT, 2], F16)
        id_offset = keep.take([2], F32)
        logits, is_max, score, slot_of = (keep.take([NT, E], F32) for _ in range(4))
        onehot16 = keep.take([NT, E], F16)
        top, top2 = (keep.take([NT], F32) for _ in range(2))
        most = keep.take([1], F32)
        more_rounds = keep.take([1], I32)
        ids_next = [keep.take([2], I32), keep.take([2], I32, parts=CB)]
        ids = [keep.take([2], I32), keep.take([2], I32, parts=CB)]
        ab_stage = keep.take([2, 2, 4], F32)
        ab_sd = keep.take([2, 2, 4], F32)
        ab = [keep.take([2, 2, 4], F16) for _ in range(2)]

        xa = Region(28 * KB, 204 * KB)
        q_off = xa.at
        qT = [xa.take([KC, T], F16) for _ in range(2)]
        wk_off = xa.at
        wk = [xa.take([KC, D], F16) for _ in range(2)]
        wv = [xa.take([KC, D], F16) for _ in range(2)]
        wo_off = xa.at
        wo = [xa.take([KC, D], F16) for _ in range(2)]
        attT = [xa.take([KC, T], F16) for _ in range(2)]
        lnT = attT
        stage_off = xa.at
        ctx_stage = [xa.take([KC, PB * LM], F32) for _ in range(2)]
        ctx_hl = [[xa.take([KC, PB * LM], F16) for _ in range(2)] for _ in range(2)]
        wq = ctx_hl[1]
        kT_off = xa.at
        kT = [xa.take([KC, PB, L + 1], F16) for _ in range(2)]
        v_hl = [xa.take([PB * 2, D], F16) for _ in range(2)]
        q_bd = [xa.take([KC, PB, P], F16) for _ in range(2)]
        sm_off = xa.at
        sm = xa.take([PAIRS, L], F32)
        p_off = xa.at
        p_all = xa.take([2, PAIRS, L + 1], F16)
        p_hl = [p_all[:, n] for n in range(2)]
        pt_off = xa.at
        pT = xa.take([PB, 2, 2, KC, P], F16)
        pT_last = xa.take([PAIRS, P], F16, parts=2 * PAIRS)
        vl_all = xa.take([2, STEPS, P], F16, parts=2 * PAIRS)
        vl_cur = xa.take([2, P], F16, parts=2 * PAIRS)
        att_st = [xa.take([KC, PB, S], F16) for _ in range(2)]
        klast = [xa.take([KC, B], F16) for _ in range(2)]
        ctxl_stage = xa.take([KC, B], F32)
        ctxl = [xa.take([KC, B], F16) for _ in range(2)]
        bk_col = xa.take([KC], F32)
        bv_col = xa.take([KC], F32)
        mask_int = view(sm_off, [L], I32)
        q_f = [view(pt_off + n * 2 * KB, [D], F32) for n in range(2)]
        bv_bc = [view(pt_off + 4 * KB + n * KB, [KC, P], F16) for n in range(2)]
        bo_bc = view(pt_off + 6 * KB, [D], F32)
        vlast = [view(sm_off + 2 * KB + n * KB, [D], F16, parts=B) for n in range(2)]
        bias_tile = view(sm_off + 4 * KB, [D], F32)

        W_HALF = 4 * KB
        wt_off = 204 * KB - 7 * W_HALF
        assert wt_off >= xa.at
        spare_at = [wt_off, wt_off + 2 * W_HALF, wt_off + 4 * W_HALF]
        a_at = [wt_off + (1 + 2 * n) * W_HALF for n in range(3)]
        wt_stage = [view(a, [KC, D], F32) for a in a_at]
        wt_a = [view(a, [2, D], F32) for a in a_at]
        wt_b = [view(a + W_HALF, [2, D], F32) for a in a_at]
        wt_sum = [view(a, [2, D], F32) for a in spare_at]
        wt = [[[view(base + n * W_HALF // 2, [2, D], F16) for n in range(2)] for base in (a_at[k], spare_at[k])]
              for k in range(3)]
        xhat0 = view(wt_off, [NT, D], F32)
        wq_stage, wk_stage = ctx_stage
        wv_stage, wo_stage = wt_stage[2], view(p_off, [KC, D], F32)

        xhat1 = view(q_off, [NT, D], F32)
        ln1T = [[view(wk_off + (half * 2 + n) * 4 * KB, [KC, D], F16) for n in range(2)] for half in range(2)]
        fa = Region(stage_off, 204 * KB)
        dft_off = fa.at
        dft = [fa.take([2, 2, NF], F16) for _ in range(2)]
        idft = fa.take([KC, NF], F32)
        wf_off = fa.at
        wf = [[fa.take([KC, D], F16) for _ in range(2)] for _ in range(3)]
        assert fa.at <= kT_off
        spec_off = fa.at
        spec = [[fa.take([KC, D], F32) for _ in range(2)] for _ in range(3)]
        after_spec = fa.at
        prod = view(dft_off, [2, D], F32)

        PW = KC * 512
        PIECE = 8 * KB
        e_stage = [view((172 + 8 * n) * KB, [PW], F32) for n in range(4)]
        assert wo_off + 3 * PIECE <= dft_off and after_spec + PIECE <= 172 * KB
        piece_at = [wo_off, wo_off + PIECE, wo_off + 2 * PIECE, after_spec,
                    wf_off, wf_off + PIECE, wf_off + 2 * PIECE, dft_off]
        w_hl = [[view(at + n * PIECE // 2, [PW], F16) for n in range(2)] for at in piece_at]
        l2_f = xhat1
        l2_hl = [[view(wk_off + (half * 2 + n) * 4 * KB, [HT, D], F16) for n in range(2)] for half in range(2)]

        def l2_tile(n, t):
            return l2_hl[t // HT][n][:, t % HT]

        ea = Region(spec_off, after_spec)
        l2T = ea.take([NT, 2, KC, P], F16)
        hid_hl = [ea.take([FC, CAP], F16) for _ in range(2)]
        hid_f = [ea.take([2, CAP], F32) for _ in range(4)]
        xs = ea.take([KC, 2, CAP], F16)
        yT = ea.take([KC, CAP], F32)
        y_rows = [ea.take([D], F32), ea.take([D], F32, parts=CB)]
        x2_rows = [ea.take([D], F32), ea.take([D], F32, parts=CB)]

        names = """x_landed0 x_landed1 x_landed2 ident_landed consts_landed wq_landed wk_landed wv_landed wo_landed
        ctxl_landed bias_landed ctx_landed0 ctx_landed1 dft_landed idft_landed wt_landed0 wt_landed1
        wt_landed2 ab_landed vlast_stored vl_landed ln_var ln_rstd ln_out tr_ps tr_hi tr_free w_hi w_lo
        bq_done q_ps q_f32 q_hi q_lo ctxl_split last_ps last_hi last_lo bias_ps bias_done x_biased proj_ps
        proj_hi proj_free split_hi split_lo s_ps s_free s_max s_neg exp_done sums_sc recip_done p_hi p_lo
        q_ready vl_ready pt_ps pt_dve pt_act pv_ps pv_hi pv_free att_copied wo_ps x1_done fold_ps fold_hi
        fold_free wt_sums ab_split abias_ps abias_done wt_hi wt_lo spec_ps spec_done products unbound
        irfft_ps x2_done chain_dve chain_pool pool_waits gate_landed l2_shift l2_normal x2_stored wg_split
        l2_hi l2_lo lt_ps lt_done logits_ps onehot_done rank_ps count_ps routed e_landed0 e_landed1
        e_landed2 e_landed3 e_hi e_lo perm_done xs_ps xs_done h_ps gelu_done h_hi h_lo y_ps y_done yt_ps
        y_out ids_done rows_landed scattered shifted ranks_moved""".split()
        s = {n: sem(n) for n in names}

        def from_zero(count):
            return max(count, 0) if isinstance(count, int) else count

        def lnT_tile(n, t):
            return lnT[n][:, :, t * P:(t + 1) * P]

        def ln1T_tile(n, t):
            return ln1T[t // HT][n][:, :, t % HT * P:(t % HT + 1) * P]

        def hl_passes(a, b):
            return ((a[0], b[0]), (a[0], b[1]), (a[1], b[0]))

        block = ctx.enter_context(nc.Block())

        @block.sync
        def _(sp):
            sp.dma_start(x_tok[:, 0:2], i["x_t"][:, 0:2]).then_inc(s["x_landed0"], 16)
            sp.dma_start(x_tok[:, 2:HT], i["x_t"][:, 2:HT]).then_inc(s["x_landed1"], 16)
            sp.dma_start(ident, i["ident"]).then_inc(s["ident_landed"], 16)
            sp.dma_start(wq_stage, i["wq_t"]).then_inc(s["wq_landed"], 16)
            sp.dma_start(x_tok[:, HT:NT], i["x_t"][:, HT:NT]).then_inc(s["x_landed2"], 16)
            for src, dst in ((i["ident16"], ident16), (i["bq"], bq_col), (i["bk"], bk_col),
                             (i["bv"], bv_col), (i["diag"], diag[0:2 * PAIRS]),
                             (i["own_head"], own_head)):
                sp.dma_start(dst, src).then_inc(s["consts_landed"], 16)
            for g in range(HC):
                sp.dma_start(mask_int[g * S:(g + 1) * S], i["mask"]).then_inc(s["consts_landed"], 16)
            sp.dma_start(wk_stage, i["wk_t"]).then_inc(s["wk_landed"], 16)
            sp.dma_start(ctxl_stage, i["ctx_last"]).then_inc(s["ctxl_landed"], 16)
            sp.dma_start(wv_stage, i["wv_t"]).then_inc(s["wv_landed"], 16)
            sp.dma_start(ab_stage, i["ab"]).then_inc(s["ab_landed"], 16)
            sp.dma_start(bo_bc, i["bo"].partition_broadcast(P)).then_inc(s["bias_landed"], 16)
            sp.dma_start(wo_stage, i["wo_t"]).then_inc(s["wo_landed"], 16)
            sp.wait_ge(s["w_lo"], 1)
            sp.dma_start(ctx_stage[0], i["ctx_t"][0]).then_inc(s["ctx_landed0"], 16)
            sp.wait_ge(s["w_lo"], 2)
            sp.dma_start(ctx_stage[1], i["ctx_t"][1]).then_inc(s["ctx_landed1"], 16)
            sp.wait_ge(s["tr_ps"], NT)
            sp.wait_ge(s["w_lo"], 3)
            for n in range(3):
                sp.dma_start(wt_stage[n], i["awt"][n].rearrange("p k c d -> p (k c) d")).then_inc(s[f"wt_landed{n}"], 16)
            for src, dst in ((i["slot_iota"], slot_iota), (i["tri16"], tri16), (i["ones16"], ones16),
                             (i["wg"], wg_stage), (i["bg"].partition_broadcast(P), bg_bc),
                             (i["rank_order"], rank_order), (i["tok_ids"], tok_ids), (i["id_offset"], id_offset)):
                sp.dma_start(dst, src).then_inc(s["gate_landed"], 16)
            sp.wait_ge(s["last_lo"], 2)
            for n in range(2):
                sp.dma_start(i["vlast_dram"][n], vlast[n]).then_inc(s["vlast_stored"], 16)
            sp.wait_ge(s["vlast_stored"], 32)
            for rows, dst, n in ((0, 0, 0), (PAIRS, 0, 0), (0, 1, 1), (PAIRS, 1, 1)):
                sp.dma_start(vl_all[rows:rows + PAIRS, dst],
                             i["vlast_dram"][n].rearrange("(t b) (c x) -> (b c) t x", b=PB, c=KC)
                             ).then_inc(s["vl_landed"], 16)
            with sp.Fori(1, STEPS // PB) as k:
                for par in range(2):
                    st = k * 2 + par
                    sp.wait_ge(s["split_lo"], from_zero(st - 1))
                    sp.dma_start(ctx_stage[par], i["ctx_t"][bass.ds(st, 1)].rearrange("a p c t -> p (a c) t")
                                 ).then_inc(s[f"ctx_landed{par}"], 16)
            sp.wait_ge(s["split_lo"], STEPS)
            for n in range(2):
                sp.dma_start(dft[n], i["dft16"][n]).then_inc(s["dft_landed"], 16)
            sp.dma_start(idft, i["idft"]).then_inc(s["idft_landed"], 16)

            def load_piece(e, n, done):
                sp.wait_ge(s["e_lo"], done)
                src = i["w1"] if n < 4 else i["w2"]
                sp.dma_start(e_stage[n % 4], src[bass.ds(e * 4 + n % 4, 1)].rearrange("a p x -> p (a x)")
                             ).then_inc(s[f"e_landed{n % 4}"], 16)

            sp.wait_ge(s["fold_ps"], 3 * KC)
            sp.wait_ge(s["pv_free"], STEPS * PB)
            for n in range(PIECES):
                load_piece(0, n, from_zero(n - 3))
            sp.wait_ge(s["x2_done"], NT)
            sp.dma_start(i["x2_dram"].rearrange("(t p) d -> p t d", p=P), x_tok).then_inc(s["x2_stored"], 16)

            def rest_of_round(r):
                with sp.Fori(1, E) as e:
                    for n in range(PIECES):
                        load_piece(e, n, r * (E * PIECES) + e * PIECES + (n - 3))

            rest_of_round(0)
            sp.wait_ge(s["routed"], 1)
            with sp.If(sp.value_load(more_rounds[0:1, 0:1], min_val=0, max_val=1) > 0):
                with sp.Fori(1, ROUNDS) as r:
                    for n in range(PIECES):
                        load_piece(0, n, r * (E * PIECES) + (n - 3))
                    rest_of_round(r)

        @block.gpsimd
        def _(pool):
            g = nc.gpsimd

            def power(n):
                ts = slice(LN_GROUPS[n][0], LN_GROUPS[n][-1] + 1)
                pool.wait_ge(s["ln_var"], n + 1)
                g.tensor_tensor(rstd[:, ts], var_eps[:, ts], minus_half[:, ts], ALU.pow).then_inc(s["ln_rstd"], 1)

            g.memset(minus_half, -0.5).then_inc(s["chain_pool"], 1)
            pool.wait_ge(s["chain_pool"], 1)
            power(0)
            power(1)
            for n in range(KC * 2):
                pool.wait_ge(s["q_f32"], n + 1)
                half, c = divmod(n, KC)
                g.tensor_copy(qT[0][:, c, half * D:(half + 1) * D], q_f[n % 2]).then_inc(s["q_hi"], 1)
            pool.wait_ge(s["q_lo"], KC * 2)
            pool.wait_ge(s["last_lo"], 1)

            def weight_sums(k):
                pool.wait_ge(s[f"wt_landed{k}"], 16)
                pool.wait_ge(s["wt_lo"], 2 * k)
                g.tensor_tensor(wt_sum[k], wt_a[k], wt_b[k], ALU.add).then_inc(s["wt_sums"], 1)
                pool.wait_ge(s["wt_sums"], 2 * k + 1)
                g.tensor_tensor(wt_b[k], wt_a[k], wt_b[k], ALU.subtract).then_inc(s["wt_sums"], 1)

            def step(st, cur=True, prev=True):
                if prev:
                    pool.wait_ge(s["vl_landed"], 64)
                    pool.wait_ge(s["pv_ps"], from_zero(st * 2 - 2))
                    pool.sem_inc(s["pool_waits"], 1)
                    g.tensor_copy(vl_cur, vl_all[:, :, bass.ds(st - 1, 1), :].rearrange("p h a x -> p h (a x)")
                                  ).then_inc(s["vl_ready"], 1)
                if cur:
                    pool.wait_ge(s["s_ps"], st * PAIRS)
                    pool.sem_inc(s["pool_waits"], 1)
                    for n in range(2):
                        for b in range(PB):
                            g.tensor_tensor(q_bd[n][:, :, b, :].rearrange("p c (r q) -> p c r q", r=HC),
                                            qT[n][:, :, bass.ds(st * (PB * S) + b * S, S)].unsqueeze(2)
                                            .broadcast_to((P, KC, HC, S)),
                                            own_head.unsqueeze(1).unsqueeze(3).broadcast_to((P, KC, HC, S)), ALU.mult)
                        last = g.tensor_copy(kT[n][:, :, :, LM], klast[n][:, :, bass.ds(st * PB, PB)])
                    last.then_inc(s["q_ready"], 1)
                if prev:
                    pool.wait_ge(s["pv_free"], st * 2)
                    pool.sem_inc(s["pool_waits"], 1)
                    for n in range(2):
                        last = g.tensor_copy(attT[n][:, :, bass.ds(st * (PB * S) - PB * S, PB * S)],
                                             att_st[n].rearrange("p c b q -> p c (b q)"))
                    last.then_inc(s["att_copied"], 1)

            step(0, prev=False)
            pool.wait_ge(s["bias_done"], 1)
            pool.wait_ge(s["ln_out"], NT)
            g.tensor_tensor(x_tok, x_tok, bias_tile.unsqueeze(1).broadcast_to((P, NT, D)), ALU.add
                            ).then_inc(s["x_biased"], 1)
            weight_sums(0)
            step(1)
            weight_sums(1)
            with pool.Fori(1, STEPS // 2 - 1) as k:
                for par in range(2):
                    step(k * 2 + par)
            step(STEPS - 2)
            weight_sums(2)
            step(STEPS - 1)
            step(STEPS, cur=False)
            def l2_lo(t):
                pool.wait_ge(s["l2_hi"], t + 1)
                g.tensor_tensor(l2_tile(1, t), l2_f[:, t, :], l2_tile(0, t), ALU.subtract).then_inc(s["l2_lo"], 1)

            for n in range(2, 5):
                power(n)
            for t in LN_GROUPS[4]:
                l2_lo(t)
            power(5)
            l2_lo(LN_GROUPS[5][0])
            l2_lo(LN_GROUPS[5][1])
            power(6)
            pool.wait_ge(s["x2_stored"], 16)

            out_rows = out.rearrange("b q d -> (b q) d")

            def scatter(n):
                pool.wait_ge(s["y_out"], n + 1)
                pool.sem_inc(s["pool_waits"], 1)
                for part in range(2):
                    g.indirect_dma_start(out=out_rows, out_offset=bass.IndirectOffsetOnAxis(
                                             ap=ids[part][:, 1:2].bitcast(U32), axis=0),
                                         in_=y_rows[part], in_offset=None, bounds_check=T - 1, oob_is_err=False
                                         ).then_inc(s["scattered"], 16)

            def expert(n, prev=True):
                for k in range(FC // 2):
                    pool.wait_ge(s["gelu_done"], n * 8 + k + 1)
                    pool.sem_inc(s["pool_waits"], 1)
                    g.tensor_scalar(hid_hl[0][:, 2 * k:2 * k + 2, :], hid_f[k % 4], SH, 1.0, ALU.mult, ALU.mult
                                    ).then_inc(s["h_hi"], 1)
                if prev:
                    scatter(n - 1)
                pool.wait_ge(s["shifted"], n + 1)
                pool.sem_inc(s["pool_waits"], 1)
                for part in range(2):
                    g.indirect_dma_start(out=x2_rows[part], out_offset=None, in_=i["x2_dram"],
                                         in_offset=bass.IndirectOffsetOnAxis(ap=ids[part][:, 0:1].bitcast(U32), axis=0)
                                         ).then_inc(s["rows_landed"], 16)

            def round_(r):
                expert(r * E, prev=False)
                with pool.Fori(1, E) as e:
                    expert(r * E + e)
                scatter(r * E + (E - 1))
                pool.wait_ge(s["scattered"], r * (32 * E) + 32 * E)
                pool.sem_inc(s["pool_waits"], 1)

            round_(0)
            pool.wait_ge(s["routed"], 1)
            with pool.If(pool.value_load(more_rounds[0:1, 0:1], min_val=0, max_val=1) > 0):
                with pool.Fori(1, ROUNDS) as r:
                    round_(r)

        @block.scalar
        def _(act):
            a = nc.scalar

            def hi(dst, src, scale):
                return a.activation(dst, src, ACT.Copy, scale=scale)

            def weight_hi(dst, src, landed):
                act.wait_ge(s[landed], 16)
                hi(dst[0], src, SW).then_inc(s["w_hi"], 1)

            def tokens_hi(dst, base, half):
                for t in range(half * HT, (half + 1) * HT):
                    act.wait_ge(s["tr_ps"], base + t + 1)
                    hi(dst(0, t), TR_BANKS[t % 4][:].rearrange("p (c x) -> p c x", c=KC), SX
                       ).then_inc(s["tr_hi"], 1)

            weight_hi(wq, wq_stage, "wq_landed")
            tokens_hi(lnT_tile, 0, 0)
            act.wait_ge(s["bq_done"], 1)
            for n in range(KC * 2):
                if n == 1:
                    weight_hi(wk, wk_stage, "wk_landed")
                if n == 3:
                    tokens_hi(lnT_tile, 0, 1)
                act.wait_ge(s["q_ps"], n + 1)
                act.wait_ge(s["q_lo"], from_zero(n - 1))
                c = n % KC
                a.activation(q_f[n % 2], (BC, BD)[n % 2][:], ACT.Identity, bias=bq_scaled[:, c:c + 1],
                             scale=1.0 / SW).then_inc(s["q_f32"], 1)
                if n == 4:
                    act.wait_ge(s["ctxl_landed"], 16)
                    hi(ctxl[0], ctxl_stage, SX).then_inc(s["ctxl_split"], 1)
                    act.wait_ge(s["ab_split"], 1)
                    hi(ab[0], ab_sd, SW).then_inc(s["ab_split"], 1)
                    weight_hi(wv, wv_stage, "wv_landed")
                if n == 5:
                    weight_hi(wo, wo_stage, "wo_landed")
                if n == 6:
                    act.wait_ge(s["ctx_landed0"], 16)
                    hi(ctx_hl[0][0], ctx_stage[0], SX).then_inc(s["split_hi"], 1)
            act.wait_ge(s["last_ps"], 1)
            hi(klast[0], BE[:, 0:KC * B].rearrange("p (c b) -> p c b", c=KC), SK / (SX * SW)).then_inc(s["last_hi"], 1)
            act.wait_ge(s["last_ps"], 2)
            hi(vlast[0], BF[0:B, :], 1.0 / SW).then_inc(s["last_hi"], 1)

            def mixing_weights_hi(k, n):
                act.wait_ge(s["wt_sums"], 2 * k + 2)
                if n == 1:
                    act.wait_ge(s["wt_lo"], 2 * k + 1)
                hi(wt[k][n][0], (wt_sum[k], wt_b[k])[n], SW).then_inc(s["wt_hi"], 1)

            def fold_hi(n):
                act.wait_ge(s["fold_ps"], n + 1)
                hi(wf[n // KC][0][:, n % KC, :], FOLD_BANKS[n % 4][:], SF / (SW * SW)).then_inc(s["fold_hi"], 1)

            def step(st, par, landed, cur=True, prev=True, nxt=True, mixing=None):
                n0 = st * 8

                def k_hi(c):
                    if cur:
                        act.wait_ge(s["proj_ps"], n0 + c + 1)
                        hi(kT[0][:, c, :, 0:LM], proj_banks[c % 2][:].rearrange("p (b x) -> p b x", b=PB),
                           SK / (SX * SW)).then_inc(s["proj_hi"], 1)
                    else:
                        fold_hi(2 * c)
                        fold_hi(2 * c + 1)

                def v_hi(t):
                    if cur:
                        act.wait_ge(s["proj_ps"], n0 + 5 + t)
                        hi(v_hl[0][:, t, :], proj_banks[t % 2][:], 1.0 / SW).then_inc(s["proj_hi"], 1)
                    else:
                        fold_hi(8 + t)

                def exp(m, b):
                    act.wait_ge(s["s_neg"], m * 2 + 1 + b)
                    for j in range(b * KC, b * KC + KC):
                        a.activation(sm[:, j, :], sm[:, j, :], ACT.Exp, bias=neg_max[:, j:j + 1],
                                     scale=ISD / (SX * SK), accum_out=score_sums[:, j:j + 1]
                                     ).then_inc(s["exp_done"], 1)

                def p_hi(m, b):
                    act.wait_ge(s["recip_done"], m * 2 + 1 + b)
                    for j in range(b * KC, b * KC + KC):
                        hi(p_hl[0][:, j, 0:L], sm[:, j, :], recip[:, j:j + 1]).then_inc(s["p_hi"], 1)

                def pt_copy(b):
                    act.wait_ge(s["pt_ps"], st * 5 - 5 + (2, 5)[b])
                    a.activation(pT[:, b, 1].rearrange("p h c x -> p (h c x)"), BF[:].bitcast(F16), ACT.Copy
                                 ).then_inc(s["pt_act"], 1)

                if prev:
                    exp(st - 1, 1)
                k_hi(0)
                if prev:
                    p_hi(st - 1, 1)
                k_hi(1)
                if prev:
                    pt_copy(0)
                if nxt:
                    act.wait_ge(s[f"ctx_landed{1 - par}"], landed)
                    hi(ctx_hl[1 - par][0], ctx_stage[1 - par], SX).then_inc(s["split_hi"], 1)
                k_hi(2)
                if prev:
                    pt_copy(1)
                k_hi(3)
                if mixing is not None:
                    mixing_weights_hi(mixing, 0)
                if prev:
                    act.wait_ge(s["att_copied"], from_zero(st - 1))
                    for b in range(PB):
                        act.wait_ge(s["pv_ps"], st * 2 - 1 + b)
                        for r in range(HC):
                            rows = slice(r * DK, (r + 1) * DK)
                            last = hi(att_st[0][rows, :, b, :],
                                      (BG, BH)[b][rows, :].rearrange("p (c x) -> p c x", c=KC)[:, :, r * S:(r + 1) * S],
                                      1.0 / SP_)
                        last.then_inc(s["pv_hi"], 1)
                v_hi(0)
                if mixing is not None:
                    mixing_weights_hi(mixing, 1)
                v_hi(1)
                if cur:
                    exp(st, 0)
                v_hi(2)
                if cur:
                    p_hi(st, 0)
                v_hi(3)

            step(0, 0, 16, prev=False)
            step(1, 1, 32, mixing=0)
            with act.Fori(1, STEPS // 2 - 1) as k:
                step(k * 2, 0, k * 16 + 16)
                step(k * 2 + 1, 1, k * 16 + 32)
            step(STEPS - 2, 0, STEPS // 2 * 16, mixing=1)
            step(STEPS - 1, 1, 0, nxt=False, mixing=2)
            step(STEPS, 0, 0, cur=False, nxt=False)

            act.wait_ge(s["abias_ps"], 1)
            hi(dft_bias, BG[:, 0:KC * 4].rearrange("p (c m) -> p c m", c=KC), 1.0 / (SW * SW)).then_inc(s["abias_done"], 1)

            def piece_hi(n, k):
                act.wait_ge(s[f"e_landed{k % 4}"], n * 32 + (16 * (k // 4) + 16))
                hi(w_hl[k][0], e_stage[k % 4], SG if k < 4 else S2).then_inc(s["e_hi"], 1)

            tokens_hi(ln1T_tile, NT, 0)
            act.wait_ge(s["abias_done"], 1)
            def l2_split(t):
                if t in LN_GROUPS[5]:
                    act.wait_ge(s["l2_normal"], t - HT + 1)
                else:
                    act.wait_ge(s["ln_out"], 2 * NT + (t + 1 if t < HT else t - 1))
                hi(l2_tile(0, t), l2_f[:, t, :], 1.0).then_inc(s["l2_hi"], 1)

            def gate_transpose_out(t):
                act.wait_ge(s["lt_ps"], t + 1)
                a.activation(l2T[:, t].rearrange("p h c x -> p (h c x)"), (BG, BH)[t % 2][:].bitcast(F16), ACT.Copy
                             ).then_inc(s["lt_done"], 1)

            for n, (m, c, half) in enumerate(SPEC_ORDER):
                if n == 6:
                    tokens_hi(ln1T_tile, NT, 1)
                act.wait_ge(s["spec_ps"], n + 1)
                a.activation(spec[m][half][:, c, :], (BC, BD)[n % 2][:], ACT.Identity,
                             bias=dft_bias[:, c, m:m + 1], scale=1.0 / (SX * SF)).then_inc(s["spec_done"], 1)
                if n in EARLY_PIECES:
                    piece_hi(0, EARLY_PIECES.index(n))
                if n == 18:
                    act.wait_ge(s["gate_landed"], 16 * 8)
                    hi(wg_hl[0], wg_stage, SG).then_inc(s["wg_split"], 1)
                if n == 20:
                    for t in range(HT):
                        l2_split(t)
            act.wait_ge(s["unbound"], 2)
            for t in range(HT):
                gate_transpose_out(t)
            act.wait_ge(s["l2_shift"], 1)
            for t in LN_GROUPS[5]:
                a.activation(l2_f[:, t, :], x_tok[:, t, :], ACT.Identity, bias=shift[:, t:t + 1],
                             scale=rstd[:, t:t + 1]).then_inc(s["l2_normal"], 1)
                l2_split(t)
            act.wait_ge(s["unbound"], 4)
            gate_transpose_out(HT)
            l2_split(HT + 2)
            gate_transpose_out(HT + 1)
            l2_split(HT + 3)
            gate_transpose_out(HT + 2)
            gate_transpose_out(HT + 3)
            for k in range(4, PIECES - 1):
                piece_hi(0, k)

            def expert(n, nxt=True):
                for k in range(FC // 2):
                    act.wait_ge(s["h_ps"], n * 8 + k + 1)
                    act.wait_ge(s["h_lo"], from_zero(n * 8 + k - 3))
                    a.activation(hid_f[k % 4], proj_banks[k % 2][:, 0:2 * CAP].rearrange("p (c x) -> p c x", c=2),
                                 ACT.Gelu_apprx_tanh, scale=1.0 / (SX * SG)).then_inc(s["gelu_done"], 1)
                    if k == 1:
                        piece_hi(n, PIECES - 1)
                    elif nxt and k % 2:
                        piece_hi(n + 1, k // 2 - 1)
                if nxt:
                    piece_hi(n + 1, 3)
                for c in range(KC):
                    act.wait_ge(s["y_ps"], n * 4 + c + 1)
                    hi(yT[:, c, :], (BC, BD)[c % 2][:, 0:CAP], 1.0 / (S2 * SH)).then_inc(s["y_done"], 1)
                    if nxt and c < KC - 1:
                        piece_hi(n + 1, 4 + c)

            def experts(r):
                expert(r * E)
                with act.Fori(1, E - 1) as e:
                    expert(r * E + e)
                expert(r * E + (E - 1), nxt=False)

            experts(0)
            act.wait_ge(s["routed"], 1)
            with act.If(act.value_load(more_rounds[0:1, 0:1], min_val=0, max_val=1) > 0):
                with act.Fori(1, ROUNDS) as r:
                    for k in range(PIECES - 1):
                        piece_hi(r * E, k)
                    experts(r)

        @block.vector
        def _(dve):
            v = nc.vector
            chain = count(1)

            def lo(dst, src, scale, h):
                return v.scalar_tensor_tensor(dst, src, scale, h, ALU.mult, ALU.subtract)

            def variances(ts, scale=1.0):
                for t in ts:
                    last = v.bn_aggr(mean_var[:, t, :], stats[:, t, :])
                last.then_inc(s["chain_dve"], 1)
                dve.wait_ge(s["chain_dve"], next(chain))
                v.tensor_scalar(var_eps[:, ts[0]:ts[-1] + 1], mean_var[:, ts[0]:ts[-1] + 1, 1], EPS, scale, ALU.add,
                                ALU.mult).then_inc(s["ln_var"], 1)

            def normalise(n, dst):
                dve.wait_ge(s["ln_rstd"], n + 1)
                for t in LN_GROUPS[n]:
                    v.tensor_scalar(dst[:, t, :], x_tok[:, t, :], mean_var[:, t, 0:1], rstd[:, t:t + 1],
                                    ALU.subtract, ALU.mult).then_inc(s["ln_out"], 1)

            def tokens_lo(dst, base, ts):
                for t in ts:
                    dve.wait_ge(s["tr_hi"], base + t + 1)
                    lo(dst(1, t), TR_BANKS[t % 4][:].rearrange("p (c x) -> p c x", c=KC), SX, dst(0, t)
                       ).then_inc(s["tr_free"], 1)

            def weight_lo(n, w, src):
                dve.wait_ge(s["w_hi"], n + 1)
                lo(w[1], src, SW, w[0]).then_inc(s["w_lo"], 1)

            def token_stats(half):
                for t in LN_GROUPS[half]:
                    dve.wait_ge(s[f"x_landed{min(t // 2, 2)}"], 16)
                    last = v.bn_stats(stats[:, t, :], x_tok[:, t, :])
                last.then_inc(s["chain_dve"], 1)
                dve.wait_ge(s["chain_dve"], next(chain))
                variances(LN_GROUPS[half])

            token_stats(0)
            normalise(0, xhat0)
            weight_lo(0, wq, wq_stage)
            dve.wait_ge(s["consts_landed"], 16 * (6 + HC))
            v.tensor_scalar(bq_scaled, bq_col, SX, None, ALU.mult).then_inc(s["bq_done"], 1)
            tokens_lo(lnT_tile, 0, range(HT))
            token_stats(1)
            v.tensor_scalar(mask_bias, mask_int, 0.0, NEG, ALU.is_equal, ALU.mult)
            k_bias = [kT[n][:, :, :, L] for n in range(2)]
            bk_all = bk_col.unsqueeze(2).broadcast_to((P, KC, PB))
            v.tensor_scalar(k_bias[0], bk_all, SK, None, ALU.mult).then_inc(s["chain_dve"], 1)
            dve.wait_ge(s["chain_dve"], next(chain))
            lo(k_bias[1], bk_all, SK, k_bias[0])
            normalise(1, xhat0)

            def query_lo(n):
                half, c = divmod(n, KC)
                cols = slice(half * D, (half + 1) * D)
                dve.wait_ge(s["q_hi"], n + 1)
                v.tensor_tensor(qT[1][:, c, cols], q_f[n % 2], qT[0][:, c, cols], ALU.subtract).then_inc(s["q_lo"], 1)

            query_lo(0)
            query_lo(1)
            tokens_lo(lnT_tile, 0, range(HT, NT))
            weight_lo(1, wk, wk_stage)
            query_lo(2)
            bv_all = bv_col.unsqueeze(2).broadcast_to((P, KC, P))
            v.tensor_scalar(bv_bc[0], bv_all, SW, None, ALU.mult).then_inc(s["chain_dve"], 1)
            dve.wait_ge(s["chain_dve"], next(chain))
            lo(bv_bc[1], bv_all, SW, bv_bc[0])
            dve.wait_ge(s["ab_landed"], 16)
            v.tensor_tensor(ab_sd[:, 0], ab_stage[:, 0], ab_stage[:, 1], ALU.add)
            v.tensor_tensor(ab_sd[:, 1], ab_stage[:, 0], ab_stage[:, 1], ALU.subtract).then_inc(s["ab_split"], 1)
            query_lo(3)
            query_lo(4)
            dve.wait_ge(s["ctxl_split"], 1)
            lo(ctxl[1], ctxl_stage, SX, ctxl[0]).then_inc(s["ctxl_split"], 1)
            dve.wait_ge(s["ab_split"], 2)
            lo(ab[1], ab_sd, SW, ab[0]).then_inc(s["ab_split"], 1)
            weight_lo(2, wv, wv_stage)
            query_lo(5)
            weight_lo(3, wo, wo_stage)
            query_lo(6)
            dve.wait_ge(s["split_hi"], 1)
            lo(ctx_hl[0][1], ctx_stage[0], SX, ctx_hl[0][0]).then_inc(s["split_lo"], 1)
            query_lo(7)
            dve.wait_ge(s["last_hi"], 1)
            lo(klast[1], BE[:, 0:KC * B].rearrange("p (c b) -> p c b", c=KC), SK / (SX * SW), klast[0]
               ).then_inc(s["last_lo"], 1)
            dve.wait_ge(s["last_hi"], 2)
            lo(vlast[1], BF[0:B, :], 1.0 / SW, vlast[0]).then_inc(s["last_lo"], 1)
            dve.wait_ge(s["bias_landed"], 16)
            dve.wait_ge(s["bias_ps"], 1)
            v.scalar_tensor_tensor(bias_tile, BG[:], 1.0 / (SW * SW), bo_bc, ALU.mult, ALU.add
                                   ).then_inc(s["bias_done"], 1)

            def mixing_weights_lo(k, n):
                dve.wait_ge(s["wt_hi"], 2 * k + n + 1)
                lo(wt[k][n][1], (wt_sum[k], wt_b[k])[n], SW, wt[k][n][0]).then_inc(s["wt_lo"], 1)

            def fold_lo(n):
                dve.wait_ge(s["fold_hi"], n + 1)
                lo(wf[n // KC][1][:, n % KC, :], FOLD_BANKS[n % 4][:], SF / (SW * SW), wf[n // KC][0][:, n % KC, :]
                   ).then_inc(s["fold_free"], 1)

            def step(st, par, cur=True, prev=True, nxt=True, mixing=None):
                n0 = st * 8

                def k_lo(c):
                    if cur:
                        dve.wait_ge(s["proj_hi"], n0 + c + 1)
                        lo(kT[1][:, c, :, 0:LM], proj_banks[c % 2][:].rearrange("p (b x) -> p b x", b=PB),
                           SK / (SX * SW), kT[0][:, c, :, 0:LM]).then_inc(s["proj_free"], 1)
                    else:
                        fold_lo(2 * c)
                        fold_lo(2 * c + 1)

                def v_lo(t):
                    if cur:
                        dve.wait_ge(s["proj_hi"], n0 + 5 + t)
                        lo(v_hl[1][:, t, :], proj_banks[t % 2][:], 1.0 / SW, v_hl[0][:, t, :]
                           ).then_inc(s["proj_free"], 1)
                    else:
                        fold_lo(8 + t)

                def scores(j):
                    bank = (BC, BD)[j % 2]
                    dve.wait_ge(s["s_ps"], n0 + j + 1)
                    v.scalar_tensor_tensor(sm[:, j, :], bank[:, 0:L], bank[:, L:L + 1], mask_bias,
                                           ALU.add, ALU.add).then_inc(s["s_free"], 1)

                def maxima(b):
                    js = slice(b * KC, b * KC + KC)
                    dve.wait_ge(s["s_free"], n0 + 4 + 4 * b)
                    v.reduce_max(row_max[:, js], sm[:, js, :], AX_X).then_inc(s["s_max"], 1)
                    dve.wait_ge(s["s_max"], st * 2 + 1 + b)
                    v.tensor_scalar(neg_max[:, js], row_max[:, js], -ISD / (SX * SK), None, ALU.mult
                                    ).then_inc(s["s_neg"], 1)

                def reciprocals(m, b):
                    js = slice(b * KC, b * KC + KC)
                    dve.wait_ge(s["exp_done"], m * 8 + 4 + 4 * b)
                    v.tensor_scalar(sums_scaled[:, js], score_sums[:, js], 1.0 / SP_, None, ALU.mult
                                    ).then_inc(s["sums_sc"], 1)
                    dve.wait_ge(s["sums_sc"], m * 2 + 1 + b)
                    v.reciprocal(recip[:, js], sums_scaled[:, js]).then_inc(s["recip_done"], 1)

                def p_lo(m, b):
                    for j in range(b * KC, b * KC + KC):
                        dve.wait_ge(s["p_hi"], m * 8 + 1 + j)
                        v.scalar_tensor_tensor(p_hl[1][:, j, 0:L], sm[:, j, :], recip[:, j:j + 1],
                                               p_hl[0][:, j, 0:L], ALU.mult, ALU.subtract
                                               ).then_inc(s["p_lo"], 1)

                def pt_copy(b):
                    dve.wait_ge(s["pt_ps"], st * 5 - 5 + (1, 4)[b])
                    v.tensor_copy(pT[:, b, 0].rearrange("p h c x -> p (h c x)"), BE[:].bitcast(F16)
                                  ).then_inc(s["pt_dve"], 1)

                if prev:
                    reciprocals(st - 1, 1)
                k_lo(0)
                if prev:
                    p_lo(st - 1, 1)
                k_lo(1)
                if prev:
                    pt_copy(0)
                k_lo(2)
                if prev:
                    dve.wait_ge(s["pt_ps"], st * 5 - 2)
                    v.tensor_tensor(pT_last,
                                    BH[0:2 * PAIRS, 0:P // 2].bitcast(F16).unsqueeze(1).broadcast_to((2 * PAIRS, PAIRS, P)),
                                    diag[0:2 * PAIRS].unsqueeze(2).broadcast_to((2 * PAIRS, PAIRS, P)),
                                    ALU.mult).then_inc(s["pt_dve"], 1)
                    pt_copy(1)
                if nxt:
                    dve.wait_ge(s["split_hi"], st + 2)
                    lo(ctx_hl[1 - par][1], ctx_stage[1 - par], SX, ctx_hl[1 - par][0]).then_inc(s["split_lo"], 1)
                k_lo(3)
                if mixing is not None:
                    mixing_weights_lo(mixing, 0)
                if prev:
                    for b in range(PB):
                        dve.wait_ge(s["pv_hi"], st * 2 - 1 + b)
                        for r in range(HC):
                            rows = slice(r * DK, (r + 1) * DK)
                            last = lo(att_st[1][rows, :, b, :],
                                      (BG, BH)[b][rows, :].rearrange("p (c x) -> p c x", c=KC)[:, :, r * S:(r + 1) * S],
                                      1.0 / SP_, att_st[0][rows, :, b, :])
                        last.then_inc(s["pv_free"], 1)
                v_lo(0)
                if mixing is not None:
                    mixing_weights_lo(mixing, 1)
                if cur:
                    if not prev:
                        dve.wait_ge(s["x_biased"], 1)
                        dve.wait_ge(s["vlast_stored"], 32)
                    scores(0)
                    scores(1)
                v_lo(1)
                if cur:
                    scores(2)
                    scores(3)
                    maxima(0)
                    scores(4)
                    scores(5)
                    reciprocals(st, 0)
                v_lo(2)
                if cur:
                    scores(6)
                    scores(7)
                    maxima(1)
                v_lo(3)
                if cur:
                    p_lo(st, 0)

            step(0, 0, prev=False)
            step(1, 1, mixing=0)
            with dve.Fori(1, STEPS // 2 - 1) as k:
                step(k * 2, 0)
                step(k * 2 + 1, 1)
            step(STEPS - 2, 0, mixing=1)
            step(STEPS - 1, 1, nxt=False, mixing=2)
            step(STEPS, 0, cur=False, nxt=False)

            def x1(t):
                dve.wait_ge(s["wo_ps"], t + 1)
                v.scalar_tensor_tensor(x_tok[:, t, :], (BE, BF, BA, BB)[t % 4][:], 1.0 / (SX * SW), x_tok[:, t, :],
                                       ALU.mult, ALU.add).then_inc(s["x1_done"], 1)
                dve.wait_ge(s["x1_done"], t + 1)
                return v.bn_stats(stats[:, t, :], x_tok[:, t, :])

            for t in range(HT):
                last = x1(t)
            last.then_inc(s["chain_dve"], 1)
            dve.wait_ge(s["chain_dve"], next(chain))
            variances(LN_GROUPS[2])
            x1(HT)
            normalise(2, xhat1)
            x1(HT + 1)
            x1(HT + 2)
            tokens_lo(ln1T_tile, NT, range(HT))
            last = x1(HT + 3)
            last.then_inc(s["chain_dve"], 1)
            dve.wait_ge(s["chain_dve"], next(chain))
            variances(LN_GROUPS[3])
            normalise(3, xhat1)

            def piece_lo(n, k):
                dve.wait_ge(s["e_hi"], n * 8 + k + 1)
                lo(w_hl[k][1], e_stage[k % 4], SG if k < 4 else S2, w_hl[k][0]).then_inc(s["e_lo"], 1)

            rr, ii, ri, ir = (bind_sums[:, n] for n in range(4))
            a1, a2, b2 = (lhs_bind[:, n] for n in range(3))

            def bind(half, parity):
                bs = slice(half * (B // 2), (half + 1) * (B // 2))
                k_, v_ = (spec[m][half][:, 2 * parity:2 * parity + 2] for m in (1, 2))
                by_batch = prod.rearrange("p r (b q) -> p r b q", q=S)
                done = (half * 2 + parity) * 6
                dve.wait_ge(s["spec_done"], half * 12 + parity * 6 + 4)
                v.tensor_tensor(prod, k_, v_, ALU.mult).then_inc(s["products"], 1)
                dve.wait_ge(s["products"], done + 1)
                v.reduce_sum(bind_sums[:, 0:2, parity, bs], by_batch, AX_X).then_inc(s["products"], 1)
                dve.wait_ge(s["products"], done + 2)
                v.tensor_tensor(prod[:, 0], k_[:, 0], v_[:, 1], ALU.mult)
                v.tensor_tensor(prod[:, 1], k_[:, 1], v_[:, 0], ALU.mult).then_inc(s["products"], 1)
                dve.wait_ge(s["products"], done + 3)
                v.reduce_sum(bind_sums[:, 2:4, parity, bs], by_batch, AX_X).then_inc(s["products"], 1)
                dve.wait_ge(s["products"], done + 4)
                at = (slice(None), parity, bs)
                v.tensor_tensor(a1[at], rr[at], ii[at], ALU.subtract)
                v.tensor_tensor(a2[at], ri[at], ir[at], ALU.add)
                last = v.tensor_tensor(b2[at], ii[at], rr[at], ALU.subtract)
                if parity == 0:
                    last.then_inc(s["chain_dve"], 1)
                    dve.wait_ge(s["chain_dve"], next(chain))
                    at = (slice(0, 1), 0, bs)
                    v.tensor_copy(a1[at], rr[at])
                    v.tensor_copy(b2[at], ii[at])
                    last = v.memset(a2[at], 0.0)
                last.then_inc(s["chain_dve"], 1)
                dve.wait_ge(s["chain_dve"], next(chain))

            def unbind(half, parity):
                bs = slice(half * (B // 2), (half + 1) * (B // 2))

                def over_tokens(z):
                    return z[:, parity, bs].unsqueeze(2).broadcast_to((P, B // 2, S))

                def part(m, r):
                    return spec[m][half][:, 2 * parity + r].rearrange("p (b q) -> p b q", q=S)
                n = half * 2 + parity
                dve.wait_ge(s["spec_done"], half * 12 + parity * 6 + 6)
                for r, (c0, c1) in enumerate(((a1, a2), (a2, b2))):
                    v.tensor_tensor(part(1, r), part(0, 0), over_tokens(c0), ALU.mult)
                    v.tensor_tensor(prod[:, r].rearrange("p (b q) -> p b q", q=S), part(0, 1), over_tokens(c1), ALU.mult
                                    ).then_inc(s["products"], 1)
                for r in range(2):
                    dve.wait_ge(s["products"], 6 * n + 5 + r)
                    last = v.tensor_tensor(part(1, r), part(1, r), prod[:, r].rearrange("p (b q) -> p b q", q=S), ALU.add)
                last.then_inc(s["unbound"], 1)
                dve.wait_ge(s["unbound"], n + 1)

            def x2(t):
                bank = (BA, BB, BE, BF)[t % 4]
                even, odd = bank[:, 0:NF], bank[:, NF:D]
                both = x_tok[:, t, :].rearrange("p (h n) -> p h n", h=2)
                dve.wait_ge(s["irfft_ps"], t + 1)
                v.tensor_tensor(both, both, even.unsqueeze(1).broadcast_to((P, 2, NF)), ALU.add
                                ).then_inc(s["chain_dve"], 1)
                dve.wait_ge(s["chain_dve"], next(chain))
                v.tensor_tensor(both[:, 0], both[:, 0], odd, ALU.add)
                v.tensor_tensor(both[:, 1], both[:, 1], odd, ALU.subtract).then_inc(s["x2_done"], 1)
                dve.wait_ge(s["x2_done"], t + 1)
                return v.bn_stats(stats[:, t, :], x_tok[:, t, :])

            def l2_lo(t):
                dve.wait_ge(s["l2_hi"], t + 1)
                v.tensor_tensor(l2_tile(1, t), l2_f[:, t, :], l2_tile(0, t), ALU.subtract).then_inc(s["l2_lo"], 1)

            piece_lo(0, 0)
            bind(0, 0)
            tokens_lo(ln1T_tile, NT, range(HT, NT))
            unbind(0, 0)
            piece_lo(0, 1)
            bind(0, 1)
            unbind(0, 1)
            piece_lo(0, 2)
            bind(1, 0)
            unbind(1, 0)
            for t in range(HT):
                last = x2(t)
            last.then_inc(s["chain_dve"], 1)
            dve.wait_ge(s["chain_dve"], next(chain))
            variances(LN_GROUPS[4], SX ** -2)
            dve.wait_ge(s["wg_split"], 1)
            lo(wg_hl[1], wg_stage, SG, wg_hl[0]).then_inc(s["wg_split"], 1)
            normalise(4, l2_f)
            bind(1, 1)
            unbind(1, 1)
            for n, (t, u) in ((5, LN_GROUPS[5]), (6, LN_GROUPS[6])):
                x2(t)
                x2(u).then_inc(s["chain_dve"], 1)
                dve.wait_ge(s["chain_dve"], next(chain))
                variances((t, u), SX ** -2)
                if n == 5:
                    dve.wait_ge(s["ln_rstd"], n + 1)
                    v.scalar_tensor_tensor(shift[:, t:u + 1], mean_var[:, t:u + 1, 0], -1.0, rstd[:, t:u + 1],
                                           ALU.mult, ALU.mult).then_inc(s["l2_shift"], 1)
            normalise(6, l2_f)
            dve.wait_ge(s["l2_lo"], HT + 2)
            for t in LN_GROUPS[6]:
                l2_lo(t)
            piece_lo(0, 3)

            def by_tile(z):
                return z.unsqueeze(1).broadcast_to((P, NT, E))

            def by_expert(z):
                return z.unsqueeze(2).broadcast_to((P, NT, E))

            dve.wait_ge(s["logits_ps"], 1)
            v.scalar_tensor_tensor(
                logits, BC[:, 0:NT * E].rearrange("p (t e) -> p t e", e=E), 1.0 / (SX * SG), by_tile(bg_bc),
                ALU.mult, ALU.add).then_inc(s["chain_dve"], 1)
            dve.wait_ge(s["chain_dve"], next(chain))
            v.reduce_max(top, logits, AX_X).then_inc(s["chain_dve"], 1)
            dve.wait_ge(s["chain_dve"], next(chain))
            v.tensor_tensor(is_max, logits, by_expert(top), ALU.is_equal).then_inc(s["chain_dve"], 1)
            dve.wait_ge(s["chain_dve"], next(chain))
            v.tensor_tensor(score, is_max, by_tile(rank_order), ALU.mult).then_inc(s["chain_dve"], 1)
            dve.wait_ge(s["chain_dve"], next(chain))
            v.reduce_max(top2, score, AX_X).then_inc(s["chain_dve"], 1)
            dve.wait_ge(s["chain_dve"], next(chain))
            v.tensor_tensor(onehot16, score, by_expert(top2), ALU.is_equal).then_inc(s["onehot_done"], 1)
            dve.wait_ge(s["rank_ps"], 1)
            v.scalar_tensor_tensor(slot_of, BD[:, 0:NT * E].rearrange("p (t e) -> p t e", e=E), 1.0, onehot16,
                                   ALU.add, ALU.mult).then_inc(s["chain_dve"], 1)
            dve.wait_ge(s["chain_dve"], next(chain))

            def slots(n, e):
                dve.wait_ge(s["xs_ps"], n * 4)
                for half in range(2):
                    ts = slice(half * HT, (half + 1) * HT)
                    v.tensor_tensor(perm[:, ts], slot_iota.unsqueeze(1).broadcast_to((P, HT, CAP)),
                                    slot_of[:, ts, bass.ds(e, 1)].broadcast_to((P, HT, CAP)), ALU.is_equal
                                    ).then_inc(s["perm_done"], 1)

            def gathered(n, c):
                dve.wait_ge(s["xs_ps"], n * 4 + c + 1)
                v.tensor_copy(xs[:, c].rearrange("p h x -> p (h x)"), (BG, BH)[c % 2][:, 0:2 * CAP]
                              ).then_inc(s["xs_done"], 1)

            def take_ids(n):
                v.tensor_tensor(ids_next[0], BH[:, 2 * CAP:2 * CAP + 2], id_offset, ALU.add)
                v.tensor_tensor(ids_next[1], BH[0:CB, 2 * CAP + 2:2 * CAP + 4], id_offset[0:CB], ALU.add
                                ).then_inc(s["ids_done"], 1)

            def rows_out(n):
                dve.wait_ge(s["yt_ps"], n + 1)
                dve.wait_ge(s["rows_landed"], n * 32 + 32)
                v.tensor_tensor(y_rows[0], BE[:], x2_rows[0], ALU.add)
                v.tensor_tensor(y_rows[1], BF[0:CB, :], x2_rows[1], ALU.add).then_inc(s["y_out"], 1)

            def expert(n, e, prev=True, nxt=True, after=True):
                for k in range(FC // 2):
                    dve.wait_ge(s["h_hi"], n * 8 + k + 1)
                    v.scalar_tensor_tensor(hid_hl[1][:, 2 * k:2 * k + 2, :], hid_f[k % 4], SH,
                                           hid_hl[0][:, 2 * k:2 * k + 2, :], ALU.mult, ALU.subtract
                                           ).then_inc(s["h_lo"], 1)
                    if k == 1:
                        piece_lo(n, PIECES - 1)
                    elif nxt and k % 2:
                        piece_lo(n + 1, k // 2 - 1)
                if prev:
                    rows_out(n - 1)
                if nxt:
                    gathered(n + 1, 0)
                    gathered(n + 1, 1)
                    piece_lo(n + 1, 3)
                    gathered(n + 1, 2)
                    piece_lo(n + 1, 4)
                    gathered(n + 1, 3)
                    piece_lo(n + 1, 5)
                if after:
                    slots(n + 2, e + 2)
                dve.wait_ge(s["ids_done"], n + 1)
                dve.wait_ge(s["scattered"], n * 32)
                v.tensor_copy(ids[0], ids_next[0])
                v.tensor_copy(ids[1], ids_next[1]).then_inc(s["shifted"], 1)
                if nxt:
                    dve.wait_ge(s["shifted"], n + 1)
                    take_ids(n + 1)
                    piece_lo(n + 1, 6)

            def round_(r, first):
                slots(r * E, 0)
                if first:
                    dve.wait_ge(s["count_ps"], 1)
                    v.reduce_max(most, BE[:, 0:E], AX_X).then_inc(s["chain_dve"], 1)
                    dve.wait_ge(s["chain_dve"], next(chain))
                    v.tensor_scalar(more_rounds, most, float(CAP), None, ALU.is_gt).then_inc(s["routed"], 1)
                if first:
                    piece_lo(0, 4)
                    gathered(0, 0)
                    piece_lo(0, 5)
                else:
                    for k in range(PIECES - 1):
                        piece_lo(r * E, k)
                    gathered(r * E, 0)
                for c in range(1, KC):
                    gathered(r * E, c)
                take_ids(r * E)
                slots(r * E + 1, 1)
                if first:
                    piece_lo(0, 6)
                expert(r * E, 0, prev=False)
                with dve.Fori(1, E - 2) as e:
                    expert(r * E + e, e)
                expert(r * E + (E - 2), E - 2, after=False)
                expert(r * E + (E - 1), E - 1, nxt=False, after=False)
                rows_out(r * E + (E - 1))

            round_(0, True)
            dve.wait_ge(s["routed"], 1)
            with dve.If(dve.value_load(more_rounds[0:1, 0:1], min_val=0, max_val=1) > 0):
                with dve.Fori(1, ROUNDS) as r:
                    v.tensor_scalar(slot_of, slot_of, -float(CAP), None, ALU.add).then_inc(s["ranks_moved"], 1)
                    dve.wait_ge(s["ranks_moved"], r)
                    round_(r, False)

        @block.tensor
        def _(pe):
            m = nc.tensor

            def product(out_ap, pairs):
                pairs = list(pairs)
                for n, (w, x) in enumerate(pairs):
                    last = m.matmul(out_ap, w, x, start=(n == 0), stop=(n == len(pairs) - 1))
                return last

            def split_product(out_ap, w, x, wi, xi):
                return product(out_ap, [(u[wi(c)], z[xi(c)]) for c in range(KC) for u, z in hl_passes(w, x)])

            def transpose_tokens(base, src, half):
                for t in range(half * HT, (half + 1) * HT):
                    pe.wait_ge(s["ln_out"], base + t + 1)
                    pe.wait_ge(s["tr_free"], from_zero(base + t - 3))
                    for c in range(KC):
                        last = m.transpose(TR_BANKS[t % 4][:, c * P:(c + 1) * P], src[:, t, c * P:(c + 1) * P], ident)
                    last.then_inc(s["tr_ps"], 1)

            def queries(ns):
                for n in ns:
                    half, c = divmod(n, KC)
                    pe.wait_ge(s["q_f32"], from_zero(n - 1))
                    split_product((BC, BD)[n % 2][:], wq, lnT,
                                  lambda k: (slice(None), k, slice(c * P, (c + 1) * P)),
                                  lambda k: (slice(None), k, slice(half * D, (half + 1) * D))).then_inc(s["q_ps"], 1)

            pe.wait_ge(s["ident_landed"], 16)
            transpose_tokens(0, xhat0, 0)
            pe.wait_ge(s["w_hi"], 1)
            pe.wait_ge(s["tr_hi"], HT)
            for n in range(2):
                for k in range(KC):
                    m.matmul((BC, BD)[n][:], wq[0][:, k, n * P:(n + 1) * P], lnT[0][:, k, 0:D], start=(k == 0), stop=False)
            pe.wait_ge(s["tr_free"], HT)
            pe.wait_ge(s["w_lo"], 1)
            for n in range(2):
                for k in range(KC):
                    for u, z in ((0, 1), (1, 0)):
                        last = m.matmul((BC, BD)[n][:], wq[u][:, k, n * P:(n + 1) * P], lnT[z][:, k, 0:D],
                                        start=False, stop=(k == KC - 1 and u == 1))
                last.then_inc(s["q_ps"], 1)
            queries(range(2, 3))
            transpose_tokens(0, xhat0, 1)
            queries(range(3, KC))
            pe.wait_ge(s["tr_free"], NT)
            queries(range(KC, 2 * KC))
            pe.wait_ge(s["w_lo"], 3)
            pe.wait_ge(s["ctxl_split"], 2)
            for c in range(KC):
                last = split_product(BE[:, c * B:(c + 1) * B], wk, ctxl,
                                     lambda k: (slice(None), k, slice(c * P, (c + 1) * P)),
                                     lambda k: (slice(None), k, slice(None)))
            last.then_inc(s["last_ps"], 1)
            split_product(BF[0:B, :], ctxl, wv, lambda k: (slice(None), k, slice(None)),
                          lambda k: (slice(None), k, slice(None))).then_inc(s["last_ps"], 1)
            pe.wait_ge(s["w_lo"], 4)
            split_product(BG[:], bv_bc, wo, lambda k: (slice(None), k, slice(None)),
                          lambda k: (slice(None), k, slice(None))).then_inc(s["bias_ps"], 1)

            def fold(n):
                mm, c = divmod(n, KC)
                if n in (0, 2):
                    pe.wait_ge(s["s_free"], STEPS * 8 - (n == 0))
                if n in (1, 3):
                    pe.wait_ge(s["proj_free"], STEPS * 8 - (n == 1))
                pe.wait_ge(s["fold_free"], from_zero(n - 3))
                for parity in range(2):
                    last = product(FOLD_BANKS[n % 4][:, parity * NF:(parity + 1) * NF],
                                   [(u[:, k, c * P:(c + 1) * P], z[:, parity, k, :]) for k in range(2)
                                    for u, z in hl_passes(wt[mm][parity], dft)])
                last.then_inc(s["fold_ps"], 1)

            def step(st, par, cur=True, prev=True):
                n0 = st * 8

                def k_proj(c):
                    if cur:
                        pe.wait_ge(s["proj_free"], from_zero(n0 + c - 1))
                        split_product(proj_banks[c % 2][:], wk, ctx_hl[par],
                                      lambda k: (slice(None), k, slice(c * P, (c + 1) * P)),
                                      lambda k: (slice(None), k, slice(None))).then_inc(s["proj_ps"], 1)
                    else:
                        fold(2 * c)
                        fold(2 * c + 1)

                def v_proj(t):
                    if cur:
                        pe.wait_ge(s["proj_free"], n0 + 3 + t)
                        split_product(proj_banks[t % 2][:], ctx_hl[par], wv,
                                      lambda k: (slice(None), k, slice(t * P, (t + 1) * P)),
                                      lambda k: (slice(None), k, slice(None))).then_inc(s["proj_ps"], 1)
                    else:
                        fold(8 + t)

                def p_transposes(b):
                    for kt in range(2):
                        bank = (BE, BF)[kt][:].bitcast(F16)
                        for n in range(2):
                            for c in range(KC):
                                slot = n * KC + c
                                last = m.transpose(bank[:, slot * P:(slot + 1) * P],
                                                   p_hl[n][:, b * KC + c, kt * P:(kt + 1) * P], ident16)
                        last.then_inc(s["pt_ps"], 1)

                def attention(b):
                    for c in range(KC):
                        cols = slice(c * P, (c + 1) * P)
                        j = b * KC + c
                        pairs = [(v_hl[u][:, b * 2 + kt, cols], pT[:, b, kt, z, c, :])
                                 for kt in range(2) for u, z in ((0, 0), (0, 1), (1, 0))]
                        pairs += [(vl_cur[:, 0, :], pT_last[:, j, :]),
                                  (vl_cur[0:PAIRS, 1, :], pT_last[0:PAIRS, j, :])]
                        last = product((BG, BH)[b][:, cols], pairs)
                    last.then_inc(s["pv_ps"], 1)

                def scores(j):
                    b, c = divmod(j, KC)
                    pe.wait_ge(s["s_free"], from_zero(n0 + j - 1))
                    product((BC, BD)[j % 2][:, 0:L + 1],
                            [(u[:, c, b, :], z[:, c, b, :]) for u, z in hl_passes(q_bd, kT)]
                            ).then_inc(s["s_ps"], 1)

                if cur:
                    pe.wait_ge(s["split_lo"], st + 1)
                k_proj(0)
                k_proj(1)
                if prev:
                    pe.wait_ge(s["p_lo"], st * 8 - 4)
                    p_transposes(0)
                k_proj(2)
                if prev:
                    pe.wait_ge(s["p_lo"], st * 8)
                    pe.wait_ge(s["pv_free"], from_zero(st * 2 - 2))
                    m.transpose(BH[0:2 * PAIRS, 0:P // 2].bitcast(F16),
                                p_all[:, :, :, LM].rearrange("p h j -> p (h j)"), ident16).then_inc(s["pt_ps"], 1)
                    pe.wait_ge(s["pt_dve"], st * 3 - 2)
                    pe.wait_ge(s["pt_act"], st * 2 - 1)
                    p_transposes(1)
                k_proj(3)
                if prev:
                    pe.wait_ge(s["vl_ready"], st)
                    for b in range(PB):
                        pe.wait_ge(s["pt_dve"], st * 3 - 1 + b)
                        pe.wait_ge(s["pt_act"], st * 2 - 1 + b)
                        attention(b)
                v_proj(0)
                if cur:
                    pe.wait_ge(s["q_ready"], st + 1)
                    pe.wait_ge(s["proj_free"], n0 + 4)
                    scores(0)
                    scores(1)
                v_proj(1)
                if cur:
                    scores(2)
                    scores(3)
                v_proj(2)
                if cur:
                    scores(4)
                    scores(5)
                v_proj(3)
                if cur:
                    scores(6)
                    scores(7)

            step(0, 0, prev=False)
            step(1, 1)
            with pe.Fori(1, STEPS // 2 - 1) as k:
                step(k * 2, 0)
                step(k * 2 + 1, 1)
            step(STEPS - 2, 0)
            step(STEPS - 1, 1)
            pe.wait_ge(s["wt_lo"], 6)
            pe.wait_ge(s["dft_landed"], 32)
            step(STEPS, 0, cur=False)
            pe.wait_ge(s["ab_split"], 3)
            pe.wait_ge(s["pv_free"], STEPS * PB - 1)
            for c in range(KC):
                parity, part = divmod(c, 2)
                last = product(BG[:, c * 4:(c + 1) * 4],
                               [(z[:, parity, k, part * P:(part + 1) * P], u[:, parity, k, :]) for k in range(2)
                                for u, z in hl_passes(ab, dft)])
            last.then_inc(s["abias_ps"], 1)

            pe.wait_ge(s["att_copied"], STEPS)
            for t in range(NT):
                pe.wait_ge(s["x1_done"], from_zero(t - 3))
                if t == 2:
                    pe.wait_ge(s["fold_free"], 3 * KC)
                split_product((BE, BF, BA, BB)[t % 4][:], attT, wo,
                              lambda k: (slice(None), k, slice(t * P, (t + 1) * P)),
                              lambda k: (slice(None), k, slice(None))).then_inc(s["wo_ps"], 1)
                if t == NT - 2:
                    pe.wait_ge(s["abias_done"], 1)
                    pe.wait_ge(s["x1_done"], HT + 2)
                    transpose_tokens(NT, xhat1, 0)

            pe.wait_ge(s["x1_done"], NT)
            pe.wait_ge(s["tr_free"], NT + HT)
            def spectra(ns):
                for n in ns:
                    mm, c, half = SPEC_ORDER[n]
                    pe.wait_ge(s["spec_done"], from_zero(n - 1))
                    split_product((BC, BD)[n % 2][:], wf[mm], ln1T[half],
                                  lambda k: (slice(None), k, slice(c * P, (c + 1) * P)),
                                  lambda k: (slice(None), k, slice(None))).then_inc(s["spec_ps"], 1)

            def back(t, parity):
                pe.wait_ge(s["x2_done"], from_zero(t - 3))
                pe.wait_ge(s["unbound"], 2 * (t // HT) + parity + 1)
                return product((BA, BB, BE, BF)[t % 4][:, parity * NF:(parity + 1) * NF],
                               [(spec[1][t // HT][:, c, t % HT * P:(t % HT + 1) * P], idft[:, c, :])
                                for c in (2 * parity, 2 * parity + 1)])

            def gate_transpose(t):
                pe.wait_ge(s["l2_lo"], t + 1)
                pe.wait_ge(s["lt_done"], from_zero(t - 1))
                bank = (BG, BH)[t % 2][:].bitcast(F16)
                for n in range(2):
                    for c in range(KC):
                        slot = n * KC + c
                        last = m.transpose(bank[:, slot * P:(slot + 1) * P], l2_tile(n, t)[:, c * P:(c + 1) * P], ident16)
                last.then_inc(s["lt_ps"], 1)

            def gate(t):
                pe.wait_ge(s["lt_done"], t + 1)
                return product(BC[:, t * E:(t + 1) * E],
                               [(l2T[:, t, u, c, :], wg_hl[z][:, c, :]) for c in range(KC)
                                for u, z in ((0, 0), (0, 1), (1, 0))])

            spectra(range(6))
            transpose_tokens(NT, xhat1, 1)
            spectra(range(6, 12))
            pe.wait_ge(s["tr_free"], 2 * NT)
            spectra(range(12, 18))
            pe.wait_ge(s["idft_landed"], 16)
            for t in range(HT):
                for parity in range(2):
                    last = back(t, parity)
                last.then_inc(s["irfft_ps"], 1)
            spectra(range(18, 24))
            for t in range(HT):
                gate_transpose(t)
            for t in range(HT, NT):
                back(t, 0)
            for t in range(HT, NT):
                back(t, 1).then_inc(s["irfft_ps"], 1)
            pe.wait_ge(s["wg_split"], 2)
            pe.wait_ge(s["spec_done"], 24)
            for t in range(HT):
                gate(t)
            gate_transpose(HT)
            gate_transpose(HT + 1)
            gate_transpose(HT + 2)
            gate(HT)
            gate_transpose(HT + 3)
            for t in range(HT + 1, NT):
                last = gate(t)
            last.then_inc(s["logits_ps"], 1)
            pe.wait_ge(s["onehot_done"], 1)
            m.matmul(BD[:, 0:NT * E], tri16, onehot16.rearrange("p t e -> p (t e)"), start=True, stop=False)
            for k in range(NT - 1):
                last = m.matmul(BD[:, (k + 1) * E:NT * E].rearrange("p (t e) -> p t e", e=E), ones16,
                                onehot16[:, k:k + 1, :].broadcast_to((P, NT - 1 - k, E)), start=False, stop=(k == NT - 2))
            last.then_inc(s["rank_ps"], 1)
            product(BE[:, 0:E], [(ones16, onehot16[:, k, :]) for k in range(NT)]).then_inc(s["count_ps"], 1)

            def gather(n, c):
                bank = (BG, BH)[c % 2]
                pe.wait_ge(s["perm_done"], 2 * n + 2)
                pe.wait_ge(s["xs_done"], from_zero(n * 4 + c - 1))
                if c == 1:
                    pe.wait_ge(s["ids_done"], n)
                for z in range(2):
                    last = product(bank[:, z * CAP:(z + 1) * CAP],
                                   [(l2_tile(z, t)[:, c * P:(c + 1) * P], perm[:, t, :]) for t in range(NT)])
                if c == KC - 1:
                    product(bank[:, 2 * CAP:2 * CAP + 2], [(perm[:, t, 0:P], tok_ids[:, t, :]) for t in range(NT)])
                    last = product(bank[0:CB, 2 * CAP + 2:2 * CAP + 4],
                                   [(perm[:, t, P:CAP], tok_ids[:, t, :]) for t in range(NT)])
                last.then_inc(s["xs_ps"], 1)

            def rows(n):
                pe.wait_ge(s["y_out"], n)
                for c in range(KC):
                    pe.wait_ge(s["y_done"], n * 4 + c + 1)
                    m.transpose(BE[:, c * P:(c + 1) * P], yT[:, c, 0:P], ident)
                    last = m.transpose(BF[0:CB, c * P:(c + 1) * P], yT[:, c, P:CAP], ident)
                last.then_inc(s["yt_ps"], 1)

            def expert(n, prev=True, nxt=True):
                pe.wait_ge(s["xs_done"], n * 4 + 4)
                for k in range(FC // 2):
                    pe.wait_ge(s["e_lo"], n * 8 + k // 2 + 1)
                    pe.wait_ge(s["gelu_done"], from_zero(n * 8 + k - 1))
                    for f in range(2):
                        at = (2 * k + f) % 4 * P
                        w = [z.rearrange("p (c f) -> p c f", c=KC) for z in w_hl[k // 2]]
                        last = product(proj_banks[k % 2][:, f * CAP:(f + 1) * CAP],
                                       [(w[u][:, c, at:at + P], xs[:, c, z, :]) for c in range(KC)
                                        for u, z in ((0, 0), (0, 1), (1, 0))])
                    last.then_inc(s["h_ps"], 1)
                if prev:
                    rows(n - 1)
                if nxt:
                    gather(n + 1, 0)
                    gather(n + 1, 1)
                for c in range(KC):
                    pe.wait_ge(s["e_lo"], n * 8 + 5 + c)
                    pe.wait_ge(s["y_done"], from_zero(n * 4 + c - 1))
                    if c == 0:
                        pe.wait_ge(s["h_lo"], n * 8 + 8)
                    w = [z.rearrange("p (f d) -> p f d", f=FC) for z in w_hl[4 + c]]
                    product((BC, BD)[c % 2][:, 0:CAP],
                            [(w[u][:, f, :], hid_hl[z][:, f, :]) for f in range(FC)
                             for u, z in ((0, 0), (0, 1), (1, 0))]).then_inc(s["y_ps"], 1)
                    if nxt and c < 2:
                        gather(n + 1, 2 + c)

            def round_(r):
                for c in range(KC):
                    gather(r * E, c)
                expert(r * E, prev=False)
                with pe.Fori(1, E - 1) as e:
                    expert(r * E + e)
                expert(r * E + (E - 1), nxt=False)
                rows(r * E + (E - 1))

            round_(0)
            with pe.If(pe.value_load(more_rounds[0:1, 0:1], min_val=0, max_val=1) > 0):
                with pe.Fori(1, ROUNDS) as r:
                    round_(r)


SPEC_ORDER = [(m, 2 * a + r, h) for h in range(2) for a in range(2) for m in (1, 2, 0) for r in range(2)]
EARLY_PIECES = (1, 7, 13, 19)
LN_GROUPS = [range(HT), range(HT, NT)] * 2 + [range(HT), range(HT, HT + 2), range(HT + 2, NT)]


def host_constants():
    import numpy as np
    n = np.arange(D)
    f = np.concatenate([np.arange(0, NF, 2), np.arange(1, NF, 2)])
    ang = 2 * np.pi * ((n[:, None] * f[None, :]) % D) / D
    h = NF // 2
    fwd = np.concatenate([np.cos(ang)[:, :h], -np.sin(ang)[:, :h], np.cos(ang)[:, h:], -np.sin(ang)[:, h:]], 1)
    fwd[:, h] = np.where(n % 2, -1.0, 1.0)
    inv = fwd.T * (2.0 / D)
    inv[0] /= 2
    inv[h] /= 2
    fs = fwd[:NF] * SW
    hi = fs.astype(np.float16)
    dft16 = np.stack([hi, (fs - hi).astype(np.float16)])

    def chunks(a):
        return np.ascontiguousarray(a.reshape(KC, P, -1).swapaxes(0, 1))
    return {
        "dft16": np.ascontiguousarray(dft16.reshape(2, 2, P, 2, NF).transpose(0, 2, 3, 1, 4)),
        "idft": chunks(inv[:, :NF].astype(np.float32)),
        "ident": np.eye(P, dtype=np.float32),
        "ident16": np.eye(P, dtype=np.float16),
        "own_head": np.repeat(np.eye(HC, dtype=np.float32), DK, 0),
        "slot_iota": np.tile(np.arange(1, CAP + 1, dtype=np.float32), (P, 1)),
        "tri16": np.triu(np.ones((P, P), np.float16), 1),
        "ones16": np.ones((P, P), np.float16),
        "rank_order": np.tile(np.arange(E, 0, -1, dtype=np.float32), (P, 1)),
        "tok_ids": np.stack([np.arange(T), np.arange(T) - 2 * T], 1).reshape(NT, P, 2).swapaxes(0, 1).astype(np.float16),
        "id_offset": np.tile(np.array([0, 2 * T], np.float32), (P, 1)),
        "diag": np.tile(np.eye(PAIRS, dtype=np.float32), (2, 1)),
    }


def lay_out(x, ctx_1024, mask_1x1xSxS2_ik0, L0_xattn_Wq, L0_xattn_bq, L0_xattn_Wk, L0_xattn_bk, L0_xattn_Wv,
            L0_xattn_bv, L0_xattn_Wo, L0_xattn_bo, L0_attn_Wq, L0_attn_bq, L0_attn_Wk, L0_attn_bk, L0_attn_Wv,
            L0_attn_bv, L0_ffn_W1, L0_ffn_W2, L0_ffn_Wg, L0_ffn_bg):
    import numpy as np
    a = np.asarray

    def chunks(w):
        return np.ascontiguousarray(a(w).reshape(KC, P, -1).swapaxes(0, 1))

    def column(b):
        return np.ascontiguousarray(a(b).reshape(KC, P).T)
    c = a(ctx_1024)
    main = c[:, :LM].reshape(STEPS, PB, LM, KC, P).transpose(0, 4, 3, 1, 2).reshape(STEPS, P, KC, PB * LM)
    last = c[:, LM].reshape(B, KC, P).transpose(2, 1, 0)
    zero = np.zeros_like(a(L0_attn_bq))
    return {
        "x_t": np.ascontiguousarray(a(x).reshape(NT, P, D).swapaxes(0, 1)),
        "ctx_t": np.ascontiguousarray(main), "ctx_last": np.ascontiguousarray(last),
        "mask": np.ascontiguousarray(a(mask_1x1xSxS2_ik0).reshape(S, L)),
        "wq_t": chunks(a(L0_xattn_Wq).T), "wk_t": chunks(a(L0_xattn_Wk).T), "wv_t": chunks(a(L0_xattn_Wv).T),
        "wo_t": chunks(a(L0_xattn_Wo).T),
        "bq": column(L0_xattn_bq), "bk": column(L0_xattn_bk), "bv": column(L0_xattn_bv), "bo": a(L0_xattn_bo),
        "awt": np.stack([chunks(a(w).T).reshape(P, 2, 2, D) for w in (L0_attn_Wq, L0_attn_Wk, L0_attn_Wv)]),
        "wg": chunks(L0_ffn_Wg), "bg": a(L0_ffn_bg),
        "w1": np.ascontiguousarray(a(L0_ffn_W1).reshape(E, KC, P, 4, 512).transpose(0, 3, 2, 1, 4)).reshape(E * 4, P, -1),
        "w2": np.ascontiguousarray(a(L0_ffn_W2).reshape(E, FC, P, KC, P).transpose(0, 3, 2, 1, 4)).reshape(E * 4, P, -1),
        "ab": chunks(np.stack([a(L0_attn_bq), a(L0_attn_bk), a(L0_attn_bv), zero], 1)).reshape(P, 2, 2, 4),
    }


def kernel(**inputs):
    import numpy as np
    import concourse.bacc as bacc
    from concourse.bass_utils import run_bass_kernel_spmd

    nc = bacc.Bacc("TRN2", target_bir_lowering=False, num_devices=1)
    arrays = {**lay_out(**inputs), **host_constants()}
    i = {n: nc.dram_tensor(f"in_{n}", a.shape, mybir.dt.from_np(a.dtype), kind="ExternalInput").ap()
         for n, a in arrays.items()}
    i["vlast_dram"] = nc.dram_tensor("vlast_dram", (2, B, D), F16, kind="Internal").ap()
    i["x2_dram"] = nc.dram_tensor("x2_dram", (T, D), F32, kind="Internal").ap()
    out = nc.dram_tensor("out", (B, S, D), F32, kind="ExternalOutput").ap()
    perceiver_block(nc, i, out)
    r = run_bass_kernel_spmd(nc, [{f"in_{n}": a for n, a in arrays.items()}], core_ids=[0])
    return r.results[0]["out"]
```
